# Optimizing a Trainium2 kernel written in Bass

```python
import numpy as np
import jax
import jax.numpy as jnp

def _softmax(x, axis=-1):
    return jax.nn.softmax(x, axis=axis)

def _gelu(x):
    return jax.nn.gelu(x, approximate=True)

def _silu(x):
    return jax.nn.silu(x)

def _sigmoid(x):
    return jax.nn.sigmoid(x)

def _layernorm(x, axis=-1, eps=1e-05):
    m = jnp.mean(x, axis=axis, keepdims=True)
    v = jnp.var(x, axis=axis, keepdims=True)
    return (x - m) / jnp.sqrt(v + eps)

def _scatter_add(tgt, idx, src, axis=0):
    return tgt.at[idx].add(src)

def _segment_sum(src, seg, n):
    return jax.ops.segment_sum(src, seg, n)
kernel_name = 'mk_flamingo_gated_d2_seqx_r8_4a60b0'

def setup_inputs(seed: int=0):
    np.random.seed(seed)
    _w = jnp.asarray

    def _rec_inputs():
        import jax
        import jax.numpy as jnp
        _rk = jax.random.key(seed)
        x = 7.22e-05 + 1 * jax.random.normal(jax.random.fold_in(_rk, 1), (32, 56, 256), jnp.float32)
        _lenS = 56 - jax.random.randint(jax.random.fold_in(_rk, 7), (32,), 0, max(1, 56 // 4) + 1, jnp.int32)
        _lenS2 = 1500 - jax.random.randint(jax.random.fold_in(_rk, 8), (32,), 0, max(1, 1500 // 4) + 1, jnp.int32)
        _ctx_1024P = jax.random.normal(jax.random.fold_in(_rk, 11), (32, 16, 128), jnp.float32)
        _ctx_1024c = jax.random.dirichlet(jax.random.fold_in(_rk, 511), 0.3 * jnp.ones((16,), jnp.float32), (32, 1500))
        _ctx_1024t = jnp.einsum('bsk,bkd->bsd', _ctx_1024c, _ctx_1024P)
        _ctx_1024t = _ctx_1024t * jax.lax.rsqrt(jnp.mean(jnp.square(_ctx_1024t)) + 1e-12) * 0.953939
        ctx_1024 = -0.000673644 + 1.00013 * (_ctx_1024t + 0.3 * jax.random.normal(jax.random.fold_in(_rk, 611), (32, 1500, 128), jnp.float32))
        _validS = jnp.arange(56)[None, :] < _lenS[:, None]
        _validS2 = jnp.arange(1500)[None, :] < _lenS2[:, None]
        _causal = jnp.tril(jnp.ones((56, 56), dtype=bool))
        mask_BxS2_bf1 = jnp.ones((32, 1500), dtype=bool)
        _g = jax.random.normal(jax.random.fold_in(_rk, 9001), (2, 2), jnp.float32)
        _g = jnp.sign(_g) * jnp.maximum(jnp.abs(_g), 1.0) + (_g == 0) * 1.0
        g_xattn = _g[0]
        g_ffn = _g[1]
        return (x, ctx_1024, mask_BxS2_bf1, g_xattn, g_ffn)
    x, ctx_1024, mask_BxS2_bf1, g_xattn, g_ffn = _rec_inputs()

    def _L0_xattn_setup():
        import jax, jax.numpy as jnp
        import numpy as np
        B, S1, S2, DCA = (2, 256, 128, 16)
        QDIM, KDIM, H = (256, 128, 16)
        HD = QDIM // H
        SCALE = HD ** (-0.5)
        EPS = 1e-06
        DCA_WEIGHT = 1.0

        def _ln(t, w, b):
            m = jnp.mean(t, axis=-1, keepdims=True)
            v = jnp.var(t, axis=-1, keepdims=True)
            return (t - m) * jax.lax.rsqrt(v + EPS) * w + b

        def _attn(q, k, v):
            s = jnp.einsum('bhqd,bhkd->bhqk', q, k) * SCALE
            p = jax.nn.softmax(s, axis=-1)
            return jnp.einsum('bhqk,bhkd->bhqd', p, v)
        key = jax.random.key(seed)
        ks = jax.random.split(key, 8)
        w = lambda k, shape: jax.random.normal(k, shape, jnp.float32) * 0.02
        return {'x': jax.random.normal(ks[0], (B, S1, QDIM), jnp.float32), 'y': jax.random.normal(ks[1], (B, S2 + DCA, KDIM), jnp.float32), 'Wq': w(ks[2], (QDIM, QDIM)), 'bq': jnp.zeros((QDIM,), jnp.float32), 'Wk': w(ks[3], (KDIM, QDIM)), 'bk': jnp.zeros((QDIM,), jnp.float32), 'Wv': w(ks[4], (KDIM, QDIM)), 'bv': jnp.zeros((QDIM,), jnp.float32), 'Wkv_dca': w(ks[5], (KDIM, 2 * QDIM)), 'bkv_dca': jnp.zeros((2 * QDIM,), jnp.float32), 'qn_w': jnp.ones((HD,), jnp.float32), 'qn_b': jnp.zeros((HD,), jnp.float32), 'kn_w': jnp.ones((HD,), jnp.float32), 'kn_b': jnp.zeros((HD,), jnp.float32), 'kn_dca_w': jnp.ones((HD,), jnp.float32), 'kn_dca_b': jnp.zeros((HD,), jnp.float32), 'Wo': w(ks[6], (QDIM, QDIM)), 'bo': jnp.zeros((QDIM,), jnp.float32)}
    _L0_xattn_all = _L0_xattn_setup()
    _L0_xattn_in = {k: v for k, v in _L0_xattn_all.items() if k in ('Wq', 'bq', 'Wk', 'bk', 'Wv', 'bv', 'Wkv_dca', 'bkv_dca', 'qn_w', 'qn_b', 'kn_w', 'kn_b', 'kn_dca_w', 'kn_dca_b', 'Wo', 'bo')}
    del _L0_xattn_all

    def _L0_ffn_setup():
        import jax, jax.numpy as jnp
        import numpy as np
        FP8_MAX = 448.0
        GLOBAL_DIV = 448.0 * 6.0

        def _fp8(x):
            return x.astype(jnp.float8_e4m3fn).astype(jnp.float32)

        def _reorder_quantize_x(x, idx):
            scale = jnp.max(jnp.abs(x)) / GLOBAL_DIV
            xr = (x / scale)[:, idx]
            scale_x = jnp.max(jnp.abs(xr), axis=1, keepdims=True) / FP8_MAX
            qx = _fp8(xr / scale_x)
            return (qx, scale_x, scale)

        def _qlinear(qx, scale_x, scale, W, idx, out_idx=None):
            Wr = W[:, idx]
            w_scale = jnp.max(jnp.abs(Wr), axis=1, keepdims=True) / FP8_MAX
            qw = _fp8(Wr / w_scale)
            y = qx * scale_x @ (qw * w_scale).T * scale
            if out_idx is not None:
                y = y[:, out_idx]
            return y
        key = jax.random.key(seed)
        ks = jax.random.split(key, 6)
        B, S, H, I = (2, 128, 256, 704)
        return {'x': jax.random.normal(ks[0], (B, S, H), jnp.float32), 'w_gate': jax.random.normal(ks[1], (I, H), jnp.float32) * 0.02, 'w_up': jax.random.normal(ks[2], (I, H), jnp.float32) * 0.02, 'w_down': jax.random.normal(ks[3], (H, I), jnp.float32) * 0.02, 'up_reorder_index': jax.random.permutation(ks[4], jnp.arange(H, dtype=jnp.int64)), 'down_reorder_index': jax.random.permutation(ks[5], jnp.arange(I, dtype=jnp.int64))}
    _L0_ffn_all = _L0_ffn_setup()
    _L0_ffn_in = {k: v for k, v in _L0_ffn_all.items() if k in ('w_gate', 'w_up', 'w_down', 'up_reorder_index', 'down_reorder_index')}
    del _L0_ffn_all

    def _L1_xattn_setup():
        import jax, jax.numpy as jnp
        import numpy as np
        N_HEADS = 16
        N_KV_HEADS = 8
        HEAD_DIM = 128
        D_TEXT = 256
        D_VISION = 128
        GROUPS = N_HEADS // N_KV_HEADS
        key = jax.random.key(seed)
        ks = jax.random.split(key, 6)
        B, T_text, T_vis = (4, 256, 72)
        text_hidden = jax.random.normal(ks[0], (B, T_text, D_TEXT), dtype=jnp.float32)
        vision_tokens = jax.random.normal(ks[1], (B, T_vis, D_VISION), dtype=jnp.float32)
        vision_mask = jnp.ones((B, T_vis), dtype=bool)
        s = 0.02
        Wq = jax.random.normal(ks[2], (D_TEXT, N_HEADS * HEAD_DIM), dtype=jnp.float32) * s
        Wk = jax.random.normal(ks[3], (D_VISION, N_KV_HEADS * HEAD_DIM), dtype=jnp.float32) * s
        Wv = jax.random.normal(ks[4], (D_VISION, N_KV_HEADS * HEAD_DIM), dtype=jnp.float32) * s
        Wo = jax.random.normal(ks[5], (N_HEADS * HEAD_DIM, D_TEXT), dtype=jnp.float32) * s
        return {'text_hidden': text_hidden, 'vision_tokens': vision_tokens, 'vision_mask': vision_mask, 'Wq': Wq, 'Wk': Wk, 'Wv': Wv, 'Wo': Wo}
    _L1_xattn_all = _L1_xattn_setup()
    _L1_xattn_in = {k: v for k, v in _L1_xattn_all.items() if k in ('Wq', 'Wk', 'Wv', 'Wo')}
    del _L1_xattn_all

    def _L1_ffn_setup():
        import jax, jax.numpy as jnp
        import numpy as np
        CAPACITY_FACTOR = 1.0

        def _top1_gate(x, w_gate):
            S, E = (x.shape[0], w_gate.shape[1])
            capacity = int(CAPACITY_FACTOR * S / E)
            logits = x @ w_gate
            gates = jax.nn.softmax(logits, axis=-1)
            idx1 = jnp.argmax(gates, axis=-1)
            mask1 = jax.nn.one_hot(idx1, E, dtype=gates.dtype)
            locations1 = jnp.cumsum(mask1, axis=0) - mask1
            mask1 = mask1 * (locations1 < capacity)
            locations1_s = jnp.sum(locations1 * mask1, axis=1).astype(jnp.int32)
            gates_masked = gates * mask1
            loc_oh = jax.nn.one_hot(locations1_s, capacity, dtype=gates.dtype) * jnp.sum(mask1, axis=1, keepdims=True)
            combine_weights = jnp.einsum('se,sc->sec', gates_masked, loc_oh)
            dispatch_mask = (combine_weights > 0).astype(gates.dtype)
            return (combine_weights, dispatch_mask)
        key = jax.random.key(seed)
        k1, k2, k3, k4 = jax.random.split(key, 4)
        B, T, D, E, F = (4, 256, 256, 8, 1024)
        hidden_states = jax.random.normal(k1, (B, T, D), dtype=jnp.float32)
        w_gate = jax.random.normal(k2, (D, E), dtype=jnp.float32) * 0.02
        w1 = jax.random.normal(k3, (E, D, F), dtype=jnp.float32) * 0.02
        w2 = jax.random.normal(k4, (E, F, D), dtype=jnp.float32) * 0.02
        return {'hidden_states': hidden_states, 'w_gate': w_gate, 'w1': w1, 'w2': w2}
    _L1_ffn_all = _L1_ffn_setup()
    _L1_ffn_in = {k: v for k, v in _L1_ffn_all.items() if k in ('w_gate', 'w1', 'w2')}
    del _L1_ffn_all
    return {'x': x, 'ctx_1024': ctx_1024, 'mask_BxS2_bf1': mask_BxS2_bf1, 'g_xattn': g_xattn, 'g_ffn': g_ffn, 'L0_xattn_Wq': _L0_xattn_in['Wq'], 'L0_xattn_bq': _L0_xattn_in['bq'], 'L0_xattn_Wk': _L0_xattn_in['Wk'], 'L0_xattn_bk': _L0_xattn_in['bk'], 'L0_xattn_Wv': _L0_xattn_in['Wv'], 'L0_xattn_bv': _L0_xattn_in['bv'], 'L0_xattn_Wkv_dca': _L0_xattn_in['Wkv_dca'], 'L0_xattn_bkv_dca': _L0_xattn_in['bkv_dca'], 'L0_xattn_qn_w': _L0_xattn_in['qn_w'], 'L0_xattn_qn_b': _L0_xattn_in['qn_b'], 'L0_xattn_kn_w': _L0_xattn_in['kn_w'], 'L0_xattn_kn_b': _L0_xattn_in['kn_b'], 'L0_xattn_kn_dca_w': _L0_xattn_in['kn_dca_w'], 'L0_xattn_kn_dca_b': _L0_xattn_in['kn_dca_b'], 'L0_xattn_Wo': _L0_xattn_in['Wo'], 'L0_xattn_bo': _L0_xattn_in['bo'], 'L0_ffn_w_gate': _L0_ffn_in['w_gate'], 'L0_ffn_w_up': _L0_ffn_in['w_up'], 'L0_ffn_w_down': _L0_ffn_in['w_down'], 'L0_ffn_up_reorder_index': _L0_ffn_in['up_reorder_index'], 'L0_ffn_down_reorder_index': _L0_ffn_in['down_reorder_index'], 'L1_xattn_Wq': _L1_xattn_in['Wq'], 'L1_xattn_Wk': _L1_xattn_in['Wk'], 'L1_xattn_Wv': _L1_xattn_in['Wv'], 'L1_xattn_Wo': _L1_xattn_in['Wo'], 'L1_ffn_w_gate': _L1_ffn_in['w_gate'], 'L1_ffn_w1': _L1_ffn_in['w1'], 'L1_ffn_w2': _L1_ffn_in['w2']}

def reference(x, ctx_1024, mask_BxS2_bf1, g_xattn, g_ffn, L0_xattn_Wq, L0_xattn_bq, L0_xattn_Wk, L0_xattn_bk, L0_xattn_Wv, L0_xattn_bv, L0_xattn_Wkv_dca, L0_xattn_bkv_dca, L0_xattn_qn_w, L0_xattn_qn_b, L0_xattn_kn_w, L0_xattn_kn_b, L0_xattn_kn_dca_w, L0_xattn_kn_dca_b, L0_xattn_Wo, L0_xattn_bo, L0_ffn_w_gate, L0_ffn_w_up, L0_ffn_w_down, L0_ffn_up_reorder_index, L0_ffn_down_reorder_index, L1_xattn_Wq, L1_xattn_Wk, L1_xattn_Wv, L1_xattn_Wo, L1_ffn_w_gate, L1_ffn_w1, L1_ffn_w2):
    import jax
    import jax.numpy as jnp

    def _L0_xattn_ref(x, y, Wq, bq, Wk, bk, Wv, bv, Wkv_dca, bkv_dca, qn_w, qn_b, kn_w, kn_b, kn_dca_w, kn_dca_b, Wo, bo):
        import jax, jax.numpy as jnp
        import numpy as np
        B, S1, S2, DCA = (2, 256, 128, 16)
        QDIM, KDIM, H = (256, 128, 16)
        HD = QDIM // H
        SCALE = HD ** (-0.5)
        EPS = 1e-06
        DCA_WEIGHT = 1.0

        def _ln(t, w, b):
            m = jnp.mean(t, axis=-1, keepdims=True)
            v = jnp.var(t, axis=-1, keepdims=True)
            return (t - m) * jax.lax.rsqrt(v + EPS) * w + b

        def _attn(q, k, v):
            s = jnp.einsum('bhqd,bhkd->bhqk', q, k) * SCALE
            p = jax.nn.softmax(s, axis=-1)
            return jnp.einsum('bhqk,bhkd->bhqd', p, v)
        b, s1, _ = x.shape
        y_dca = y[:, -DCA:, :]
        y_main = y[:, :-DCA, :]
        kv_dca = (y_dca @ Wkv_dca + bkv_dca).reshape(b, DCA, 2, H, HD)
        k_dca = _ln(kv_dca[:, :, 0], kn_dca_w, kn_dca_b)
        v_dca = kv_dca[:, :, 1]
        s2 = y_main.shape[1]
        q = _ln((x @ Wq + bq).reshape(b, s1, H, HD), qn_w, qn_b)
        kv = jnp.concatenate([y_main @ Wk + bk, y_main @ Wv + bv], axis=-1)
        kv = kv.reshape(b, s2, H, 2 * HD)
        k = _ln(kv[..., :HD], kn_w, kn_b)
        v = kv[..., HD:]
        qT = q.transpose(0, 2, 1, 3)
        ctx = _attn(qT, k.transpose(0, 2, 1, 3), v.transpose(0, 2, 1, 3))
        ctx = ctx.transpose(0, 2, 1, 3).reshape(b, s1, QDIM)
        ctx_dca = _attn(qT, k_dca.transpose(0, 2, 1, 3), v_dca.transpose(0, 2, 1, 3))
        ctx_dca = ctx_dca.transpose(0, 2, 1, 3).reshape(b, s1, QDIM)
        ctx = ctx + DCA_WEIGHT * ctx_dca
        return ctx @ Wo + bo

    def _L0_ffn_ref(x, w_gate, w_up, w_down, up_reorder_index, down_reorder_index):
        import jax, jax.numpy as jnp
        import numpy as np
        FP8_MAX = 448.0
        GLOBAL_DIV = 448.0 * 6.0

        def _fp8(x):
            return x.astype(jnp.float8_e4m3fn).astype(jnp.float32)

        def _reorder_quantize_x(x, idx):
            scale = jnp.max(jnp.abs(x)) / GLOBAL_DIV
            xr = (x / scale)[:, idx]
            scale_x = jnp.max(jnp.abs(xr), axis=1, keepdims=True) / FP8_MAX
            qx = _fp8(xr / scale_x)
            return (qx, scale_x, scale)

        def _qlinear(qx, scale_x, scale, W, idx, out_idx=None):
            Wr = W[:, idx]
            w_scale = jnp.max(jnp.abs(Wr), axis=1, keepdims=True) / FP8_MAX
            qw = _fp8(Wr / w_scale)
            y = qx * scale_x @ (qw * w_scale).T * scale
            if out_idx is not None:
                y = y[:, out_idx]
            return y
        B, S, H = x.shape
        xf = x.reshape(B * S, H)
        qx, sx, sc = _reorder_quantize_x(xf, up_reorder_index)
        g = _qlinear(qx, sx, sc, w_gate, up_reorder_index, out_idx=down_reorder_index)
        u = _qlinear(qx, sx, sc, w_up, up_reorder_index, out_idx=down_reorder_index)
        t = jax.nn.silu(g) * u
        qt, st, sct = _reorder_quantize_x(t, down_reorder_index)
        y = _qlinear(qt, st, sct, w_down, down_reorder_index)
        return y.reshape(B, S, H)

    def _L1_xattn_ref(text_hidden, vision_tokens, vision_mask, Wq, Wk, Wv, Wo):
        import jax, jax.numpy as jnp
        import numpy as np
        N_HEADS = 16
        N_KV_HEADS = 8
        HEAD_DIM = 128
        D_TEXT = 256
        D_VISION = 128
        GROUPS = N_HEADS // N_KV_HEADS
        B, T_text, _ = text_hidden.shape
        T_vis = vision_tokens.shape[1]
        scale = jnp.float32(np.sqrt(HEAD_DIM))
        q = (text_hidden @ Wq).reshape(B, T_text, N_HEADS, HEAD_DIM).transpose(0, 2, 1, 3)
        k = (vision_tokens @ Wk).reshape(B, T_vis, N_KV_HEADS, HEAD_DIM).transpose(0, 2, 1, 3)
        v = (vision_tokens @ Wv).reshape(B, T_vis, N_KV_HEADS, HEAD_DIM).transpose(0, 2, 1, 3)
        k = jnp.repeat(k, GROUPS, axis=1)
        v = jnp.repeat(v, GROUPS, axis=1)
        scores = jnp.einsum('bhtd,bhsd->bhts', q, k) / scale
        mask = vision_mask[:, None, None, :]
        scores = jnp.where(mask, scores, -jnp.inf)
        attn = jax.nn.softmax(scores, axis=-1)
        attn = jnp.nan_to_num(attn, nan=0.0)
        out = jnp.einsum('bhts,bhsd->bhtd', attn, v)
        out = out.transpose(0, 2, 1, 3).reshape(B, T_text, N_HEADS * HEAD_DIM)
        return out @ Wo

    def _L1_ffn_ref(hidden_states, w_gate, w1, w2):
        import jax, jax.numpy as jnp
        import numpy as np
        CAPACITY_FACTOR = 1.0

        def _top1_gate(x, w_gate):
            S, E = (x.shape[0], w_gate.shape[1])
            capacity = int(CAPACITY_FACTOR * S / E)
            logits = x @ w_gate
            gates = jax.nn.softmax(logits, axis=-1)
            idx1 = jnp.argmax(gates, axis=-1)
            mask1 = jax.nn.one_hot(idx1, E, dtype=gates.dtype)
            locations1 = jnp.cumsum(mask1, axis=0) - mask1
            mask1 = mask1 * (locations1 < capacity)
            locations1_s = jnp.sum(locations1 * mask1, axis=1).astype(jnp.int32)
            gates_masked = gates * mask1
            loc_oh = jax.nn.one_hot(locations1_s, capacity, dtype=gates.dtype) * jnp.sum(mask1, axis=1, keepdims=True)
            combine_weights = jnp.einsum('se,sc->sec', gates_masked, loc_oh)
            dispatch_mask = (combine_weights > 0).astype(gates.dtype)
            return (combine_weights, dispatch_mask)
        B, T, D = hidden_states.shape
        x = hidden_states.reshape(-1, D)
        combine_weights, dispatch_mask = _top1_gate(x, w_gate)
        dispatched = jnp.einsum('sec,sm->ecm', dispatch_mask, x)
        h = jax.nn.gelu(jnp.einsum('ecd,edf->ecf', dispatched, w1))
        expert_out = jnp.einsum('ecf,efd->ecd', h, w2)
        combined = jnp.einsum('sec,ecm->sm', combine_weights, expert_out)
        return combined.reshape(B, T, D)
    x = x + jnp.tanh(g_xattn[0]) * _L0_xattn_ref(_layernorm(x, axis=-1), ctx_1024, L0_xattn_Wq, L0_xattn_bq, L0_xattn_Wk, L0_xattn_bk, L0_xattn_Wv, L0_xattn_bv, L0_xattn_Wkv_dca, L0_xattn_bkv_dca, L0_xattn_qn_w, L0_xattn_qn_b, L0_xattn_kn_w, L0_xattn_kn_b, L0_xattn_kn_dca_w, L0_xattn_kn_dca_b, L0_xattn_Wo, L0_xattn_bo)
    x = x + jnp.tanh(g_ffn[0]) * _L0_ffn_ref(_layernorm(x, axis=-1), L0_ffn_w_gate, L0_ffn_w_up, L0_ffn_w_down, L0_ffn_up_reorder_index, L0_ffn_down_reorder_index)
    x = x + jnp.tanh(g_xattn[1]) * _L1_xattn_ref(_layernorm(x, axis=-1), ctx_1024, mask_BxS2_bf1, L1_xattn_Wq, L1_xattn_Wk, L1_xattn_Wv, L1_xattn_Wo)
    x = x + jnp.tanh(g_ffn[1]) * _L1_ffn_ref(_layernorm(x, axis=-1), L1_ffn_w_gate, L1_ffn_w1, L1_ffn_w2)
    return x

_drawn_inputs = setup_inputs


def setup_inputs(seed=0):
    import zlib

    import numpy as np

    out = dict(_drawn_inputs(seed))
    spreads = {'g_ffn': (-1.0, 0.6),
     'L0_xattn_bq': (0.0, 0.8),
     'L0_xattn_bk': (0.0, 0.523),
     'L0_xattn_bv': (0.0, 0.429),
     'L0_xattn_bkv_dca': (0.0, 0.318),
     'L0_xattn_qn_w': (1.0, 0.6),
     'L0_xattn_qn_b': (0.0, 0.8),
     'L0_xattn_kn_w': (1.0, 0.6),
     'L0_xattn_kn_b': (0.0, 0.8),
     'L0_xattn_kn_dca_w': (1.0, 0.6),
     'L0_xattn_kn_dca_b': (0.0, 0.8),
     'L0_xattn_bo': (0.0, 0.1)}
    factors = {'L0_xattn_Wq': 3.36,
     'L0_xattn_Wk': 2.78,
     'L0_xattn_Wv': 2.737,
     'L1_xattn_Wq': 8.0,
     'L1_xattn_Wk': 8.0,
     'L1_ffn_w_gate': 3.554,
     'L1_ffn_w1': 3.397,
     'L1_ffn_w2': 3.319}
    for name, (base, spread) in spreads.items():
        noise = np.random.default_rng([zlib.crc32(name.encode()), seed]).standard_normal(out[name].shape)
        drawn = base * np.exp(spread * noise) if base else spread * noise
        out[name] = jnp.asarray(drawn.astype(out[name].dtype))
    for name, factor in factors.items():
        out[name] = (out[name] * factor).astype(out[name].dtype)
    return out
```

```python
from contextlib import ExitStack

import concourse.bass as bass
from concourse import mybir
from concourse.alu_op_type import AluOpType as ALU

ACT = mybir.ActivationFunctionType
AX = mybir.AxisListType
F32 = mybir.dt.float32
BF16 = mybir.dt.bfloat16
U32 = mybir.dt.uint32
I32 = mybir.dt.int32
U8 = mybir.dt.uint8

P = 128
BATCH, SEQ, D = 32, 56, 256
KEYS, DC = 1500, 128
PAIRS = BATCH // 2
TT = 2 * SEQ
NT = PAIRS
TOK = BATCH * SEQ
DK = D // P
BANK = 512
HEADS = 16
HQ = HEADS * SEQ
HALF = HQ // 2
QT = HQ // P
CHUNKS = 12
LN_EPS = 1e-5

HD0 = 16
DCA = 16
MAIN = KEYS - DCA
QK_EPS = 1e-6
CH0 = 124
SPAN0 = 4 * CH0
STEP0 = (MAIN - SPAN0) // 2
DUP0 = SPAN0 - STEP0
SCALE0 = HD0 ** -0.5


class Turns:

    def __init__(self, prologue, first, middle, last, epilogue):
        self.lists = {"pro": prologue, "first": first, "mid": middle, "last": last, "epi": epilogue}
        self.base = {"pro": 0, "first": len(prologue)}
        self.base["mid"] = self.base["first"] + len(first)
        self.base["last"] = self.base["mid"] + (PAIRS - 2) * len(middle)
        self.base["epi"] = self.base["last"] + len(last)

    def number(self, part, pair, unit):
        n = self.base[part] + self.lists[part].index(unit)
        if part == "mid":
            return (pair - 1) * len(self.lists["mid"]) + n
        return n


def at_least(eng, sem, value):
    if isinstance(value, int) and value <= 0:
        return
    eng.wait_ge(sem, value)


def wait_alone(k, eng, sem, value):
    eng.wait_ge(sem, value).then_inc(k.waits_passed, 1)


class Chain:

    def __init__(self, eng, sem):
        self.eng, self.sem, self.n = eng, sem, 0

    def mark(self, ins):
        ins.then_inc(self.sem, 1)
        self.n += 1
        return self.n

    def settle(self):
        self.eng.wait_ge(self.sem, self.n)


class Kit:

    def __init__(self, nc, inputs, out):
        self.nc, self.i, self.out = nc, inputs, out
        self.keep = ExitStack()

    def sem(self, name):
        return self.keep.enter_context(self.nc.semaphore(name))

    def sems(self, *names):
        return [self.sem(n) for n in names]

    def sbuf(self, stack, name, shape, dt=F32):
        return stack.enter_context(self.nc.sbuf_tensor(name, shape, dt))

    def bank(self, n, rows, cols, at=0):
        lo = n * BANK + at
        return self.psum[rows[0]:rows[1], lo:lo + cols]

    def banks(self, n, count, rows, cols):
        return self.psum[rows[0]:rows[1], n * BANK:(n + count) * BANK].rearrange(
            "p (b c) -> p b c", c=BANK)[:, :, 0:cols]


def make_persistent(k):
    k.psum = k.keep.enter_context(k.nc.psum_tensor("psum", [P, 8 * BANK], F32))
    sb = lambda name, shape, dt=F32: k.sbuf(k.keep, name, shape, dt)
    k.resid = sb("resid", [TT, NT, D])
    k.ident = sb("ident", [P, P])
    k.ident_bf = sb("ident_bf", [P, P], BF16)
    k.ones_row = sb("ones_row", [1, P])
    k.bn = sb("bn", [TT, NT, 6])
    k.moments = sb("moments", [TT, NT, 2])
    k.var_eps = sb("var_eps", [TT, NT])
    k.log_var = sb("log_var", [TT, NT])
    k.rough = sb("rough", [TT, NT])
    k.newton = sb("newton", [TT, NT])
    k.newton2 = sb("newton2", [TT, NT])
    k.rstd = sb("rstd", [TT, NT])
    k.eps_ln = sb("eps_ln", [P, 1])
    k.eps_qk = sb("eps_qk", [P, 1])
    k.gates = sb("gates", [P, 4])
    k.gates_raw = sb("gates_raw", [1, 4])
    k.gates_th = sb("gates_th", [1, 4])
    k.norm = Norm(k)
    k.waits_passed = k.sem("waits_passed")
    with ExitStack() as s:
        k.normed = k.sbuf(s, "normed", [TT, NT, D])
        k.normed_t = k.sbuf(s, "normed_t", [P, DK, TOK])
    with ExitStack() as s:
        k.probs = [k.sbuf(s, f"probs{i}", [P, 2, HALF]) for i in range(2)]
        k.heads_n = k.sbuf(s, "heads_n", [P, QT, DC])
        k.heads_dn = k.sbuf(s, "heads_dn", [P, QT, DC])
        k.heads_t = k.sbuf(s, "heads_t", [DC, HEADS, 2, SEQ])
        k.heads_dt = k.sbuf(s, "heads_dt", [DC, HEADS, 2, SEQ])
    k.sbuf(k.keep, "norm_area", [P, NT * D + DK * TOK])


class Turner:

    def __init__(self, k):
        self.k, self.runs = k, 0
        self.turned, self.copied_a, self.copied_v = k.sems("turned", "copied_a", "copied_v")

    def start_turn(self, tiles_counted=False):
        self.base = self.runs * (NT // 4)
        self.tiles_counted = tiles_counted
        self.runs += 1

    def _group(self, g, piece):
        return self.k.bank(2 * (g % 2) + piece, (0, P), 4 * TT)

    def tensor(self, pe):
        k = self.k
        for t in range(NT):
            g = t // 4
            if self.tiles_counted:
                self.wait_tiles(pe, t + 1)
            if t % 4 == 0 and g >= 2:
                pe.wait_ge(self.copied_a, self.base + g - 1)
                pe.wait_ge(self.copied_v, self.base + g - 1)
            for c in range(DK):
                last = pe.transpose(self._group(g, c)[:, (t % 4) * TT:(t % 4 + 1) * TT],
                                    k.normed[:, t, c * P:(c + 1) * P], k.ident[0:TT, 0:TT])
            if t % 4 == 3:
                last.then_inc(self.turned, 1)

    def copy_scalar(self, a):
        k = self.k
        for g in range(NT // 4):
            a.wait_ge(self.turned, self.base + g + 1)
            a.activation(k.normed_t[:, 0, g * 4 * TT:(g + 1) * 4 * TT], self._group(g, 0),
                         ACT.Identity).then_inc(self.copied_a, 1)

    def copy_vector(self, v):
        k = self.k
        for g in range(NT // 4):
            v.wait_ge(self.turned, self.base + g + 1)
            v.tensor_copy(k.normed_t[:, 1, g * 4 * TT:(g + 1) * 4 * TT],
                          self._group(g, 1)).then_inc(self.copied_v, 1)

    def wait_all(self, eng):
        eng.wait_ge(self.copied_a, self.base + NT // 4)
        eng.wait_ge(self.copied_v, self.base + NT // 4)


class Norm(Turner):

    def __init__(self, k):
        super().__init__(k)
        self.norms = 0
        self.stats, self.rough, self.tile, self.log_done = k.sems(
            "norm_stats", "norm_rough", "norm_tile", "norm_log")

    def start(self):
        self.norms += 1
        self.start_turn(tiles_counted=True)
        return self

    def wait_tiles(self, eng, count):
        eng.wait_ge(self.tile, NT * (self.norms - 1) + count)

    def vector(self, v, chain):
        k = self.k
        for t in range(NT):
            chain.mark(v.bn_stats(k.bn[:, t, :], k.resid[:, t, :]))
        chain.settle()
        for t in range(NT):
            chain.mark(v.bn_aggr(k.moments[:, t, :], k.bn[:, t, :]))
        chain.settle()
        v.tensor_scalar(k.var_eps[:, :], k.moments[:, :, 1], LN_EPS, None, ALU.add).then_inc(self.stats, 1)
        v.wait_ge(self.stats, self.norms)
        v.wait_ge(self.rough, self.norms)
        chain.mark(v.tensor_tensor(k.newton[:, :], k.var_eps[:, :], k.rough[:, :], ALU.mult))
        chain.settle()
        chain.mark(v.tensor_tensor(k.newton2[:, :], k.newton[:, :], k.rough[:, :], ALU.mult))
        chain.settle()
        chain.mark(v.tensor_scalar(k.newton[:, :], k.newton2[:, :], -0.5, 1.5, ALU.mult, ALU.add))
        chain.settle()
        chain.mark(v.tensor_tensor(k.rstd[:, :], k.newton[:, :], k.rough[:, :], ALU.mult))
        chain.settle()
        for t in range(NT):
            v.tensor_scalar(k.normed[:, t, :], k.resid[:, t, :], k.moments[:, t, 0:1],
                            k.rstd[:, t:t + 1], ALU.subtract, ALU.mult).then_inc(self.tile, 1)

    def scalar(self, a):
        k = self.k
        a.wait_ge(self.stats, self.norms)
        a.activation(k.log_var[:, :], k.var_eps[:, :], ACT.Ln).then_inc(self.log_done, 1)
        a.wait_ge(self.log_done, self.norms)
        a.activation(k.rough[:, :], k.log_var[:, :], ACT.Exp, scale=-0.5).then_inc(self.rough, 1)



def layer0_memory(k, s):
    sb = lambda name, shape, dt=F32: k.sbuf(s, name, shape, dt)
    k.q_all = sb("q_all", [P, 2, TOK])
    k.wq = sb("wq", [P, DK, D])
    k.wk = sb("wk", [DC, D])
    k.wkv_d = sb("wkv_d", [DC, 2 * D])
    k.wv = sb("wv", [DC, D])
    k.wo0 = sb("wo0", [P, DK, D])
    k.wmean = sb("wmean", [P, 4, HEADS])
    k.same_head = sb("same_head", [P, P])
    k.head_mask = sb("head_mask", [P, 8])
    k.rep16 = sb("rep16", [HD0, P])
    k.small16 = sb("small16", [HD0, 6])
    k.lnwb = sb("lnwb", [P, 6])
    k.bias_in = sb("bias_in", [P, 6])
    k.bias_c = sb("bias_c", [P, 6])
    k.bv_in = sb("bv_in", [P, 4])
    k.bv_sum = sb("bv_sum", [P, 2])
    k.bo_row = sb("bo_row", [1, D])
    k.bo_b = sb("bo_b", [TT, D])
    k.pick = sb("pick", [2, 2, P], BF16)
    k.wv_pad = sb("wv_pad", [P, 2, 2, 8 * 144])
    with ExitStack() as tmp:
        k.qtmp, k.qsq, k.qlog, k.qrs, k.qhat = (k.sbuf(tmp, name, [P, 2, 4 * TT]) for name in (
            "qtmp", "qsq", "qlog", "qrs", "qhat"))
    k.keys = [sb(f"keys{i}", [P, 2, 3, BANK]) for i in range(2)]
    k.rows_raw = [sb(f"rows_raw{i}", [CH0, CHUNKS, DC]) for i in range(2)]
    k.rows_pv = [sb(f"rows_pv{i}", [CH0, CHUNKS, DC + 1]) for i in range(2)]
    k.rows_d = [sb(f"rows_d{i}", [DCA, DC + 1]) for i in range(2)]
    k.ctx_t = sb("ctx_t", [DC, 3, BANK])
    k.kc = sb("kc", [P, 2, 3, BANK])
    k.ksq = sb("ksq", [P, 2, 3, BANK])
    k.krs = sb("krs", [P, 3, BANK])
    k.klog = sb("klog", [P, 3, BANK])
    k.keys_bf = sb("keys_bf", [P, 2, 3, BANK], BF16)
    k.q_diag = [sb(f"q_diag{i}", [P, 2, 8, SEQ]) for i in range(2)]
    k.q_diag_bf = sb("q_diag_bf", [P, 2, 8, SEQ], BF16)
    k.shift_col = sb("shift_col", [TT, 2, 8], BF16)
    k.shift_row = [sb(f"shift_row{i}", [2, 2, HALF], BF16) for i in range(2)]
    k.probs_d = sb("probs_d", [DCA, 2, HALF])
    k.rsum = sb("rsum", [P, QT])
    k.rsum_d = sb("rsum_d", [P, QT])
    k.att_t = sb("att_t", [P, 2, TT])
    k.ytmp = sb("ytmp", [TT, D])


def setup(k):
    nc, i = k.nc, k.i
    norm = k.norm.start()
    (ld_x, ld_small, ld_w, consts, pool_own, w_ready, pe_small, small_ready, q_full, q_cen, q_log,
     q_rstd, q_var, q_hat, q_done, vec, gates_rd, gates_bc, act_own, q_read) = k.sems(
        "ld_x", "ld_small", "ld_w", "consts", "pool_own", "w_ready", "pe_small", "small_ready",
        "q_full", "q_cen", "q_log", "q_rstd", "q_var", "q_hat", "q_done", "vec", "gates_rd",
        "gates_bc", "act_own", "q_read")
    k.vec = vec
    N_SMALL = 6 + 3 + 2 + 1 + 4
    GROUP = 4 * TT

    with nc.Block() as block:
        @block.sync
        def _(sp):
            x_tiles = i["x"].rearrange("(t b) s d -> (b s) t d", b=2)
            sp.dma_start(k.resid[:, 0:8, :], x_tiles[:, 0:8, :]).then_inc(ld_x, 16)
            sp.dma_start(k.resid[:, 8:16, :], x_tiles[:, 8:16, :]).then_inc(ld_x, 16)
            sp.dma_start(k.wq[:, :, :], i["L0_xattn_Wq"].rearrange("(c p) n -> p c n", p=P)).then_inc(ld_w, 16)
            sp.dma_start(k.wk[:, :], i["L0_xattn_Wk"]).then_inc(ld_w, 16)
            sp.dma_start(k.wkv_d[:, :], i["L0_xattn_Wkv_dca"]).then_inc(ld_w, 16)
            sp.dma_start(k.wv[:, :], i["L0_xattn_Wv"]).then_inc(ld_w, 16)
            sp.dma_start(k.wo0[:, :, :], i["L0_xattn_Wo"].rearrange("(c p) n -> p c n", p=P)).then_inc(ld_w, 16)

        @block.gpsimd
        def _(g):
            g.memset(k.ident[:, :], 0.0).then_inc(pool_own, 1)
            g.memset(k.same_head[:, :], 1.0 / HD0).then_inc(pool_own, 1)
            g.memset(k.head_mask[:, :], 1.0).then_inc(pool_own, 1)
            g.memset(k.rep16[:, :], 0.0).then_inc(pool_own, 1)
            g.memset(k.pick[:, :, :], 0.0).then_inc(pool_own, 1)
            g.wait_ge(pool_own, 5)
            g.affine_select(out=k.ident[:, :], in_=k.ident[:, :], compare_op=ALU.not_equal, fill=1.0,
                            base=0, pattern=[[-1, P]], channel_multiplier=1).then_inc(pool_own, 1)
            heads = k.same_head[:, :].rearrange("p (e d) -> p e d", d=HD0)
            g.affine_select(out=heads, in_=heads, compare_op=ALU.is_ge, fill=0.0, base=0,
                            pattern=[[-HD0, 8], [0, HD0]], channel_multiplier=1).then_inc(pool_own, 1)
            g.affine_select(out=k.head_mask[:, :], in_=k.head_mask[:, :], compare_op=ALU.is_ge, fill=0.0,
                            base=0, pattern=[[-HD0, 8]], channel_multiplier=1).then_inc(pool_own, 1)
            rep = k.rep16[:, :].rearrange("p (e d) -> p e d", d=HD0)
            g.affine_select(out=rep, in_=rep, compare_op=ALU.not_equal, fill=1.0, base=0,
                            pattern=[[0, 8], [-1, HD0]], channel_multiplier=1).then_inc(pool_own, 1)
            g.affine_select(out=k.pick[:, :, :], in_=k.pick[:, :, :], compare_op=ALU.not_equal, fill=1.0,
                            base=0, pattern=[[-1, 2], [0, P]], channel_multiplier=1).then_inc(pool_own, 1)
            g.wait_ge(pool_own, 10)
            g.affine_select(out=heads, in_=heads, compare_op=ALU.is_ge, fill=0.0, base=HD0 - 1,
                            pattern=[[HD0, 8], [0, HD0]], channel_multiplier=-1).then_inc(pool_own, 1)
            g.affine_select(out=k.head_mask[:, :], in_=k.head_mask[:, :], compare_op=ALU.is_ge, fill=0.0,
                            base=HD0 - 1, pattern=[[HD0, 8]], channel_multiplier=-1).then_inc(pool_own, 1)
            g.tensor_copy(k.ident_bf[:, :], k.ident[:, :]).then_inc(pool_own, 1)
            g.memset(k.ones_row[:, :], 1.0).then_inc(pool_own, 1)
            g.memset(k.eps_ln[:, :], LN_EPS).then_inc(pool_own, 1)
            g.memset(k.eps_qk[:, :], QK_EPS).then_inc(pool_own, 1)
            g.wait_ge(pool_own, 16)
            g.memset(k.wv_pad[:, :, :, :], 0.0).then_inc(consts, 1)
            for n, name in enumerate(("qn_w", "qn_b", "kn_w", "kn_b", "kn_dca_w", "kn_dca_b")):
                g.dma_start(k.small16[:, n:n + 1],
                            i["L0_xattn_" + name].rearrange("(d o) -> d o", o=1)).then_inc(ld_small, 16)
            rows = lambda v: v.rearrange("(c p) -> p c", p=P)
            g.dma_start(k.bias_in[:, 0:2], rows(i["L0_xattn_bq"]), allow_slow_non_contiguous=True).then_inc(ld_small, 16)
            g.dma_start(k.bias_in[:, 2:4], rows(i["L0_xattn_bk"]), allow_slow_non_contiguous=True).then_inc(ld_small, 16)
            g.dma_start(k.bias_in[:, 4:6], rows(i["L0_xattn_bkv_dca"][0:D]), allow_slow_non_contiguous=True).then_inc(ld_small, 16)
            g.dma_start(k.bv_in[:, 0:2], rows(i["L0_xattn_bv"]), allow_slow_non_contiguous=True).then_inc(ld_small, 16)
            g.dma_start(k.bv_in[:, 2:4], rows(i["L0_xattn_bkv_dca"][D:2 * D]), allow_slow_non_contiguous=True).then_inc(ld_small, 16)
            g.dma_start(k.bo_row[:, :], i["L0_xattn_bo"].rearrange("(o d) -> o d", o=1)).then_inc(ld_small, 16)
            g.dma_start(k.gates_raw[:, 0:2], i["g_xattn"].rearrange("(o d) -> o d", o=1)).then_inc(ld_small, 16)
            g.dma_start(k.gates_raw[:, 2:4], i["g_ffn"].rearrange("(o d) -> o d", o=1)).then_inc(ld_small, 16)
            for n in range(2):
                g.memset(k.rows_pv[n][:, :, DC:DC + 1], 1.0).then_inc(consts, 1)
                g.memset(k.rows_d[n][:, DC:DC + 1], 1.0).then_inc(consts, 1)
            g.memset(k.kc[:, :, :, :], 0.0).then_inc(consts, 1)
            g.memset(k.ksq[:, :, :, :], 0.0).then_inc(consts, 1)
            g.wait_ge(consts, 7)

        @block.vector
        def _(v):
            chain = Chain(v, vec)
            v.wait_ge(ld_w, 80)
            groups = ((k.wq[:, 0, :], 0), (k.wq[:, 1, :], 1), (k.wk[:, :], 2), (k.wkv_d[:, 0:D], 3))
            for w, n in groups:
                chain.mark(v.tensor_reduce(k.wmean[:, n, :], w.rearrange("p (h d) -> p h d", d=HD0),
                                           AX.X, ALU.add))
            chain.settle()
            chain.mark(v.tensor_scalar(k.wmean[:, :, :], k.wmean[:, :, :], 1.0 / HD0, None, ALU.mult))
            chain.settle()
            for w, n in groups:
                w3 = w.rearrange("p (h d) -> p h d", d=HD0)
                v.tensor_tensor(w3, w3, k.wmean[:, n, :].unsqueeze(2).to_broadcast([P, HEADS, HD0]),
                                ALU.subtract).then_inc(w_ready, 1)
            v.wait_ge(consts, 1)
            for s, w in ((0, k.wv[:, :]), (1, k.wkv_d[:, D:2 * D])):
                for h in range(2):
                    diag = k.wv_pad[:, s, h, :].rearrange("p (e s) -> p e s", s=144)[:, :, 0:HD0]
                    src = w[:, h * P:(h + 1) * P].rearrange("p (e d) -> p e d", d=HD0)
                    v.tensor_copy(diag, src).then_inc(w_ready, 1)
            v.wait_ge(ld_x, 32)
            norm.vector(v, chain)
            v.wait_ge(ld_small, 16 * 14)
            v.wait_ge(pe_small, 1)
            v.tensor_copy(k.lnwb[:, :], k.bank(4, (0, P), 6)).then_inc(small_ready, 1)
            v.tensor_tensor(k.bias_c[:, :], k.bias_in[:, :], k.bank(4, (0, P), 6, 8), ALU.subtract
                            ).then_inc(small_ready, 1)
            v.tensor_tensor(k.bv_sum[:, :], k.bv_in[:, 0:2], k.bv_in[:, 2:4], ALU.add
                            ).then_inc(small_ready, 1)
            v.tensor_copy(k.bo_b[:, :], k.bank(5, (0, TT), D)).then_inc(small_ready, 1)
            v.tensor_copy(k.gates[:, :], k.bank(4, (0, P), 4, 16)).then_inc(small_ready, 1)
            norm.copy_vector(v)
            for n in range(8):
                g, h = divmod(n, 2)
                v.wait_ge(q_rstd, n + 1)
                v.wait_ge(small_ready, 5)
                v.tensor_tensor(k.qhat[:, n % 2, :], k.qtmp[:, n % 2, :], k.qrs[:, n % 2, :],
                                ALU.mult).then_inc(q_hat, 1)
                v.wait_ge(q_hat, n + 1)
                v.tensor_scalar(k.q_all[:, h, g * GROUP:(g + 1) * GROUP], k.qhat[:, n % 2, :],
                                k.lnwb[:, 0:1], k.lnwb[:, 1:2], ALU.mult, ALU.add).then_inc(q_done, 1)
            v.wait_ge(q_done, 8)
            v.wait_ge(w_ready, 8)

        @block.tensor
        def _(pe):
            pe.wait_ge(pool_own, 16)
            pe.wait_ge(ld_small, 16 * 14)
            pe.wait_ge(gates_rd, 1)
            pe.matmul(k.bank(4, (0, P), 6), k.rep16[:, :], k.small16[:, :], start=True, stop=True)
            pe.matmul(k.bank(4, (0, P), 6, 8), k.same_head[:, :], k.bias_in[:, :], start=True, stop=True)
            pe.matmul(k.bank(4, (0, P), 4, 16), k.ones_row[:, :], k.gates_th[:, :], start=True, stop=True)
            pe.matmul(k.bank(5, (0, TT), D), k.ones_row[:, 0:TT], k.bo_row[:, :], start=True,
                      stop=True).then_inc(pe_small, 1)
            norm.tensor(pe)
            norm.wait_all(pe)
            pe.wait_ge(w_ready, 4)
            for n in range(9):
                if n < 8:
                    g, h = divmod(n, 2)
                    q = k.bank(n % 2, (0, P), GROUP)
                    if n >= 2:
                        pe.wait_ge(q_cen, n - 1)
                    for c in range(DK):
                        last = pe.matmul(q, k.wq[:, c, h * P:(h + 1) * P],
                                         k.normed_t[:, c, g * GROUP:(g + 1) * GROUP],
                                         start=(c == 0), stop=(c == DK - 1))
                    last.then_inc(q_full, 1)
                if n >= 1:
                    m = n - 1
                    pe.wait_ge(q_cen, m + 1)
                    if m >= 2:
                        pe.wait_ge(q_log, m - 1)
                    pe.matmul(k.bank(2 + m % 2, (0, P), GROUP), k.same_head[:, :], k.qsq[:, m % 2, :],
                              start=True, stop=True).then_inc(q_var, 1)

        @block.scalar
        def _(a):
            a.wait_ge(ld_small, 16 * 14)
            a.activation(k.gates_th[:, :], k.gates_raw[:, :], ACT.Tanh).then_inc(gates_rd, 1)
            norm.scalar(a)
            norm.copy_scalar(a)
            a.wait_ge(small_ready, 5)
            a.wait_ge(pool_own, 16)
            for n in range(9):
                if n < 8:
                    h = n % 2
                    a.wait_ge(q_full, n + 1)
                    if n >= 2:
                        a.wait_ge(q_hat, n - 1)
                        a.wait_ge(q_var, n - 1)
                    src = k.bank(n % 2, (0, P), GROUP)
                    a.activation(k.qtmp[:, h, :], src, ACT.Identity, bias=k.bias_c[:, h:h + 1]
                                 ).then_inc(act_own, 1)
                    a.activation(k.qsq[:, h, :], src, ACT.Square, bias=k.bias_c[:, h:h + 1]
                                 ).then_inc(q_cen, 1)
                if n >= 1:
                    m = n - 1
                    a.wait_ge(q_var, m + 1)
                    a.activation(k.qlog[:, m % 2, :], k.bank(2 + m % 2, (0, P), GROUP), ACT.Ln,
                                 bias=k.eps_qk[:, 0:1]).then_inc(q_log, 1)
                    a.wait_ge(q_log, m + 1)
                    if m >= 2:
                        a.wait_ge(q_hat, m - 1)
                    a.activation(k.qrs[:, m % 2, :], k.qlog[:, m % 2, :], ACT.Exp, scale=-0.5
                                 ).then_inc(q_rstd, 1)


PREP0 = ["T", "K0", "K1", "V0", "V1"] + [f"M{m}" for m in range(8)] + ["R"]
SLOTS0 = {0: (["SD"], ["T"]), 1: (["PD"], ["K0"]), 2: (["OT"], ["K1"]), 3: (["C"], ["V0"]),
          4: (["Y"], ["V1"]), 5: (["ODT"], []), 6: ([], ["M0"]), 7: (["M1"], ["M2"]),
          8: (["M3"], ["M4"]), 9: (["M5"], ["M6"]), 10: (["M7"], ["R"]), 11: ([], [])}


def runs0(part, odd, unit):
    if unit in ("C", "Y") and odd:
        return False
    if part == "first" and not odd and unit in ("OT", "C", "Y"):
        return False
    return not (part == "last" and odd and unit in PREP0)


def order0(part):
    return [(odd, u) for odd in range(2) for j in range(CHUNKS) for side in SLOTS0[j] for u in side
            if runs0(part, odd, u)]


def pair_loop(eng, body):
    body("first", 0)
    with eng.Fori(1, PAIRS - 1) as pair:
        body("mid", pair)
    body("last", PAIRS - 1)


def layer0_attention(k):
    nc, i = k.nc, k.i
    turns = Turns(PREP0, order0("first"), order0("mid"), order0("last"), ["OT", "C", "Y"])
    (full, free, s_full, exp_done, pv_done, rstd, khat, keys_ready, keys_bf, q_ready, q_bf_ready,
     pv_rows, dup_rows, row_ready, o_read, rs_own, rsd_own, shift_done, y_own, resid_done,
     att_own, nc_log) = k.sems(
        "a0_shared_full", "a0_shared_free", "a0_scores_full", "a0_exp_done", "a0_pv_done", "a0_rstd",
        "a0_khat", "a0_keys_ready", "a0_keys_bf", "a0_q_ready", "a0_q_bf_ready", "a0_pv_rows",
        "a0_dup_rows", "a0_row_ready", "a0_o_read", "a0_rs_own", "a0_rsd_own", "a0_shift_done",
        "a0_y_own", "a0_resid_done", "a0_att_own", "a0_nc_log")
    loaded = k.sems("a0_loaded0", "a0_loaded1")
    LOADS = 4
    S, O, SHARED = 0, 2, 5

    def shared(count, rows, cols):
        return k.banks(SHARED, count, rows, cols)

    def chunk_cols(j):
        return j // 4, (j % 4) * CH0

    with nc.Block() as block:
        @block.sync
        def _(sp):
            def load(pair, odd, batch):
                par = odd
                for b in range(3):
                    sp.dma_start(
                        k.rows_raw[par][:, 4 * b:4 * b + 4, :],
                        i["ctx"][bass.ds(batch, 1), b * STEP0:b * STEP0 + SPAN0, :].rearrange(
                            "o (c p) d -> p (o c) d", p=CH0)).then_inc(loaded[par], 16)
                sp.dma_start(k.rows_d[par][:, 0:DC],
                             i["ctx"][bass.ds(batch, 1), MAIN:KEYS, :].rearrange("o p d -> p (o d)")
                             ).then_inc(loaded[par], 16)

            def body(part, pair):
                for odd in range(2):
                    batch = 2 * pair + odd
                    wait_alone(k, sp, pv_rows, batch + 1)
                    sp.wait_ge(full, turns.number(part, pair, (odd, "PD")) + 1)
                    if part != "last":
                        load(pair, odd, batch + 2)

            load(0, 0, 0)
            load(0, 1, 1)
            pair_loop(sp, body)

        @block.tensor
        def _(pe):
            def take(number, unit_full=None):
                at_least(pe, free, number)

            def unit(part, pair, odd, name, number, batch):
                take(number)
                nxt = 1 - odd
                if name == "T":
                    pe.wait_ge(loaded[nxt], 16 * LOADS * ((batch + 1 - nxt) // 2 + 1)
                               if isinstance(batch, int) else 16 * LOADS * (pair + odd + 1))
                    for j in range(CHUNKS):
                        b, c = chunk_cols(j)
                        pe.transpose(shared(3, (0, P), BANK)[:, b, c:c + CH0],
                                     k.rows_raw[nxt][:, j, :], k.ident[0:CH0, 0:CH0])
                    last = pe.transpose(shared(3, (0, P), BANK)[:, 2, SPAN0:BANK],
                                        k.rows_d[nxt][:, 0:DC], k.ident[0:DCA, 0:DCA])
                elif name in ("K0", "K1"):
                    h = int(name[1])
                    for b in range(3):
                        last = pe.matmul(shared(3, (0, P), SPAN0)[:, b, :], k.wk[:, h * P:(h + 1) * P],
                                         k.ctx_t[:, b, 0:SPAN0], start=True, stop=True)
                    last = pe.matmul(shared(3, (0, P), BANK)[:, 2, SPAN0:BANK],
                                     k.wkv_d[:, h * P:(h + 1) * P], k.ctx_t[:, 2, SPAN0:BANK],
                                     start=True, stop=True)
                elif name in ("V0", "V1"):
                    h = int(name[1])
                    for b in range(3):
                        last = pe.matmul(shared(3, (0, P), BANK)[:, b, :], k.same_head[:, :],
                                         k.ksq[:, h, b, :], start=True, stop=True)
                elif name[0] == "M":
                    m = int(name[1])
                    h, pr = divmod(m, 4)
                    pe.wait_ge(keys_bf, 2 * (batch + 1) + h + 1)
                    pe.wait_ge(q_bf_ready, batch + 2)
                    lhs = k.q_diag_bf[:, h, 2 * pr:2 * pr + 2, :]
                    for b in range(3):
                        n = BANK if b == 2 else SPAN0
                        last = pe.matmul(shared(3, (0, TT), BANK)[:, b, 0:n], lhs, k.keys_bf[:, h, b, 0:n],
                                         start=True, stop=True)
                elif name == "R":
                    for m in range(8):
                        last = pe.matmul(shared(2, (0, 2), HALF)[:, m // 4, (m % 4) * TT:(m % 4 + 1) * TT],
                                         k.shift_col[:, :, m], k.ident_bf[0:TT, 0:TT], start=True, stop=True)
                elif name == "SD":
                    pe.wait_ge(keys_ready, 2 * batch + 2)
                    pe.wait_ge(row_ready, batch + 1)
                    for h in range(2):
                        dst = shared(2, (0, DCA), HALF)[:, h, :]
                        pe.matmul(dst, k.keys[odd][:, h, 2, SPAN0:BANK], k.q_diag[odd][:, h, :, :],
                                  start=True, stop=False)
                        last = pe.matmul(dst, k.pick[:, 1, 0:DCA], k.shift_row[odd][:, h, :],
                                         start=False, stop=True)
                elif name == "PD":
                    pv(k.probs_d, k.rows_d[odd][:, :], DCA, shared(3, (0, P), BANK), True, True)
                    last = pv.last
                elif name in ("OT", "ODT"):
                    src = k.heads_n if name == "OT" else k.heads_dn
                    if name == "OT":
                        pe.wait_ge(o_read, batch)
                    for t in range(QT):
                        last = pe.transpose(k.bank(SHARED, (0, P), P, t * P), src[:, t, :], k.ident[:, :])
                elif name == "C":
                    for h in range(2):
                        dst = k.bank(SHARED, (0, P), TT, h * P)
                        n = 0
                        for s, src in ((0, k.heads_t), (1, k.heads_dt)):
                            for e in range(8):
                                last = pe.matmul(dst, k.wv_pad[:, s, h, e * P:(e + 1) * P],
                                                 src[:, 8 * h + e, :, :], start=(n == 0), stop=(n == 15))
                                n += 1
                else:
                    for h in range(2):
                        last = pe.matmul(k.bank(SHARED, (0, TT), D), k.att_t[:, h, :], k.wo0[:, h, :],
                                         start=(h == 0), stop=(h == 1))
                last.then_inc(full, 1)

            def pv(probs, rows, n, dst, start, stop):
                flat = probs[0:n, :, :].rearrange("p h c -> p (h c)")
                for t in range(QT):
                    pv.last = pe.matmul(dst[:, t // 3, (t % 3) * (DC + 1):(t % 3 + 1) * (DC + 1)],
                                        flat[:, t * P:(t + 1) * P], rows,
                                        start=start and t % 3 == 0, stop=stop, skip_group_check=True)

            def scores(batch, odd, j):
                n = CHUNKS * batch + j
                if j == 0:
                    pe.wait_ge(keys_ready, 2 * batch + 2)
                    pe.wait_ge(q_ready, batch + 1)
                    pe.wait_ge(row_ready, batch + 1)
                at_least(pe, exp_done, n)
                b, c = chunk_cols(j)
                for h in range(2):
                    dst = k.banks(S, 2, (0, CH0), HALF)[:, h, :]
                    pe.matmul(dst, k.keys[odd][:, h, b, c:c + CH0], k.q_diag[odd][:, h, :, :],
                              start=True, stop=False)
                    last = pe.matmul(dst, k.pick[:, 0, 0:CH0], k.shift_row[odd][:, h, :],
                                     start=False, stop=True)
                last.then_inc(s_full, 1)

            def values(batch, odd, j):
                pe.wait_ge(exp_done, CHUNKS * batch + j + 1)
                if j == 0:
                    pe.wait_ge(dup_rows, batch + 1)
                    at_least(pe, o_read, batch)
                pv(k.probs[j % 2], k.rows_pv[odd][:, j, :], CH0, k.banks(O, 3, (0, P), BANK),
                   j == 0, j == CHUNKS - 1)
                pv.last.then_inc(pv_done, 1)

            def body(part, pair):
                for odd in range(2):
                    batch = 2 * pair + odd
                    for j in range(CHUNKS):
                        scores(batch, odd, j)
                        before, after = SLOTS0[j]
                        for name in before:
                            if runs0(part, odd, name):
                                unit(part, pair, odd, name, turns.number(part, pair, (odd, name)), batch)
                        if j > 0:
                            values(batch, odd, j - 1)
                        elif not (part == "first" and odd == 0):
                            values(batch - 1, 1 - odd, CHUNKS - 1)
                        for name in after:
                            if runs0(part, odd, name):
                                unit(part, pair, odd, name, turns.number(part, pair, (odd, name)), batch)

            for name in PREP0:
                unit("pro", 0, 1, name, turns.number("pro", 0, name), -1)
            pair_loop(pe, body)
            values(BATCH - 1, 1, CHUNKS - 1)
            for name in ("OT", "C", "Y"):
                unit("epi", PAIRS, 0, name, turns.number("epi", 0, name), BATCH)

        @block.scalar
        def _(a):
            def unit(part, pair, odd, name, number, batch):
                a.wait_ge(full, number + 1)
                if name == "T":
                    last = a.activation(k.ctx_t[:, :, 0:SPAN0], shared(3, (0, P), SPAN0), ACT.Identity)
                    last = a.activation(k.ctx_t[:, 2, SPAN0:BANK], shared(3, (0, P), BANK)[:, 2, SPAN0:BANK],
                                        ACT.Identity)
                elif name in ("K0", "K1"):
                    h = int(name[1])
                    for dst, f in ((k.kc, ACT.Identity), (k.ksq, ACT.Square)):
                        a.activation(dst[:, h, :, 0:SPAN0], shared(3, (0, P), SPAN0), f,
                                     bias=k.bias_c[:, 2 + h:3 + h])
                        last = a.activation(dst[:, h, 2, SPAN0:BANK],
                                            shared(3, (0, P), BANK)[:, 2, SPAN0:BANK], f,
                                            bias=k.bias_c[:, 4 + h:5 + h])
                elif name in ("V0", "V1"):
                    h = int(name[1])
                    at_least(a, rstd, 2 * (batch + 1) + h)
                    a.activation(k.klog[:, :, :], shared(3, (0, P), BANK), ACT.Ln,
                                 bias=k.eps_qk[:, 0:1]).then_inc(free, 1)
                    a.wait_ge(free, number + 1)
                    at_least(a, khat, 2 * (batch + 1) + h)
                    a.activation(k.krs[:, :, :], k.klog[:, :, :], ACT.Exp, scale=-0.5).then_inc(rstd, 1)
                    return
                elif name == "SD":
                    last = a.activation(k.probs_d[:, :, :], shared(2, (0, DCA), HALF), ACT.Exp, scale=SCALE0)
                elif name in ("OT", "ODT"):
                    dst = k.heads_t if name == "OT" else k.heads_dt
                    par = 1 - odd if name == "OT" else odd
                    last = a.activation(dst[:, :, par, :],
                                        k.bank(SHARED, (0, P), HQ).rearrange("p (h q) -> p h q", q=SEQ),
                                        ACT.Identity)
                elif name == "C":
                    for h in range(2):
                        last = a.activation(k.att_t[:, h, :], k.bank(SHARED, (0, P), TT, h * P),
                                            ACT.Identity, bias=k.bv_sum[:, h:h + 1])
                last.then_inc(free, 1)

            MINE = ("T", "K0", "K1", "V0", "V1", "SD", "OT", "ODT", "C")

            def body(part, pair):
                for odd in range(2):
                    batch = 2 * pair + odd
                    for j in range(CHUNKS):
                        n = CHUNKS * batch + j
                        a.wait_ge(s_full, n + 1)
                        if not (part == "first" and odd == 0 and j < 2):
                            a.wait_ge(pv_done, n - 1)
                        a.activation(k.probs[j % 2][0:CH0, :, :], k.banks(S, 2, (0, CH0), HALF), ACT.Exp,
                                     scale=SCALE0).then_inc(exp_done, 1)
                        for side in SLOTS0[j]:
                            for name in side:
                                if name in MINE and runs0(part, odd, name):
                                    unit(part, pair, odd, name, turns.number(part, pair, (odd, name)), batch)

            a.preload_act_table_set("natural_log_exp_and_others")
            for name in PREP0:
                if name in MINE:
                    unit("pro", 0, 1, name, turns.number("pro", 0, name), -1)
            pair_loop(a, body)
            for name in ("OT", "C"):
                unit("epi", PAIRS, 0, name, turns.number("epi", 0, name), BATCH)

        @block.vector
        def _(v):
            def normalise(dst, src, sums, own, count):
                tiles = src[:, :, 0:3 * (DC + 1)].rearrange("p b (t c) -> p b t c", c=DC + 1)
                v.reciprocal(sums[:, 0:6].rearrange("p (b t) -> p b t", t=3), tiles[:, 0:2, :, DC]
                             ).then_inc(own, 1)
                v.reciprocal(sums[:, 6:7], tiles[:, 2, 0, DC:DC + 1]).then_inc(own, 1)
                v.wait_ge(own, 2 * count + 2)
                for b in range(3):
                    m = 3 if b < 2 else 1
                    last = v.tensor_tensor(
                        dst[:, 3 * b:3 * b + m, :], tiles[:, b, 0:m, 0:DC],
                        sums[:, 3 * b:3 * b + m].unsqueeze(2).to_broadcast([P, m, DC]), ALU.mult)
                return last

            def read_sums(batch):
                v.wait_ge(pv_done, CHUNKS * batch + CHUNKS)
                normalise(k.heads_n, k.banks(O, 3, (0, P), BANK), k.rsum, rs_own, batch).then_inc(o_read, 1)

            def finish_keys(nb, nxt, h):
                v.wait_ge(rstd, 2 * nb + h + 1)
                v.tensor_tensor(k.kc[:, h, :, :], k.kc[:, h, :, :], k.krs[:, :, :], ALU.mult
                                ).then_inc(khat, 1)
                v.wait_ge(khat, 2 * nb + h + 1)
                v.tensor_scalar(k.keys[nxt][:, h, :, 0:SPAN0], k.kc[:, h, :, 0:SPAN0],
                                k.lnwb[:, 2:3], k.lnwb[:, 3:4], ALU.mult, ALU.add)
                v.tensor_scalar(k.keys[nxt][:, h, 2, SPAN0:BANK], k.kc[:, h, 2, SPAN0:BANK],
                                k.lnwb[:, 4:5], k.lnwb[:, 5:6], ALU.mult, ALU.add).then_inc(keys_ready, 1)

            def unit(part, pair, odd, name, number, batch):
                v.wait_ge(full, number + 1)
                if name == "PD":
                    last = normalise(k.heads_dn, shared(3, (0, P), BANK), k.rsum_d, rsd_own, batch)
                elif name[0] == "M":
                    m = int(name[1])
                    v.tensor_reduce(k.shift_col[:, 0, m:m + 1], shared(3, (0, TT), SPAN0), AX.XY, ALU.max,
                                    negate=True)
                    last = v.tensor_reduce(k.shift_col[:, 1, m:m + 1],
                                           shared(3, (0, TT), BANK)[:, 2, SPAN0:BANK], AX.X, ALU.max,
                                           negate=True)
                elif name == "R":
                    last = v.tensor_copy(k.shift_row[1 - odd][:, :, :], shared(2, (0, 2), HALF))
                    last.then_inc(free, 1)
                    v.wait_ge(free, number + 1).then_inc(row_ready, 1)
                    return
                elif name == "Y":
                    prev = pair - 1
                    v.tensor_tensor(k.ytmp[:, :], k.bank(SHARED, (0, TT), D), k.bo_b[:, :], ALU.add
                                    ).then_inc(free, 1)
                    v.wait_ge(free, number + 1)
                    row = k.resid[:, bass.ds(prev, 1), :].rearrange("p o d -> p (o d)")
                    v.scalar_tensor_tensor(out=row, in0=k.ytmp[:, :], scalar=k.gates[0:TT, 0:1],
                                           in1=row, op0=ALU.mult, op1=ALU.add).then_inc(resid_done, 1)
                    return
                last.then_inc(free, 1)

            def body(part, pair):
                for odd in range(2):
                    batch = 2 * pair + odd
                    if not (part == "first" and odd == 0):
                        read_sums(batch - 1)
                    for j in range(CHUNKS):
                        for side in SLOTS0[j]:
                            for name in side:
                                if name in ("PD", "Y", "R") or name[0] == "M":
                                    if runs0(part, odd, name):
                                        unit(part, pair, odd, name, turns.number(part, pair, (odd, name)),
                                             batch)
                        if j == 5 and not (part == "last" and odd):
                            for h in range(2):
                                finish_keys(batch + 1, 1 - odd, h)

            for h in range(2):
                finish_keys(0, 0, h)
            for name in PREP0:
                if name[0] in "MR":
                    unit("pro", 0, 1, name, turns.number("pro", 0, name), -1)
            pair_loop(v, body)
            read_sums(BATCH - 1)
            unit("epi", PAIRS, 0, "Y", turns.number("epi", 0, "Y"), BATCH)
            v.wait_ge(resid_done, PAIRS)

        @block.gpsimd
        def _(g):
            def prepare(nb, nxt, count, scores_done):
                if not (isinstance(nb, int) and nb == 0):
                    g.wait_ge(s_full, scores_done + 1)
                q = k.q_all[:, :, bass.ds(nb * SEQ, SEQ)].unsqueeze(2).to_broadcast([P, 2, 8, SEQ])
                mask = k.head_mask[:, :].unsqueeze(1).unsqueeze(3).to_broadcast([P, 2, 8, SEQ])
                g.tensor_tensor(k.q_diag_bf[:, :, :, :], q, mask, ALU.mult).then_inc(q_bf_ready, 1)
                g.tensor_tensor(k.q_diag[nxt][:, :, :, :], q, mask, ALU.mult).then_inc(q_ready, 1)
                at_least(g, pv_done, scores_done)
                wait_alone(k, g, loaded[nxt], 16 * LOADS * count)
                g.tensor_copy(k.rows_pv[nxt][:, :, 0:DC], k.rows_raw[nxt][:, :, :]).then_inc(pv_rows, 1)
                wait_alone(k, g, pv_rows, nb + 1)
                g.memset(k.rows_pv[nxt][0:DUP0, 4:12:4, :], 0.0).then_inc(dup_rows, 1)
                for h in range(2):
                    wait_alone(k, g, keys_ready, 2 * nb + h + 1)
                    g.tensor_copy(k.keys_bf[:, h, :, 0:SPAN0], k.keys[nxt][:, h, :, 0:SPAN0])
                    g.tensor_copy(k.keys_bf[:, h, 2, SPAN0:BANK], k.keys[nxt][:, h, 2, SPAN0:BANK]
                                  ).then_inc(keys_bf, 1)

            def body(part, pair):
                for odd in range(2):
                    batch = 2 * pair + odd
                    if not (part == "last" and odd):
                        prepare(batch + 1, 1 - odd, pair + odd + 1, CHUNKS * batch)

            prepare(0, 0, 1, 0)
            pair_loop(g, body)



INNER = 704
IC = 6
ITAIL = INNER - 5 * P
IPAD = IC * P
IHALF = INNER // 2
FP8_MAX = 448.0
EXP_BITS = 0x7F800000
FP8_LEAST = 2.0 ** -6
FP8_MAGIC = 1.5 * 2.0 ** 20


def ffn_memory(k, s):
    sb = lambda name, shape, dt=F32: k.sbuf(s, name, shape, dt)
    k.up_row_i = sb("up_row_i", [1, D], I32)
    k.down_row_i = sb("down_row_i", [1, INNER], I32)
    k.up_row = sb("up_row", [1, D])
    k.down_row = sb("down_row", [1, INNER])
    k.down_col = sb("down_col", [P, IC], I32)
    k.ones = sb("ones", [P, P])
    k.feature_i = sb("feature_i", [P, IC], I32)
    k.feature = sb("feature", [P, IC])
    k.up_count = sb("up_count", [P, DK])
    k.down_count = sb("down_count", [P, IC])
    k.diag = sb("diag", [P, 2, P])
    k.count_b = sb("count_b", [P, D])
    k.up_mask = sb("up_mask", [P, D])
    k.down_mask = sb("down_mask", [P, IPAD])
    k.amax_w = sb("amax_w", [P, 2 * IC + DK])
    k.inv_w = sb("inv_w", [P, 2 * IC + DK])
    k.gate_scale = sb("gate_scale", [TT, IPAD])
    k.up_scale = sb("up_scale", [TT, IPAD])
    k.down_scale = sb("down_scale", [TT, D])
    k.qg_t = sb("qg_t", [P, DK, INNER], BF16)
    k.qu_t = sb("qu_t", [P, DK, INNER], BF16)
    k.qd_t = sb("qd_t", [P, IC, D], BF16)
    k.amax_x = sb("amax_x", [TT, NT])
    k.inv_x = sb("inv_x", [TT, NT])
    k.scale_x = sb("scale_x", [TT, NT])
    k.amax_t = sb("amax_t", [TT, NT])
    k.inv_t = sb("inv_t", [TT, NT])
    k.scale_t = sb("scale_t", [TT, NT])
    k.qx_t = sb("qx_t", [P, DK, TOK], BF16)
    with ExitStack() as prep:
        k.wg = sb2(k, prep, "wg", [P, IC, D])
        k.wu = sb2(k, prep, "wu", [P, IC, D])
        k.wd = sb2(k, prep, "wd", [P, DK, INNER])
        k.wtmp = sb2(k, prep, "wtmp", [P, IC * D])
        k.equal = sb2(k, prep, "equal", [P, INNER])
        k.idx_b = sb2(k, prep, "idx_b", [P, INNER])
        k.qg = sb2(k, prep, "qg", [P, IC, D], BF16)
        k.qu = sb2(k, prep, "qu", [P, IC, D], BF16)
        k.qd = sb2(k, prep, "qd", [P, DK, IPAD], BF16)
        k.xs = sb2(k, prep, "xs", [TT, NT, D])
        k.xm = sb2(k, prep, "xm", [TT, NT, D])
        k.qx = sb2(k, prep, "qx", [TT, NT, D], BF16)
    k.gate = sb("gate", [TT, NT, INNER])
    k.hidden = sb("hidden", [TT, NT, INNER])
    k.q_hidden = sb("q_hidden", [TT, 2, IPAD], BF16)
    k.qh_t = sb("qh_t", [P, 2, IC, TT], BF16)
    k.down_tmp = sb("down_tmp", [TT, 2, D])


def sb2(k, s, name, shape, dt=F32):
    return k.sbuf(s, name, shape, dt)


def round_fp8(v, chain, value, magic, out):
    chain.mark(v.tensor_scalar(magic.bitcast(U32), value.bitcast(U32), EXP_BITS, None, ALU.bitwise_and))
    chain.settle()
    chain.mark(v.tensor_scalar(magic, magic, FP8_LEAST, FP8_MAGIC, ALU.max, ALU.mult))
    chain.settle()
    chain.mark(v.tensor_tensor(value, value, magic, ALU.add))
    chain.settle()
    return v.tensor_tensor(out, value, magic, ALU.subtract)


def ffn_prepare(k):
    nc, i = k.nc, k.i
    norm = k.norm.start()
    (ld, gathered, consts, own_p, casts, vec, counted, spread, wq_done, turned, turned_read, tok_read,
     x_done, scales, ld_w) = k.sems(*("f0_" + n for n in (
         "ld", "gathered", "consts", "own_p", "casts", "vec", "counted", "spread", "wq_done",
         "turned", "turned_read", "tok_read", "x_done", "scales", "ld_w")))

    def chunk(c):
        return P if c < IC - 1 else ITAIL

    with nc.Block() as block:
        @block.sync
        def _(sp):
            one = lambda v: v.rearrange("(o d) -> o d", o=1)
            up, down = i["L0_ffn_up_reorder_index"], i["L0_ffn_down_reorder_index"]
            sp.dma_start(k.down_col[:, 0:IC - 1], down[0:5 * P].rearrange("(c p) -> p c", p=P),
                         allow_slow_non_contiguous=True).then_inc(ld, 16)
            sp.dma_start(k.down_col[0:ITAIL, IC - 1:IC], down[5 * P:INNER].rearrange("(p o) -> p o", o=1)
                         ).then_inc(ld, 16)
            sp.dma_start(k.up_row_i[:, :], one(up)).then_inc(ld, 16)
            sp.dma_start(k.down_row_i[:, :], one(down)).then_inc(ld, 16)
            sp.dma_start(k.wd[:, :, :], i["L0_ffn_w_down"].rearrange("(c p) n -> p c n", p=P)
                         ).then_inc(ld_w, 16)

        @block.gpsimd
        def _(g):
            g.memset(k.ones[:, :], 1.0).then_inc(consts, 1)
            g.iota(k.feature_i[:, :], [[P, IC]], base=0, channel_multiplier=1).then_inc(consts, 1)
            for w in (k.wg, k.wu):
                g.memset(w[:, IC - 1, :], 1.0).then_inc(own_p, 1)
            g.memset(k.qd[:, :, INNER:IPAD], 0.0).then_inc(consts, 1)
            g.wait_ge(ld, 64)
            g.wait_ge(own_p, 2)
            for w, name in ((k.wg, "L0_ffn_w_gate"), (k.wu, "L0_ffn_w_up")):
                for c in range(IC):
                    n = chunk(c)
                    g.indirect_dma_start(w[0:n, c, :], None, i[name], bass.IndirectOffsetOnAxis(
                        ap=k.down_col[0:n, c:c + 1], axis=0)).then_inc(gathered, 16)
            g.wait_ge(gathered, 16 * 2 * IC)

        @block.tensor
        def _(pe):
            pe.wait_ge(casts, 3)
            pe.matmul(k.bank(0, (0, P), D), k.ones_row[:, :], k.up_row[:, :], start=True, stop=True)
            for h in range(2):
                last = pe.matmul(k.bank(1 + h, (0, P), IHALF), k.ones_row[:, :],
                                 k.down_row[:, h * IHALF:(h + 1) * IHALF], start=True, stop=True)
            last.then_inc(spread, 1)
            pe.wait_ge(consts, 3)
            n = 0
            for _name, count, _dst in spreads(k):
                for c in range(count):
                    pe.wait_ge(scales, n + 1)
                    pe.matmul(spread_bank(k, _name, c), k.ones[:, :], k.diag[:, n % 2, :],
                              start=True, stop=True).then_inc(counted, 1)
                    n += 1
            norm.tensor(pe)
            n = 0
            for src, outer, inner in ((k.qg, IC, DK), (k.qu, IC, DK), (k.qd, DK, IC)):
                pe.wait_ge(wq_done, (k.qg, k.qu, k.qd).index(src) + 1)
                for c in range(inner):
                    if n >= 2:
                        pe.wait_ge(turned_read, n - 1)
                    for o in range(outer):
                        rows = chunk(o) if outer == IC else P
                        last = pe.transpose(turn_bank(k, n)[:, o * P:o * P + rows],
                                            src[0:rows, o, c * P:(c + 1) * P], k.ident_bf[0:rows, 0:rows])
                    last.then_inc(turned, 1)
                    n += 1
            for q in range(NT // 4):
                pe.wait_ge(x_done, q + 1)
                for c in range(DK):
                    pe.wait_ge(turned_read, 2 * DK + IC)
                    at_least(pe, tok_read, n - (2 * DK + IC) - 1)
                    for t in range(4):
                        last = pe.transpose(turn_bank(k, n)[:, t * TT:(t + 1) * TT],
                                            k.qx[:, 4 * q + t, c * P:(c + 1) * P], k.ident_bf[0:TT, 0:TT])
                    last.then_inc(turned, 1)
                    n += 1

        @block.scalar
        def _(a):
            norm.scalar(a)
            norm.copy_scalar(a)
            n = 2 * DK + IC
            for q in range(NT // 4):
                for c in range(DK):
                    a.wait_ge(turned, n + 1)
                    a.activation(k.qx_t[:, c, q * 4 * TT:(q + 1) * 4 * TT], turn_bank(k, n)[:, 0:4 * TT],
                                 ACT.Identity).then_inc(tok_read, 1)
                    n += 1

        @block.vector
        def _(v):
            chain = Chain(v, vec)
            v.wait_ge(ld, 64)
            v.wait_ge(consts, 3)
            v.tensor_copy(k.up_row[:, :], k.up_row_i[:, :]).then_inc(casts, 1)
            v.tensor_copy(k.down_row[:, :], k.down_row_i[:, :]).then_inc(casts, 1)
            v.tensor_copy(k.feature[:, :], k.feature_i[:, :]).then_inc(casts, 1)
            v.wait_ge(casts, 3)
            v.wait_ge(spread, 1)
            for size, pieces, count in ((D, DK, k.up_count), (INNER, IC, k.down_count)):
                if size == D:
                    src = k.bank(0, (0, P), D)
                    chain.mark(v.tensor_copy(k.idx_b[:, 0:D], src))
                else:
                    for h in range(2):
                        chain.mark(v.tensor_copy(k.idx_b[:, h * IHALF:(h + 1) * IHALF],
                                                 k.bank(1 + h, (0, P), IHALF)))
                chain.settle()
                for c in range(pieces):
                    chain.mark(v.tensor_scalar(k.equal[:, 0:size], k.idx_b[:, 0:size],
                                               k.feature[:, c:c + 1], None, ALU.is_equal))
                    chain.settle()
                    chain.mark(v.tensor_reduce(count[:, c:c + 1], k.equal[:, 0:size], AX.X, ALU.add))
                    chain.settle()
            n = 0

            def spread_column(name, column, pieces, dst, rows):
                nonlocal n
                for c in range(pieces):
                    if n >= 2:
                        v.wait_ge(counted, n - 1)
                    v.tensor_scalar(k.diag[:, n % 2, :], k.ident[:, :], column[:, c:c + 1], None,
                                    ALU.mult).then_inc(scales, 1)
                    n += 1
                v.wait_ge(counted, n)
                chain.mark(v.tensor_copy(dst[:, 0:pieces * P],
                                         spread_bank(k, name, 0, pieces * P)[0:rows, :]))
                chain.settle()

            spread_column("up_count", k.up_count, DK, k.up_mask, P)
            chain.mark(v.tensor_scalar(k.up_mask[:, :], k.up_mask[:, :], 1.0, None, ALU.min))
            chain.settle()
            spread_column("down_count", k.down_count, IC, k.down_mask, P)
            chain.mark(v.tensor_scalar(k.down_mask[:, :], k.down_mask[:, :], 1.0, None, ALU.min))
            chain.settle()
            v.wait_ge(gathered, 16 * 2 * IC)
            v.wait_ge(ld_w, 16)
            for m, (w, q, mask, pieces, size, at) in enumerate((
                    (k.wg, k.qg, k.up_mask, IC, D, 0), (k.wu, k.qu, k.up_mask, IC, D, IC),
                    (k.wd, k.qd, k.down_mask, DK, INNER, 2 * IC))):
                tmp = k.wtmp[:, 0:pieces * size].rearrange("p (c n) -> p c n", n=size)
                mb = mask[:, 0:size].unsqueeze(1).to_broadcast([P, pieces, size])
                at_least(v, wq_done, m)
                chain.mark(v.tensor_tensor(tmp, w[:, :, :], mb, ALU.mult))
                chain.settle()
                chain.mark(v.tensor_reduce(k.amax_w[:, at:at + pieces], tmp, AX.X, ALU.max,
                                           apply_absolute_value=True))
                chain.settle()
                chain.mark(v.reciprocal(k.inv_w[:, at:at + pieces], k.amax_w[:, at:at + pieces]))
                chain.mark(v.tensor_scalar(k.amax_w[:, at:at + pieces], k.amax_w[:, at:at + pieces],
                                           1.0 / FP8_MAX, None, ALU.mult))
                chain.settle()
                for c in range(pieces):
                    chain.mark(v.tensor_scalar(w[:, c, :], w[:, c, :], k.inv_w[:, at + c:at + c + 1],
                                               FP8_MAX, ALU.mult, ALU.mult))
                chain.settle()
                round_fp8(v, chain, w[:, :, :], tmp, q[:, :, 0:size]).then_inc(wq_done, 1)
            v.wait_ge(wq_done, 3)
            spread_column("gate_scale", k.amax_w[:, 0:IC], IC, k.gate_scale, TT)
            spread_column("up_scale", k.amax_w[:, IC:2 * IC], IC, k.up_scale, TT)
            chain.mark(v.tensor_tensor(k.up_scale[:, :], k.up_scale[:, :], k.down_mask[0:TT, :], ALU.mult))
            spread_column("down_scale", k.amax_w[:, 2 * IC:], DK, k.down_scale, TT)
            chain.mark(v.tensor_scalar(k.down_scale[:, :], k.down_scale[:, :], k.gates[0:TT, 2:3], None,
                                       ALU.mult))
            norm.vector(v, chain)
            norm.copy_vector(v)
            norm.wait_tiles(v, NT)
            m = 0
            for dst, counts, pieces, width in ((k.qg_t, k.up_count, DK, INNER), (k.qu_t, k.up_count, DK, INNER),
                                               (k.qd_t, k.down_count, IC, D)):
                for c in range(pieces):
                    v.wait_ge(turned, m + 1)
                    v.tensor_scalar(dst[:, c, :], turn_bank(k, m)[:, 0:width], counts[:, c:c + 1], None,
                                    ALU.mult).then_inc(turned_read, 1)
                    m += 1
            for q in range(NT // 4):
                ts = slice(4 * q, 4 * q + 4)
                mb = k.up_mask[0:TT, :].unsqueeze(1).to_broadcast([TT, 4, D])
                chain.mark(v.tensor_tensor(k.xm[:, ts, :], k.normed[:, ts, :], mb, ALU.mult))
                chain.settle()
                chain.mark(v.tensor_reduce(k.amax_x[:, ts], k.xm[:, ts, :], AX.X, ALU.max,
                                           apply_absolute_value=True))
                chain.settle()
                chain.mark(v.reciprocal(k.inv_x[:, ts], k.amax_x[:, ts]))
                chain.mark(v.tensor_scalar(k.scale_x[:, ts], k.amax_x[:, ts], 1.0 / FP8_MAX, None, ALU.mult))
                chain.settle()
                for t in range(4 * q, 4 * q + 4):
                    chain.mark(v.tensor_scalar(k.xs[:, t, :], k.normed[:, t, :], k.inv_x[:, t:t + 1], FP8_MAX,
                                               ALU.mult, ALU.mult))
                chain.settle()
                round_fp8(v, chain, k.xs[:, ts, :], k.xm[:, ts, :], k.qx[:, ts, :]).then_inc(x_done, 1)
            v.wait_ge(x_done, 4)


def spreads(k):
    return (("up_count", DK, None), ("down_count", IC, None), ("gate_scale", IC, None),
            ("up_scale", IC, None), ("down_scale", DK, None))


def spread_bank(k, name, c, cols=P):
    n = [s[0] for s in spreads(k)].index(name)
    return k.bank(3 + 2 * (n % 2), (0, P), cols, c * P)


def turn_bank(k, n):
    return k.bank(n % 2 + 6, (0, P), BANK).bitcast(BF16)


def ffn_run(k):
    nc = k.nc
    (g_full, u_full, g_read, u_read, silu_done, hid_done, amax_done, scaled, rounding, rounded, turned,
     turned_read, y_full, y_read, resid_done, vec, consts) = k.sems(*("f1_" + n for n in (
         "g_full", "u_full", "g_read", "u_read", "silu_done", "hid_done", "amax_done", "scaled", "rounding",
         "rounded", "turned", "turned_read", "y_full", "y_read", "resid_done", "vec", "consts")))
    HALVES = NT // 2

    def gu_banks(which):
        return k.banks(2 * which, 2, (0, TT), IHALF)

    def halves(ap):
        return ap.rearrange("p (h n) -> p h n", n=IHALF)

    def tile(ap, t):
        return ap[:, bass.ds(t, 1), :].rearrange("p o n -> p (o n)")

    def turned_bank(par):
        return k.bank(4 + par, (0, P), BANK).bitcast(BF16)

    with nc.Block() as block:
        @block.tensor
        def _(pe):
            with pe.Fori(0, NT) as t:
                for which, w, read, full in ((0, k.qg_t, g_read, g_full), (1, k.qu_t, u_read, u_full)):
                    pe.wait_ge(read, t + 1)
                    for h in range(2):
                        for c in range(DK):
                            last = pe.matmul(gu_banks(which)[:, h, :], k.qx_t[:, c, bass.ds(t * TT, TT)],
                                             w[:, c, h * IHALF:(h + 1) * IHALF],
                                             start=(c == 0), stop=(c == DK - 1))
                    last.then_inc(full, 1)
            with pe.Fori(0, HALVES) as u:
                for par in range(2):
                    t = 2 * u + par
                    pe.wait_ge(rounded, t + 1)
                    pe.wait_ge(turned_read, t + 1)
                    for c in range(IC):
                        last = pe.transpose(turned_bank(par)[:, c * TT:(c + 1) * TT],
                                            k.q_hidden[:, par, c * P:(c + 1) * P], k.ident_bf[0:TT, 0:TT])
                    last.then_inc(turned, 1)
                    pe.wait_ge(turned_read, t + 3)
                    pe.wait_ge(y_read, t + 1)
                    for c in range(IC):
                        last = pe.matmul(k.bank(6 + par, (0, TT), D), k.qh_t[:, par, c, :], k.qd_t[:, c, :],
                                         start=(c == 0), stop=(c == IC - 1))
                    last.then_inc(y_full, 1)

        @block.vector
        def _(v):
            v.engine_nop().then_inc(g_read, 1)
            v.engine_nop().then_inc(u_read, 1)
            for _n in range(2):
                v.engine_nop().then_inc(y_read, 1)
            with v.Fori(0, NT) as t:
                for which, src, dst, full, read in ((0, k.gate_scale, k.gate, g_full, g_read),
                                                    (1, k.up_scale, k.hidden, u_full, u_read)):
                    v.wait_ge(full, t + 1)
                    v.scalar_tensor_tensor(out=halves(tile(dst, t)), in0=gu_banks(which),
                                           scalar=k.scale_x[:, bass.ds(t, 1)], in1=halves(src[:, 0:INNER]),
                                           op0=ALU.mult, op1=ALU.mult).then_inc(read, 1)
            chain = Chain(v, vec)
            for q in range(NT // 4):
                ts = slice(4 * q, 4 * q + 4)
                v.wait_ge(hid_done, 4 * q + 4)
                chain.mark(v.tensor_reduce(k.amax_t[:, ts], k.hidden[:, ts, :], AX.X, ALU.max,
                                           apply_absolute_value=True))
                chain.settle()
                chain.mark(v.reciprocal(k.inv_t[:, ts], k.amax_t[:, ts]))
                chain.mark(v.tensor_scalar(k.scale_t[:, ts], k.amax_t[:, ts], 1.0 / FP8_MAX, None, ALU.mult))
                chain.settle()
                v.tensor_scalar(k.inv_t[:, ts], k.inv_t[:, ts], FP8_MAX, None, ALU.mult).then_inc(amax_done, 1)
                v.wait_ge(scaled, 4 * q + 4)
                value, magic = k.hidden[:, ts, :], k.gate[:, ts, :]
                chain.mark(v.tensor_scalar(magic.bitcast(U32), value.bitcast(U32), EXP_BITS, None,
                                           ALU.bitwise_and))
                chain.settle()
                chain.mark(v.tensor_scalar(magic, magic, FP8_LEAST, FP8_MAGIC, ALU.max, ALU.mult))
                chain.settle()
                v.tensor_tensor(value, value, magic, ALU.add).then_inc(rounding, 1)
            with v.Fori(0, HALVES) as u:
                for par in range(2):
                    t = 2 * u + par
                    v.wait_ge(y_full, t + 1)
                    v.scalar_tensor_tensor(out=k.down_tmp[:, par, :], in0=k.bank(6 + par, (0, TT), D),
                                           scalar=k.scale_t[:, bass.ds(t, 1)], in1=k.down_scale[:, :],
                                           op0=ALU.mult, op1=ALU.mult).then_inc(y_read, 1)
                    v.wait_ge(y_read, t + 3)
                    v.tensor_tensor(tile(k.resid, t), tile(k.resid, t), k.down_tmp[:, par, :], ALU.add
                                    ).then_inc(resid_done, 1)
            v.wait_ge(resid_done, NT)

        @block.scalar
        def _(a):
            for _n in range(2):
                a.nop().then_inc(turned_read, 1)
            with a.Fori(0, NT) as t:
                a.wait_ge(g_read, t + 2)
                a.activation(tile(k.gate, t), tile(k.gate, t), ACT.Silu).then_inc(silu_done, 1)
            for t in range(NT):
                if t % 4 == 0:
                    a.wait_ge(amax_done, t // 4 + 1)
                a.activation(k.hidden[:, t, :], k.hidden[:, t, :], ACT.Identity,
                             scale=k.inv_t[:, t:t + 1]).then_inc(scaled, 1)
            with a.Fori(0, HALVES) as u:
                for par in range(2):
                    t = 2 * u + par
                    a.wait_ge(turned, t + 1)
                    a.wait_ge(y_read, t + 1)
                    a.activation(k.qh_t[:, par, :, :].rearrange("p c n -> p (c n)"),
                                 turned_bank(par)[:, 0:IC * TT], ACT.Identity).then_inc(turned_read, 1)

        @block.gpsimd
        def _(g):
            g.memset(k.q_hidden[:, :, INNER:IPAD], 0.0).then_inc(consts, 1)
            with g.Fori(0, NT) as t:
                g.wait_ge(silu_done, t + 1)
                g.wait_ge(u_read, t + 2)
                g.tensor_tensor(tile(k.hidden, t), tile(k.gate, t), tile(k.hidden, t), ALU.mult
                                ).then_inc(hid_done, 1)
            g.wait_ge(consts, 1)
            with g.Fori(0, NT // 4) as q:
                g.wait_ge(rounding, q + 1)
                for n in range(4):
                    t = 4 * q + n
                    g.wait_ge(turned_read, t + 1)
                    g.tensor_tensor(k.q_hidden[:, n % 2, 0:INNER], tile(k.hidden, t), tile(k.gate, t),
                                    ALU.subtract).then_inc(rounded, 1)



HD1 = 128
KV = 8
CH1 = KEYS // CHUNKS
SPAN1 = 4 * CH1
SCALE1 = HD1 ** -0.5
MASKED = -1e30

PREP1 = ["T", "B"] + [f"M{m}" for m in range(QT)] + ["R"]
SLOTS1 = {0: ([], []), 1: (["OT"], ["B"]), 2: (["Y"], []), 3: ([], []), 4: (["T"], []),
          5: (["M0"], ["M1"]), 6: (["M2"], ["M3"]), 7: (["M4"], ["M5"]), 8: (["M6"], []),
          9: (["R"], []), 10: ([], []), 11: ([], [])}
PREP1_ORDER = ["B", "T"] + PREP1[2:]


def runs1(part, odd, unit):
    if unit == "Y" and odd:
        return False
    if part == "first" and not odd and unit in ("OT", "Y"):
        return False
    return not (part == "last" and odd and unit in PREP1)


def order1(part):
    return [(odd, u) for odd in range(2) for j in range(CHUNKS) for side in SLOTS1[j] for u in side
            if runs1(part, odd, u)]


def layer1_memory(k, s):
    sb = lambda name, shape, dt=F32: k.sbuf(s, name, shape, dt)
    k.qk_w = sb("qk_w", [P, DK, HEADS, DC])
    k.vo_w = sb("vo_w", [DC, HEADS, D])
    k.mask_col8 = sb("mask_col8", [CH1, BATCH, CHUNKS], U8)
    k.mask_row8 = sb("mask_row8", [BATCH, KEYS], U8)
    k.mask_row = sb("mask_row", [BATCH, KEYS])
    k.any_col = sb("any_col", [BATCH, 1])
    k.any_diag = sb("any_diag", [BATCH, BATCH])
    k.ones_bc = sb("ones_bc", [BATCH, P])
    k.any_key = sb("any_key", [P, BATCH])
    k.mask_bias = sb("mask_bias", [CH1, BATCH, CHUNKS])
    k.ones_bf = sb("ones_bf", [1, P], BF16)
    with ExitStack() as prep:
        k.wq1 = k.sbuf(prep, "wq1", [P, DK, HEADS * HD1])
        k.wk1 = k.sbuf(prep, "wk1", [DC, KV, HD1])
        k.wv1 = k.sbuf(prep, "wv1", [DC, KV, HD1])
        k.wo1 = k.sbuf(prep, "wo1", [HD1, HEADS, D])
        k.wk1_t = k.sbuf(prep, "wk1_t", [HD1, KV, DC])
        k.wv1_t = k.sbuf(prep, "wv1_t", [HD1, KV, DC])
        k.wq1_t = k.sbuf(prep, "wq1_t", [HD1, 2, D])
        k.q_stage = [k.sbuf(prep, f"q_stage{n}", [DC, 8, HEADS, SEQ]) for n in range(2)]
    k.rows1 = [sb(f"rows1_{n}", [CH1, CHUNKS, DC + 1]) for n in range(2)]
    k.ctx1_t = [sb(f"ctx1_t{n}", [DC, 3, SPAN1]) for n in range(2)]
    k.ctx1_bf = sb("ctx1_bf", [DC, 3, SPAN1], BF16)
    k.q1 = [sb(f"q1_{n}", [DC, HQ]) for n in range(2)]
    k.q1_bf = sb("q1_bf", [DC, HQ], BF16)
    k.bias_bc = sb("bias_bc", [CH1, CHUNKS, P], BF16)
    k.bias_row = sb("bias_row", [P, 3, SPAN1])
    k.masked = sb("masked", [P, 3, SPAN1], BF16)
    k.max_f = sb("max_f", [P, QT])
    k.max_col = sb("max_col", [P, QT], BF16)
    k.row1 = [sb(f"row1_{n}", [1, HQ], BF16) for n in range(2)]
    k.rsum1 = sb("rsum1", [P, QT])
    k.rinv1 = sb("rinv1", [P, QT])


def layer1_prepare(k):
    nc, i = k.nc, k.i
    norm = k.norm.start()
    k.q1_dram = nc.dram_tensor("q1_scratch", (P, BATCH, HQ), F32, kind="Internal").ap()
    (ld_w, ld_m, consts, own_p, kv_turned, kv_read, q_turned, q_read, w_full, w_read, mask_v, any_full,
     q_full, stage_a, stage_v, vec, own_a) = k.sems(*("p1_" + n for n in (
         "ld_w", "ld_m", "consts", "own_p", "kv_turned", "kv_read", "q_turned", "q_read", "w_full", "w_read",
         "mask_v", "any_full", "q_full", "stage_a", "stage_v", "vec", "own_a")))
    stored = k.sems("p1_stored0", "p1_stored1")
    GROUPS, GC = 4, 4 * TT

    with nc.Block() as block:
        @block.sync
        def _(sp):
            sp.dma_start(k.wk1[:, :, :], i["L1_xattn_Wk"].rearrange("p (g d) -> p g d", d=HD1)).then_inc(ld_w, 16)
            sp.dma_start(k.wv1[:, :, :], i["L1_xattn_Wv"].rearrange("p (g d) -> p g d", d=HD1)).then_inc(ld_w, 16)
            sp.dma_start(k.wq1[:, :, :], i["L1_xattn_Wq"].rearrange("(c p) n -> p c n", p=P)).then_inc(ld_w, 16)
            sp.dma_start(k.wo1[:, :, :], i["L1_xattn_Wo"].rearrange("(h p) n -> p h n", p=P)).then_inc(ld_w, 16)
            sp.dma_start(k.mask_row8[:, :], i["mask"]).then_inc(ld_m, 16)
            sp.dma_start(k.mask_col8[:, :, :], i["mask"].rearrange("b (p j) -> p b j", j=CHUNKS)
                         ).then_inc(ld_m, 16)
            for g in range(GROUPS):
                sp.wait_ge(stage_a, 8 * (g + 1))
                sp.wait_ge(stage_v, 8 * (g + 1))
                sp.dma_start(k.q1_dram[:, 8 * g:8 * g + 8, :],
                             k.q_stage[g % 2][:, :, :, :].rearrange("p b h q -> p b (h q)")).then_inc(stored[g % 2], 16)
            for n in range(2):
                sp.wait_ge(stored[n], 16 * (GROUPS // 2))

        @block.gpsimd
        def _(g):
            g.memset(k.ones_bc[:, :], 1.0).then_inc(consts, 1)
            g.memset(k.ones_bf[:, :], 1.0).then_inc(consts, 1)
            g.wait_ge(ld_m, 32)
            g.tensor_scalar(k.mask_bias[:, :, :], k.mask_col8[:, :, :], -MASKED, MASKED, ALU.mult, ALU.add
                            ).then_inc(own_p, 1)
            g.wait_ge(own_p, 1)
            g.wait_ge(mask_v, 2)
            g.tensor_tensor(k.mask_bias[:, :, :], k.mask_bias[:, :, :],
                            k.any_key[0:CH1, :].unsqueeze(2).to_broadcast([CH1, BATCH, CHUNKS]), ALU.mult
                            ).then_inc(own_p, 1)
            g.wait_ge(own_p, 2)

        @block.tensor
        def _(pe):
            pe.wait_ge(ld_w, 64)
            for g in range(KV):
                if g >= 2:
                    pe.wait_ge(kv_read, g - 1)
                pe.transpose(k.bank(g % 2, (0, P), P), k.wk1[:, g, :], k.ident[:, :])
                pe.transpose(k.bank(g % 2, (0, P), P, P), k.wv1[:, g, :], k.ident[:, :]).then_inc(kv_turned, 1)
            for h in range(HEADS + 1):
                if h < HEADS:
                    if h >= 2:
                        pe.wait_ge(q_read, h - 1)
                    for c in range(DK):
                        last = pe.transpose(k.bank(2 + h % 2, (0, P), P, c * P),
                                            k.wq1[:, c, h * P:(h + 1) * P], k.ident[:, :])
                    last.then_inc(q_turned, 1)
                if h >= 1:
                    m = h - 1
                    pe.wait_ge(q_read, m + 1)
                    pe.wait_ge(kv_read, m // 2 + 1)
                    if m >= 2:
                        pe.wait_ge(w_read, m - 1)
                    for c in range(DK):
                        pe.matmul(k.bank(4 + m % 2, (0, P), P, c * P), k.wq1_t[:, m % 2, c * P:(c + 1) * P],
                                  k.wk1_t[:, m // 2, :], start=True, stop=True)
                    pe.matmul(k.bank(4 + m % 2, (0, P), D, D), k.wv1_t[:, m // 2, :], k.wo1[:, m, :],
                              start=True, stop=True).then_inc(w_full, 1)
            pe.wait_ge(mask_v, 1)
            pe.wait_ge(consts, 2)
            pe.matmul(k.bank(6, (0, P), BATCH), k.ones_bc[:, :], k.any_diag[:, :], start=True, stop=True
                      ).then_inc(any_full, 1)
            norm.tensor(pe)
            norm.wait_all(pe)
            pe.wait_ge(w_read, HEADS)
            n = 0
            for g in range(GROUPS):
                for h in range(HEADS):
                    if n >= 4:
                        pe.wait_ge(stage_a, (n - 4) // 2 + 1)
                        pe.wait_ge(stage_v, (n - 4 + 1) // 2)
                    for c in range(DK):
                        last = pe.matmul(k.bank(4 + n % 4, (0, P), GC), k.qk_w[:, c, h, :],
                                         k.normed_t[:, c, g * GC:(g + 1) * GC], start=(c == 0), stop=(c == DK - 1))
                    last.then_inc(q_full, 1)
                    n += 1

        def stage(eng_copy, n):
            g, h = divmod(n, HEADS)
            return eng_copy(k.q_stage[g % 2][:, :, h, :],
                            k.bank(4 + n % 4, (0, P), GC).rearrange("p (b q) -> p b q", q=SEQ))

        @block.scalar
        def _(a):
            for m in range(HEADS):
                a.wait_ge(w_full, m + 1)
                a.activation(k.qk_w[:, :, m, :], k.bank(4 + m % 2, (0, P), D).rearrange("p (c n) -> p c n", n=P),
                             ACT.Identity).then_inc(own_a, 1)
                a.activation(k.vo_w[:, m, :], k.bank(4 + m % 2, (0, P), D, D), ACT.Identity).then_inc(w_read, 1)
            norm.scalar(a)
            norm.copy_scalar(a)
            for n in range(0, GROUPS * HEADS, 2):
                a.wait_ge(q_full, n + 1)
                if n % HEADS == 0 and n // HEADS >= 2:
                    a.wait_ge(stored[n // HEADS % 2], 16 * (n // HEADS // 2))
                stage(lambda o, s: a.activation(o, s, ACT.Identity), n).then_inc(stage_a, 1)

        @block.vector
        def _(v):
            chain = Chain(v, vec)
            for g in range(KV):
                v.wait_ge(kv_turned, g + 1)
                chain.mark(v.tensor_copy(k.wk1_t[:, g, :], k.bank(g % 2, (0, P), P)))
                v.tensor_copy(k.wv1_t[:, g, :], k.bank(g % 2, (0, P), P, P)).then_inc(kv_read, 1)
            for h in range(HEADS):
                v.wait_ge(q_turned, h + 1)
                if h >= 2:
                    v.wait_ge(w_full, h - 1)
                v.tensor_copy(k.wq1_t[:, h % 2, :], k.bank(2 + h % 2, (0, P), D)).then_inc(q_read, 1)
            v.wait_ge(ld_m, 32)
            chain.mark(v.tensor_copy(k.mask_row[:, :], k.mask_row8[:, :]))
            chain.settle()
            chain.mark(v.tensor_reduce(k.any_col[:, :], k.mask_row[:, :], AX.X, ALU.max))
            chain.settle()
            v.tensor_scalar(k.any_diag[:, :], k.ident[0:BATCH, 0:BATCH], k.any_col[:, 0:1], None, ALU.mult
                            ).then_inc(mask_v, 1)
            v.wait_ge(any_full, 1)
            v.tensor_copy(k.any_key[:, :], k.bank(6, (0, P), BATCH)).then_inc(mask_v, 1)
            norm.vector(v, chain)
            norm.copy_vector(v)
            for n in range(1, GROUPS * HEADS, 2):
                v.wait_ge(q_full, n + 1)
                if n % HEADS == 1 and n // HEADS >= 2:
                    v.wait_ge(stored[n // HEADS % 2], 16 * (n // HEADS // 2))
                stage(v.tensor_copy, n).then_inc(stage_v, 1)


def layer1_attention(k):
    nc, i = k.nc, k.i
    turns = Turns(PREP1_ORDER, order1("first"), order1("mid"), order1("last"), ["OT", "Y"])
    (full, free, row_ready, s_full, exp_done, pv_done, bc_ready, q_bf_ready, ctx_bf_ready, o_read, rs_own, max_own,
     resid_done, consts) = k.sems(*("a1_" + n for n in (
         "shared_full", "shared_free", "row_ready", "scores_full", "exp_done", "pv_done", "bc_ready", "q_bf_ready",
         "ctx_bf_ready", "o_read", "rs_own", "max_own", "resid_done", "consts")))
    loaded = k.sems("a1_loaded0", "a1_loaded1")
    q_loaded = k.sems("a1_q_loaded0", "a1_q_loaded1")
    S, O, SHARED = 0, 2, 5

    def shared(count, rows, cols):
        return k.banks(SHARED, count, rows, cols)

    def each_unit(part, odd, j, mine):
        return [name for side in SLOTS1[j] for name in side if name in mine and runs1(part, odd, name)]

    with nc.Block() as block:
        @block.sync
        def _(sp):
            def load(par, batch):
                sp.dma_start(k.rows1[par][:, :, 0:DC],
                             i["ctx"][bass.ds(batch, 1), :, :].rearrange("o (p j) d -> p (o j) d", j=CHUNKS)
                             ).then_inc(loaded[par], 16)

            def load_q(par, batch):
                sp.dma_start(k.q1[par][:, :], k.q1_dram[:, bass.ds(batch, 1), :].rearrange("p o n -> p (o n)")
                             ).then_inc(q_loaded[par], 16)

            def body(part, pair):
                for odd in range(2):
                    batch = 2 * pair + odd
                    if part == "last" and odd:
                        continue
                    at_least(sp, pv_done, CHUNKS * batch)
                    if not (part == "first" and odd == 0):
                        load(1 - odd, batch + 1)
                        load_q(1 - odd, batch + 1)

            load(0, 0)
            load_q(0, 0)
            load(1, 1)
            load_q(1, 1)
            pair_loop(sp, body)

        @block.tensor
        def _(pe):
            def unit(part, pair, odd, name, number, batch):
                at_least(pe, free, number)
                nxt = 1 - odd
                if name == "B":
                    pe.wait_ge(bc_ready, batch + 2)
                    for j in range(CHUNKS):
                        last = pe.matmul(shared(3, (0, P), SPAN1)[:, j // 4, (j % 4) * CH1:(j % 4 + 1) * CH1],
                                         k.bias_bc[:, j, :], k.ident_bf[0:CH1, 0:CH1], start=True, stop=True)
                elif name == "T":
                    pe.wait_ge(loaded[nxt], 16 * (pair + odd + 1))
                    for j in range(CHUNKS):
                        last = pe.transpose(shared(3, (0, P), SPAN1)[:, j // 4, (j % 4) * CH1:(j % 4 + 1) * CH1],
                                            k.rows1[nxt][:, j, 0:DC], k.ident[0:CH1, 0:CH1])
                elif name[0] == "M":
                    m = int(name[1])
                    pe.wait_ge(q_bf_ready, batch + 2)
                    pe.wait_ge(ctx_bf_ready, batch + 2)
                    for b in range(3):
                        last = pe.matmul(shared(3, (0, P), SPAN1)[:, b, :], k.q1_bf[:, m * P:(m + 1) * P],
                                         k.ctx1_bf[:, b, :], start=True, stop=True)
                elif name == "R":
                    pe.wait_ge(max_own, batch + 2)
                    for m in range(QT):
                        last = pe.matmul(k.bank(SHARED, (0, 1), P, m * P), k.max_col[:, m:m + 1],
                                         k.ident_bf[:, :], start=True, stop=True)
                elif name == "OT":
                    pe.wait_ge(o_read, batch)
                    for t in range(QT):
                        last = pe.transpose(k.bank(SHARED, (0, P), P, t * P), k.heads_n[:, t, :], k.ident[:, :])
                else:
                    for h in range(HEADS):
                        last = pe.matmul(k.bank(SHARED, (0, TT), D), k.heads_t[:, h, :, :], k.vo_w[:, h, :],
                                         start=(h == 0), stop=(h == HEADS - 1))
                last.then_inc(full, 1)

            def scores(pair, batch, odd, j):
                if j == 0:
                    pe.wait_ge(q_loaded[odd], 16 * (pair + 1))
                    pe.wait_ge(row_ready, batch + 1)
                at_least(pe, exp_done, CHUNKS * batch + j)
                ctx = k.ctx1_t[odd][:, :, :].rearrange("p b c -> p (b c)")[:, j * CH1:(j + 1) * CH1]
                for h in range(2):
                    dst = k.banks(S, 2, (0, CH1), HALF)[:, h, :]
                    pe.matmul(dst, ctx, k.q1[odd][:, h * HALF:(h + 1) * HALF], start=True, stop=False)
                    last = pe.matmul(dst, k.ones_bf[:, 0:CH1], k.row1[odd][:, h * HALF:(h + 1) * HALF],
                                     start=False, stop=True)
                last.then_inc(s_full, 1)

            def values(batch, odd, j):
                pe.wait_ge(exp_done, CHUNKS * batch + j + 1)
                if j == 0:
                    at_least(pe, o_read, batch)
                flat = k.probs[j % 2][0:CH1, :, :].rearrange("p h c -> p (h c)")
                dst = k.banks(O, 3, (0, P), BANK)
                for t in range(QT):
                    last = pe.matmul(dst[:, t // 3, (t % 3) * (DC + 1):(t % 3 + 1) * (DC + 1)],
                                     flat[:, t * P:(t + 1) * P], k.rows1[odd][:, j, :],
                                     start=(j == 0 and t % 3 == 0), stop=(j == CHUNKS - 1),
                                     skip_group_check=True)
                last.then_inc(pv_done, 1)

            def body(part, pair):
                for odd in range(2):
                    batch = 2 * pair + odd
                    for j in range(CHUNKS):
                        scores(pair, batch, odd, j)
                        before, after = SLOTS1[j]
                        for name in before:
                            if runs1(part, odd, name):
                                unit(part, pair, odd, name, turns.number(part, pair, (odd, name)), batch)
                        if j > 0:
                            values(batch, odd, j - 1)
                        elif not (part == "first" and odd == 0):
                            values(batch - 1, 1 - odd, CHUNKS - 1)
                        for name in after:
                            if runs1(part, odd, name):
                                unit(part, pair, odd, name, turns.number(part, pair, (odd, name)), batch)

            pe.wait_ge(consts, 2)
            for name in PREP1_ORDER:
                unit("pro", -1, 1, name, turns.number("pro", 0, name), -1)
            pair_loop(pe, body)
            values(BATCH - 1, 1, CHUNKS - 1)
            for name in ("OT", "Y"):
                unit("epi", PAIRS, 0, name, turns.number("epi", 0, name), BATCH)

        @block.scalar
        def _(a):
            def unit(part, pair, odd, name, number, batch):
                a.wait_ge(full, number + 1)
                if name == "T":
                    last = a.activation(k.ctx1_t[1 - odd][:, :, :], shared(3, (0, P), SPAN1), ACT.Identity)
                elif name == "B":
                    last = a.activation(k.bias_row[:, :, :], shared(3, (0, P), SPAN1), ACT.Identity)
                elif name == "OT":
                    last = a.activation(k.heads_t[:, :, 1 - odd, :],
                                        k.bank(SHARED, (0, P), HQ).rearrange("p (h q) -> p h q", q=SEQ),
                                        ACT.Identity)
                elif name == "R":
                    a.activation(k.row1[1 - odd][:, :], k.bank(SHARED, (0, 1), HQ), ACT.Identity, scale=-1.0
                                 ).then_inc(free, 1)
                    a.wait_ge(free, number + 1).then_inc(row_ready, 1)
                    return
                last.then_inc(free, 1)

            def body(part, pair):
                for odd in range(2):
                    batch = 2 * pair + odd
                    for j in range(CHUNKS):
                        n = CHUNKS * batch + j
                        a.wait_ge(s_full, n + 1)
                        if not (part == "first" and odd == 0 and j < 2):
                            a.wait_ge(pv_done, n - 1)
                        bias = k.mask_bias[:, bass.ds(batch, 1), j]
                        a.activation(k.probs[j % 2][0:CH1, :, :], k.banks(S, 2, (0, CH1), HALF), ACT.Exp,
                                     bias=bias, scale=SCALE1).then_inc(exp_done, 1)
                        for name in each_unit(part, odd, j, ("T", "B", "OT", "R")):
                            unit(part, pair, odd, name, turns.number(part, pair, (odd, name)), batch)

            for name in PREP1_ORDER:
                if name in ("T", "B", "R"):
                    unit("pro", -1, 1, name, turns.number("pro", 0, name), -1)
            pair_loop(a, body)
            unit("epi", PAIRS, 0, "OT", turns.number("epi", 0, "OT"), BATCH)

        @block.vector
        def _(v):
            def read_sums(batch):
                v.wait_ge(pv_done, CHUNKS * batch + CHUNKS)
                src = k.banks(O, 3, (0, P), BANK)
                tiles = src[:, :, 0:3 * (DC + 1)].rearrange("p b (t c) -> p b t c", c=DC + 1)
                v.tensor_scalar(k.rsum1[:, 0:6].rearrange("p (b t) -> p b t", t=3), tiles[:, 0:2, :, DC],
                                1e-30, None, ALU.max)
                v.tensor_scalar(k.rsum1[:, 6:7], tiles[:, 2, 0, DC:DC + 1], 1e-30, None, ALU.max
                                ).then_inc(rs_own, 1)
                v.wait_ge(rs_own, 3 * batch + 1)
                v.reciprocal(k.rinv1[:, :], k.rsum1[:, :]).then_inc(rs_own, 1)
                v.wait_ge(rs_own, 3 * batch + 2)
                v.tensor_scalar(k.rsum1[:, :], k.rinv1[:, :], k.any_key[:, bass.ds(batch, 1)], None, ALU.mult
                                ).then_inc(rs_own, 1)
                v.wait_ge(rs_own, 3 * batch + 3)
                for b in range(3):
                    m = 3 if b < 2 else 1
                    last = v.tensor_tensor(
                        k.heads_n[:, 3 * b:3 * b + m, :], tiles[:, b, 0:m, 0:DC],
                        k.rsum1[:, 3 * b:3 * b + m].unsqueeze(2).to_broadcast([P, m, DC]), ALU.mult)
                last.then_inc(o_read, 1)

            def unit(part, pair, odd, name, number, batch):
                wait_alone(k, v, full, number + 1)
                if name[0] == "M":
                    m = int(name[1])
                    if m == 0 and part != "pro":
                        wait_alone(k, v, max_own, batch + 1)
                    elif m > 0:
                        wait_alone(k, v, free, number)
                    v.tensor_tensor_reduce(k.masked[:, :, :], shared(3, (0, P), SPAN1), k.bias_row[:, :, :],
                                           1.0, -3e38, ALU.add, ALU.max, k.max_f[:, m:m + 1]).then_inc(free, 1)
                    if m == QT - 1:
                        v.wait_ge(free, number + 1)
                        v.tensor_copy(k.max_col[:, :], k.max_f[:, :]).then_inc(max_own, 1)
                else:
                    row = k.resid[:, bass.ds(pair - 1, 1), :].rearrange("p o d -> p (o d)")
                    v.scalar_tensor_tensor(out=row, in0=k.bank(SHARED, (0, TT), D), scalar=k.gates[0:TT, 1:2],
                                           in1=row, op0=ALU.mult, op1=ALU.add).then_inc(free, 1)

            def body(part, pair):
                for odd in range(2):
                    batch = 2 * pair + odd
                    if not (part == "first" and odd == 0):
                        read_sums(batch - 1)
                    for j in range(CHUNKS):
                        for name in each_unit(part, odd, j, ["Y"] + [f"M{m}" for m in range(QT)]):
                            unit(part, pair, odd, name, turns.number(part, pair, (odd, name)), batch)

            for m in range(QT):
                unit("pro", -1, 1, f"M{m}", turns.number("pro", 0, f"M{m}"), -1)
            pair_loop(v, body)
            read_sums(BATCH - 1)
            unit("epi", PAIRS, 0, "Y", turns.number("epi", 0, "Y"), BATCH)
            v.wait_ge(free, turns.number("epi", 0, "Y") + 1)

        @block.gpsimd
        def _(g):
            for n in range(2):
                g.memset(k.rows1[n][:, :, DC:DC + 1], 1.0).then_inc(consts, 1)

            def prepare(nb, nxt, count, turned):
                if not (isinstance(nb, int) and nb == 0):
                    wait_alone(k, g, s_full, CHUNKS * (nb - 1) + 1)
                g.tensor_copy(k.bias_bc[:, :, :],
                              k.mask_bias[:, bass.ds(nb, 1), :].rearrange("p o j -> p (o j)").unsqueeze(2)
                              .to_broadcast([CH1, CHUNKS, P])).then_inc(bc_ready, 1)
                wait_alone(k, g, q_loaded[nxt], 16 * count)
                g.tensor_copy(k.q1_bf[:, :], k.q1[nxt][:, :]).then_inc(q_bf_ready, 1)
                wait_alone(k, g, free, turned + 1)
                g.tensor_copy(k.ctx1_bf[:, :, :], k.ctx1_t[nxt][:, :, :]).then_inc(ctx_bf_ready, 1)

            def body(part, pair):
                for odd in range(2):
                    if not (part == "last" and odd):
                        prepare(2 * pair + odd + 1, 1 - odd, pair + odd + 1,
                                turns.number(part, pair, (odd, "T")))

            prepare(0, 0, 1, turns.number("pro", 0, "T"))
            pair_loop(g, body)



EXPERTS = 8
FF = 1024
CAP = TOK // EXPERTS
FC = FF // P
SLOTS = EXPERTS * CAP
assert CAP == 2 * TT


def moe_memory(k, s):
    sb = lambda name, shape, dt=F32: k.sbuf(s, name, shape, dt)
    k.w1 = [sb(f"w1_{n}", [P, DK, FF]) for n in range(2)]
    k.w2 = [sb(f"w2_{n}", [P, FC, D]) for n in range(2)]
    k.ff = [sb(f"ff{n}", [P, FC, CAP]) for n in range(2)]
    k.back = sb("back", [TT, NT, D])
    k.w_router = sb("w_router", [P, DK, EXPERTS])
    k.zeros = sb("zeros", [P, D])
    k.earlier = sb("earlier", [TT, TT], BF16)
    k.ones_tt = sb("ones_tt", [TT, TT], BF16)
    k.expert_i = sb("expert_i", [TT, EXPERTS], I32)
    k.token_i = sb("token_i", [TT, NT], I32)
    k.rank = sb("rank", [TT, EXPERTS])
    k.first_slot = sb("first_slot", [TT, EXPERTS])
    k.spill = sb("spill", [TT, NT])
    k.logits, k.e_gates, k.e_eq, k.e_tmp, k.e_tmp2 = (sb(name, [TT, NT, EXPERTS]) for name in (
        "logits", "e_gates", "e_eq", "e_tmp", "e_tmp2"))
    k.chosen = sb("chosen", [TT, NT, EXPERTS], BF16)
    (k.m_max, k.m_top, k.m_sum, k.m_inv, k.m_rank, k.m_loc, k.m_kept, k.m_slot, k.m_w, k.m_diff,
     k.m_put) = (sb(name, [TT, NT]) for name in (
         "m_max", "m_top", "m_sum", "m_inv", "m_rank", "m_loc", "m_kept", "m_slot", "m_w", "m_diff", "m_put"))
    k.put_i = sb("put_i", [TT, NT], I32)
    k.get_i = sb("get_i", [TT, NT], I32)


def load_expert(k, eng, par, e, loaded1, loaded2):
    eng.dma_start(k.w1[par][:, :, :], k.i["L1_ffn_w1"][bass.ds(e, 1), :, :].rearrange(
        "o (c p) f -> p (o c) f", p=P)).then_inc(loaded1[par], 16)
    eng.dma_start(k.w2[par][:, :, :], k.i["L1_ffn_w2"][bass.ds(e, 1), :, :].rearrange(
        "o (c p) d -> p (o c) d", p=P)).then_inc(loaded2[par], 16)


def moe_route(k):
    nc, i = k.nc, k.i
    norm = k.norm.start()
    k.dispatch = nc.dram_tensor("dispatch_scratch", (SLOTS + TOK, D), F32, kind="Internal").ap()
    k.expert_out = nc.dram_tensor("expert_scratch", (SLOTS, D), F32, kind="Internal").ap()
    k.w1_loaded, k.w2_loaded = k.sems("m_w1_loaded0", "m_w1_loaded1"), k.sems("m_w2_loaded0", "m_w2_loaded1")
    (ld, consts, own_p, zeroed, logits_full, shifted, exp_done, chosen, counted, indices, scattered,
     vec, casts) = k.sems(*("m0_" + n for n in (
         "ld", "consts", "own_p", "zeroed", "logits_full", "shifted", "exp_done", "chosen", "counted", "indices",
         "scattered", "vec", "casts")))

    with nc.Block() as block:
        @block.sync
        def _(sp):
            sp.dma_start(k.w_router[:, :, :], i["L1_ffn_w_gate"].rearrange("(c p) e -> p c e", p=P)
                         ).then_inc(ld, 16)
            sp.wait_ge(consts, 1)
            sp.dma_start(k.dispatch[0:SLOTS, :].rearrange("(j p) d -> p j d", p=P),
                         k.zeros[:, :].unsqueeze(1).to_broadcast([P, SLOTS // P, D])).then_inc(zeroed, 16)
            for par in range(2):
                load_expert(k, sp, par, par, k.w1_loaded, k.w2_loaded)

        @block.gpsimd
        def _(g):
            g.memset(k.zeros[:, :], 0.0).then_inc(consts, 1)
            g.memset(k.ones_tt[:, :], 1.0).then_inc(consts, 1)
            g.memset(k.earlier[:, :], 1.0).then_inc(own_p, 1)
            g.iota(k.expert_i[:, :], [[1, EXPERTS]], base=0, channel_multiplier=0).then_inc(casts, 1)
            g.iota(k.token_i[:, :], [[TT, NT]], base=SLOTS, channel_multiplier=1).then_inc(casts, 1)
            g.wait_ge(own_p, 1)
            g.affine_select(out=k.earlier[:, :], in_=k.earlier[:, :], compare_op=ALU.is_ge, fill=0.0, base=-1,
                            pattern=[[1, TT]], channel_multiplier=-1).then_inc(consts, 1)
            norm.wait_tiles(g, NT)
            g.wait_ge(zeroed, 16)
            g.wait_ge(indices, 2)
            for t in range(NT):
                g.indirect_dma_start(k.dispatch, bass.IndirectOffsetOnAxis(ap=k.put_i[:, t:t + 1], axis=0),
                                     k.normed[:, t, :], None).then_inc(scattered, 16)
            g.wait_ge(scattered, 16 * NT)

        @block.tensor
        def _(pe):
            norm.tensor(pe)
            norm.wait_all(pe)
            pe.wait_ge(ld, 16)
            for t in range(NT):
                for c in range(DK):
                    last = pe.matmul(k.bank(4, (0, TT), EXPERTS, t * EXPERTS), k.normed_t[:, c, t * TT:(t + 1) * TT],
                                     k.w_router[:, c, :], start=(c == 0), stop=(c == DK - 1))
            last.then_inc(logits_full, 1)
            pe.wait_ge(consts, 3)
            pe.wait_ge(chosen, 1)
            counts = k.bank(5, (0, TT), NT * EXPERTS)
            pe.matmul(counts, k.earlier[:, :], k.chosen[:, :, :], start=True, stop=False, skip_group_check=True)
            for t in range(NT - 1):
                last = pe.matmul(counts[:, (t + 1) * EXPERTS:], k.ones_tt[:, :],
                                 k.chosen[:, t:t + 1, :].to_broadcast([TT, NT - 1 - t, EXPERTS]),
                                 start=False, stop=(t == NT - 2), skip_group_check=True)
            last.then_inc(counted, 1)

        @block.scalar
        def _(a):
            norm.scalar(a)
            norm.copy_scalar(a)
            a.wait_ge(shifted, 1)
            a.activation(k.e_gates[:, :, :], k.logits[:, :, :], ACT.Exp).then_inc(exp_done, 1)

        @block.vector
        def _(v):
            chain = Chain(v, vec)
            each = lambda ap: ap[:, :].unsqueeze(2).to_broadcast([TT, NT, EXPERTS])
            row = lambda ap: ap[:, :].unsqueeze(1).to_broadcast([TT, NT, EXPERTS])

            def step(ins):
                chain.mark(ins)
                chain.settle()

            v.wait_ge(casts, 2)
            v.tensor_scalar(k.rank[:, :], k.expert_i[:, :], -1.0, float(EXPERTS), ALU.mult, ALU.add
                            ).then_inc(casts, 1)
            v.tensor_scalar(k.first_slot[:, :], k.expert_i[:, :], float(CAP), None, ALU.mult).then_inc(casts, 1)
            v.tensor_copy(k.spill[:, :], k.token_i[:, :]).then_inc(casts, 1)
            v.wait_ge(casts, 5)
            norm.vector(v, chain)
            norm.copy_vector(v)
            v.wait_ge(logits_full, 1)
            step(v.tensor_copy(k.logits[:, :, :], k.bank(4, (0, TT), NT * EXPERTS).rearrange(
                "p (t e) -> p t e", e=EXPERTS)))
            step(v.tensor_reduce(k.m_max[:, :], k.logits[:, :, :], AX.X, ALU.max))
            v.tensor_tensor(k.logits[:, :, :], k.logits[:, :, :], each(k.m_max), ALU.subtract
                            ).then_inc(shifted, 1)
            v.wait_ge(exp_done, 1)
            step(v.tensor_reduce(k.m_top[:, :], k.e_gates[:, :, :], AX.X, ALU.max))
            step(v.tensor_tensor(k.e_eq[:, :, :], k.e_gates[:, :, :], each(k.m_top), ALU.is_equal))
            step(v.tensor_tensor(k.e_tmp[:, :, :], k.e_eq[:, :, :], row(k.rank), ALU.mult))
            step(v.tensor_reduce(k.m_rank[:, :], k.e_tmp[:, :, :], AX.X, ALU.max))
            v.tensor_tensor(k.chosen[:, :, :], k.e_tmp[:, :, :], each(k.m_rank), ALU.is_equal
                            ).then_inc(chosen, 1)
            v.wait_ge(chosen, 1)
            chain.mark(v.tensor_reduce(k.m_sum[:, :], k.e_gates[:, :, :], AX.X, ALU.add))
            step(v.tensor_tensor(k.e_tmp2[:, :, :], k.chosen[:, :, :], row(k.first_slot), ALU.mult))
            chain.mark(v.tensor_reduce(k.m_slot[:, :], k.e_tmp2[:, :, :], AX.X, ALU.add))
            step(v.reciprocal(k.m_inv[:, :], k.m_sum[:, :]))
            chain.mark(v.tensor_tensor(k.m_w[:, :], k.m_top[:, :], k.m_inv[:, :], ALU.mult))
            v.wait_ge(counted, 1)
            step(v.tensor_tensor(k.e_tmp[:, :, :], k.chosen[:, :, :], k.bank(5, (0, TT), NT * EXPERTS).rearrange(
                "p (t e) -> p t e", e=EXPERTS), ALU.mult))
            step(v.tensor_reduce(k.m_loc[:, :], k.e_tmp[:, :, :], AX.X, ALU.add))
            chain.mark(v.tensor_scalar(k.m_kept[:, :], k.m_loc[:, :], float(CAP), None, ALU.is_lt))
            step(v.tensor_tensor(k.m_slot[:, :], k.m_slot[:, :], k.m_loc[:, :], ALU.add))
            chain.mark(v.tensor_tensor(k.m_diff[:, :], k.m_slot[:, :], k.spill[:, :], ALU.subtract))
            chain.mark(v.tensor_tensor(k.m_slot[:, :], k.m_slot[:, :], k.m_kept[:, :], ALU.mult))
            step(v.tensor_tensor(k.m_w[:, :], k.m_w[:, :], k.m_kept[:, :], ALU.mult))
            step(v.tensor_tensor(k.m_diff[:, :], k.m_diff[:, :], k.m_kept[:, :], ALU.mult))
            step(v.tensor_tensor(k.m_put[:, :], k.m_diff[:, :], k.spill[:, :], ALU.add))
            v.tensor_copy(k.put_i[:, :], k.m_put[:, :]).then_inc(indices, 1)
            v.tensor_copy(k.get_i[:, :], k.m_slot[:, :]).then_inc(indices, 1)
            step(v.tensor_scalar(k.m_w[:, :], k.m_w[:, :], k.gates[0:TT, 3:4], None, ALU.mult))


def moe_experts(k):
    nc = k.nc
    turn = k.norm
    turn.start_turn()
    rows_in, = k.sems("m1_rows_in")
    (h_full, gelu_done, expert_done, y_read, stored) = k.sems(*("m1_" + n for n in (
        "h_full", "gelu_done", "expert_done", "y_read", "stored")))

    with nc.Block() as block:
        @block.sync
        def _(sp):
            sp.dma_start(k.normed[:, :, :], k.dispatch[0:SLOTS, :].rearrange("(t p) d -> p t d", p=TT)
                         ).then_inc(rows_in, 16)

            def store_rows(e):
                sp.wait_ge(y_read, e + 3)
                sp.dma_start(k.expert_out[bass.ds(e * CAP, CAP), :].rearrange("(h p) d -> p h d", p=TT),
                             k.normed[:, bass.ds(2 * e, 2), :]).then_inc(stored, 16)

            with sp.Fori(0, EXPERTS // 2 - 1) as u:
                for par in range(2):
                    e = 2 * u + par
                    sp.wait_ge(expert_done, e + 3)
                    load_expert(k, sp, par, e + 2, k.w1_loaded, k.w2_loaded)
                    store_rows(e)
            for par in range(2):
                store_rows(EXPERTS - 2 + par)
            sp.wait_ge(stored, 16 * EXPERTS)

        @block.tensor
        def _(pe):
            pe.wait_ge(rows_in, 16)
            turn.tensor(pe)
            turn.wait_all(pe)
            for _n in range(2):
                pe.nop().then_inc(expert_done, 1)
            with pe.Fori(0, EXPERTS // 2) as u:
                for par in range(2):
                    e = 2 * u + par
                    pe.wait_ge(k.w1_loaded[par], 16 * (u + 1))
                    for f in range(FC):
                        if f % 2 == 0:
                            pe.wait_ge(gelu_done, 4 * e + f // 2 + 1)
                        for c in range(DK):
                            last = pe.matmul(k.bank(f // 2, (0, P), CAP, (f % 2) * CAP),
                                             k.w1[par][:, c, f * P:(f + 1) * P],
                                             k.normed_t[:, c, bass.ds(e * CAP, CAP)],
                                             start=(c == 0), stop=(c == DK - 1))
                        if f % 2 == 1:
                            last.then_inc(h_full, 1)
                    pe.wait_ge(k.w2_loaded[par], 16 * (u + 1))
                    pe.wait_ge(y_read, e + 1)
                    for half in range(2):
                        for f in range(FC):
                            if half == 0 and f % 2 == 0:
                                pe.wait_ge(gelu_done, 4 * e + f // 2 + 5)
                            last = pe.matmul(k.bank(4 + par, (0, TT), D, half * D),
                                             k.ff[par][:, f, half * TT:(half + 1) * TT], k.w2[par][:, f, :],
                                             start=(f == 0), stop=(f == FC - 1))
                    last.then_inc(expert_done, 1)

        @block.scalar
        def _(a):
            turn.copy_scalar(a)
            for _n in range(4):
                a.nop().then_inc(gelu_done, 1)
            with a.Fori(0, EXPERTS // 2) as u:
                for par in range(2):
                    e = 2 * u + par
                    a.wait_ge(expert_done, e + 1)
                    for b in range(FC // 2):
                        a.wait_ge(h_full, 4 * e + b + 1)
                        a.activation(k.ff[par][:, 2 * b:2 * b + 2, :].rearrange("p f n -> p (f n)"),
                                     k.bank(b, (0, P), 2 * CAP), ACT.Gelu_apprx_tanh).then_inc(gelu_done, 1)

        @block.vector
        def _(v):
            turn.copy_vector(v)
            for _n in range(2):
                v.engine_nop().then_inc(y_read, 1)
            with v.Fori(0, EXPERTS // 2) as u:
                for par in range(2):
                    e = 2 * u + par
                    v.wait_ge(expert_done, e + 3)
                    v.tensor_copy(k.normed[:, bass.ds(2 * e, 2), :].rearrange("p h d -> p (h d)"),
                                  k.bank(4 + par, (0, TT), 2 * D)).then_inc(y_read, 1)


def moe_combine(k):
    gathered = k.sems(*(f"m2_gathered{q}" for q in range(4)))
    added, out_done = k.sems("m2_added", "m2_out_done")
    Q = NT // 4
    with k.nc.Block() as block:
        @block.gpsimd
        def _(g):
            for t in range(NT):
                g.indirect_dma_start(k.back[:, t, :], None, k.expert_out, bass.IndirectOffsetOnAxis(
                    ap=k.get_i[:, t:t + 1], axis=0)).then_inc(gathered[t // Q], 16)

        @block.vector
        def _(v):
            for t in range(NT):
                if t % Q == 0:
                    v.wait_ge(gathered[t // Q], 16 * Q)
                v.scalar_tensor_tensor(out=k.resid[:, t, :], in0=k.back[:, t, :], scalar=k.m_w[:, t:t + 1],
                                       in1=k.resid[:, t, :], op0=ALU.mult, op1=ALU.add).then_inc(added, 1)

        @block.sync
        def _(sp):
            out = k.out.rearrange("(t b) s d -> (b s) t d", b=2)
            for q in range(4):
                sp.wait_ge(added, Q * (q + 1))
                sp.dma_start(out[:, Q * q:Q * (q + 1), :], k.resid[:, Q * q:Q * (q + 1), :]).then_inc(out_done, 16)
            sp.wait_ge(out_done, 64)


def build(nc, inputs, out, upto=4):
    k = Kit(nc, inputs, out)
    with k.keep:
        make_persistent(k)
        with ExitStack() as s:
            layer0_memory(k, s)
        setup(k)
        layer0_attention(k)
        if upto >= 2:
            with ExitStack() as s:
                ffn_memory(k, s)
            ffn_prepare(k)
            ffn_run(k)
        if upto >= 3:
            with ExitStack() as s:
                layer1_memory(k, s)
            layer1_prepare(k)
            layer1_attention(k)
        if upto >= 4:
            with ExitStack() as s:
                moe_memory(k, s)
            moe_route(k)
            moe_experts(k)
            moe_combine(k)
        else:
            store(k)


def store(k):
    done, = k.sems("out_done")
    with k.nc.Block() as block:
        @block.sync
        def _(sp):
            sp.dma_start(k.out.rearrange("(t b) s d -> (b s) t d", b=2), k.resid[:, :, :]).then_inc(done, 16)
            sp.wait_ge(done, 16)


_INS = ["x", "ctx_1024", "g_xattn", "g_ffn", "L0_xattn_Wq", "L0_xattn_bq",
        "L0_xattn_Wk", "L0_xattn_bk", "L0_xattn_Wv", "L0_xattn_bv", "L0_xattn_Wkv_dca",
        "L0_xattn_bkv_dca", "L0_xattn_qn_w", "L0_xattn_qn_b", "L0_xattn_kn_w", "L0_xattn_kn_b",
        "L0_xattn_kn_dca_w", "L0_xattn_kn_dca_b", "L0_xattn_Wo", "L0_xattn_bo",
        "L0_ffn_w_gate", "L0_ffn_w_up", "L0_ffn_w_down", "L0_ffn_up_reorder_index",
        "L0_ffn_down_reorder_index", "L1_xattn_Wq", "L1_xattn_Wk", "L1_xattn_Wv", "L1_xattn_Wo",
        "L1_ffn_w_gate", "L1_ffn_w1", "L1_ffn_w2", "mask_BxS2_bf1"]


def lay_out(inputs):
    import numpy as np
    a = {n: np.asarray(inputs[n]) for n in _INS}
    for kind in ("W", "b"):
        both = np.concatenate([a[f"L0_xattn_{kind}k"], a[f"L0_xattn_{kind}v"]], axis=-1)
        both = both.reshape(both.shape[:-1] + (HEADS, 2, HD0))
        for n, name in enumerate("kv"):
            a[f"L0_xattn_{kind}{name}"] = np.ascontiguousarray(
                both[..., n, :].reshape(both.shape[:-3] + (D,)))
    a["mask_BxS2_bf1"] = a["mask_BxS2_bf1"].view(np.uint8)
    return a


def kernel(**inputs):
    import numpy as np
    import concourse.bacc as bacc
    from concourse.bass_utils import run_bass_kernel_spmd

    arrays = lay_out(inputs)
    nc = bacc.Bacc("TRN2", target_bir_lowering=False, num_devices=1)
    fed, aps = {}, {}
    for name in _INS:
        a = np.ascontiguousarray(arrays[name])
        fed[f"in_{name}_dram"] = a
        aps[name] = nc.dram_tensor(f"in_{name}_dram", a.shape, mybir.dt.from_np(a.dtype),
                                   kind="ExternalInput").ap()
    aps["ctx"], aps["mask"] = aps["ctx_1024"], aps["mask_BxS2_bf1"]
    out = nc.dram_tensor("out_0_dram", (BATCH, SEQ, D), F32, kind="ExternalOutput").ap()
    build(nc, aps, out)
    r = run_bass_kernel_spmd(nc, [fed], core_ids=[0])
    return r.results[0]["out_0_dram"]
```

```python
from contextlib import ExitStack

import concourse.bass as bass
from concourse import mybir
from concourse.alu_op_type import AluOpType as ALU

ACT = mybir.ActivationFunctionType
AX = mybir.AxisListType
F32 = mybir.dt.float32
BF16 = mybir.dt.bfloat16
F16 = mybir.dt.float16
U32 = mybir.dt.uint32
I32 = mybir.dt.int32
U8 = mybir.dt.uint8

P = 128
BATCH, SEQ, D = 32, 56, 256
KEYS, DC = 1500, 128
PAIRS = BATCH // 2
TT = 2 * SEQ
NT = PAIRS
TOK = BATCH * SEQ
DK = D // P
BANK = 512
HEADS = 16
HQ = HEADS * SEQ
HALF = HQ // 2
QT = HQ // P
CHUNKS = 12
LN_EPS = 1e-5

HD0 = 16
DCA = 16
MAIN = KEYS - DCA
QK_EPS = 1e-6
CH0 = 124
SPAN0 = 4 * CH0
STEP0 = (MAIN - SPAN0) // 2
DUP0 = SPAN0 - STEP0
SCALE0 = HD0 ** -0.5
UP = 16.0
HPAIRS = HEADS // 2
PARTS = 3 * 2 * HD0
VW = HD0 + 1
PW = 2 * VW
PSPAN = 64 + PW


class Turns:

    def __init__(self, prologue, first, middle, last, epilogue):
        self.lists = {"pro": prologue, "first": first, "mid": middle, "last": last, "epi": epilogue}
        self.base = {"pro": 0, "first": len(prologue)}
        self.base["mid"] = self.base["first"] + len(first)
        self.base["last"] = self.base["mid"] + (PAIRS - 2) * len(middle)
        self.base["epi"] = self.base["last"] + len(last)

    def number(self, part, pair, unit):
        n = self.base[part] + self.lists[part].index(unit)
        if part == "mid":
            return (pair - 1) * len(self.lists["mid"]) + n
        return n


class Ring:

    def __init__(self, full, free, **lists):
        self.full, self.free, self.lists = full, free, lists
        self.start, at = {}, {"n": 0, **{r: 0 for r in free}}
        for part in ("pro", "first", "mid", "last", "epi"):
            self.start[part] = dict(at)
            times = PAIRS - 2 if part == "mid" else 1
            for r in at:
                at[r] += times * self.per_turn(part, r)

    def per_turn(self, part, reader):
        return sum(reader in ("n", r) for _key, r in self.lists[part])

    def place(self, part, key):
        return [k for k, _r in self.lists[part]].index(key)

    def count(self, part, pair, place, reader):
        n = self.start[part][reader] + sum(reader in ("n", r) for _key, r in self.lists[part][:place])
        if part == "mid":
            return (pair - 1) * self.per_turn(part, reader) + n
        return n

    def bank(self, part, key):
        return self.place(part, key) % 3

    def wait_bank(self, pe, part, pair, key):
        place = self.place(part, key)
        if place >= 3:
            reader = self.lists[part][place - 3][1]
            pe.wait_ge(self.free[reader], self.count(part, pair, place - 3, reader) + 1)
        else:
            for reader in self.free:
                at_least(pe, self.free[reader], self.count(part, pair, 0, reader))

    def wait_full(self, eng, part, pair, key):
        eng.wait_ge(self.full, self.written(part, pair, key))

    def written(self, part, pair, key):
        return self.count(part, pair, self.place(part, key), "n") + 1

    def was_read(self, part, pair, key):
        place = self.place(part, key)
        return self.count(part, pair, place, self.lists[part][place][1]) + 1


def at_least(eng, sem, value):
    if isinstance(value, int) and value <= 0:
        return
    eng.wait_ge(sem, value)


def wait_alone(k, eng, sem, value):
    eng.wait_ge(sem, value).then_inc(k.waits_passed, 1)


class Chain:

    def __init__(self, eng, sem):
        self.eng, self.sem, self.n = eng, sem, 0

    def mark(self, ins):
        ins.then_inc(self.sem, 1)
        self.n += 1
        return self.n

    def settle(self):
        self.eng.wait_ge(self.sem, self.n)


class Kit:

    def __init__(self, nc, inputs, out):
        self.nc, self.i, self.out = nc, inputs, out
        self.keep = ExitStack()

    def sem(self, name):
        return self.keep.enter_context(self.nc.semaphore(name))

    def sems(self, *names):
        return [self.sem(n) for n in names]

    def sbuf(self, stack, name, shape, dt=F32):
        return stack.enter_context(self.nc.sbuf_tensor(name, shape, dt))

    def bank(self, n, rows, cols, at=0):
        lo = n * BANK + at
        return self.psum[rows[0]:rows[1], lo:lo + cols]

    def banks(self, n, count, rows, cols):
        return self.psum[rows[0]:rows[1], n * BANK:(n + count) * BANK].rearrange(
            "p (b c) -> p b c", c=BANK)[:, :, 0:cols]


def make_persistent(k):
    k.psum = k.keep.enter_context(k.nc.psum_tensor("psum", [P, 8 * BANK], F32))
    sb = lambda name, shape, dt=F32: k.sbuf(k.keep, name, shape, dt)
    k.resid = sb("resid", [TT, NT, D])
    k.ident = sb("ident", [P, P])
    k.ident_bf = sb("ident_bf", [P, P], BF16)
    k.ones_row = sb("ones_row", [1, P])
    k.bn = sb("bn", [TT, NT, 6])
    k.moments = sb("moments", [TT, NT, 2])
    k.var_eps = sb("var_eps", [TT, NT])
    k.log_var = sb("log_var", [TT, NT])
    k.rough = sb("rough", [TT, NT])
    k.newton = sb("newton", [TT, NT])
    k.newton2 = sb("newton2", [TT, NT])
    k.rstd = sb("rstd", [TT, NT])
    k.eps_ln = sb("eps_ln", [P, 1])
    k.eps_qk = sb("eps_qk", [P, 1])
    k.gates = sb("gates", [P, 4])
    k.gates_raw = sb("gates_raw", [1, 4])
    k.gates_th = sb("gates_th", [1, 4])
    k.norm = Norm(k)
    k.waits_passed = k.sem("waits_passed")
    with ExitStack() as s:
        k.normed = k.sbuf(s, "normed", [TT, NT, D])
        k.normed_t = k.sbuf(s, "normed_t", [P, DK, TOK])
    with ExitStack() as s:
        k.probs = [k.sbuf(s, f"probs{i}", [P, 2, HALF]) for i in range(2)]
        with ExitStack() as s1:
            k.heads_n = k.sbuf(s1, "heads_n", [P, QT, DC])
            k.heads_t = k.sbuf(s1, "heads_t", [DC, HEADS, 2, SEQ])
        with ExitStack() as s0:
            k.values_a = k.sbuf(s0, "values_a", [CH0, CHUNKS, HPAIRS * PW])
            k.rows_raw = k.sbuf(s0, "rows_raw", [CH0, CHUNKS, DC])
            k.sums_t = k.sbuf(s0, "sums_t", [P, HALF])
            k.sums_dt = k.sbuf(s0, "sums_dt", [P, HALF])
    k.sbuf(k.keep, "norm_area", [P, NT * D + DK * TOK])


class Turner:

    def __init__(self, k):
        self.k, self.runs = k, 0
        self.turned, self.copied_a, self.copied_v = k.sems("turned", "copied_a", "copied_v")

    def start_turn(self, tiles_counted=False):
        self.base = self.runs * (NT // 4)
        self.tiles_counted = tiles_counted
        self.runs += 1

    def _group(self, g, piece):
        return self.k.bank(2 * (g % 2) + piece, (0, P), 4 * TT)

    def tensor(self, pe):
        k = self.k
        for t in range(NT):
            g = t // 4
            if self.tiles_counted:
                self.wait_tiles(pe, t + 1)
            if t % 4 == 0 and g >= 2:
                pe.wait_ge(self.copied_a, self.base + g - 1)
                pe.wait_ge(self.copied_v, self.base + g - 1)
            for c in range(DK):
                last = pe.transpose(self._group(g, c)[:, (t % 4) * TT:(t % 4 + 1) * TT],
                                    k.normed[:, t, c * P:(c + 1) * P], k.ident[0:TT, 0:TT])
            if t % 4 == 3:
                last.then_inc(self.turned, 1)

    def copy_scalar(self, a):
        k = self.k
        for g in range(NT // 4):
            a.wait_ge(self.turned, self.base + g + 1)
            a.activation(k.normed_t[:, 0, g * 4 * TT:(g + 1) * 4 * TT], self._group(g, 0),
                         ACT.Identity).then_inc(self.copied_a, 1)

    def copy_vector(self, v):
        k = self.k
        for g in range(NT // 4):
            v.wait_ge(self.turned, self.base + g + 1)
            v.tensor_copy(k.normed_t[:, 1, g * 4 * TT:(g + 1) * 4 * TT],
                          self._group(g, 1)).then_inc(self.copied_v, 1)

    def wait_all(self, eng):
        eng.wait_ge(self.copied_a, self.base + NT // 4)
        eng.wait_ge(self.copied_v, self.base + NT // 4)


class Norm(Turner):

    def __init__(self, k):
        super().__init__(k)
        self.norms = 0
        self.stats, self.rough, self.tile, self.log_done = k.sems(
            "norm_stats", "norm_rough", "norm_tile", "norm_log")

    def start(self):
        self.norms += 1
        self.start_turn(tiles_counted=True)
        return self

    def wait_tiles(self, eng, count):
        eng.wait_ge(self.tile, NT * (self.norms - 1) + count)

    def vector(self, v, chain):
        k = self.k
        for t in range(NT):
            chain.mark(v.bn_stats(k.bn[:, t, :], k.resid[:, t, :]))
        chain.settle()
        for t in range(NT):
            chain.mark(v.bn_aggr(k.moments[:, t, :], k.bn[:, t, :]))
        chain.settle()
        v.tensor_scalar(k.var_eps[:, :], k.moments[:, :, 1], LN_EPS, None, ALU.add).then_inc(self.stats, 1)
        v.wait_ge(self.stats, self.norms)
        v.wait_ge(self.rough, self.norms)
        chain.mark(v.tensor_tensor(k.newton[:, :], k.var_eps[:, :], k.rough[:, :], ALU.mult))
        chain.settle()
        chain.mark(v.tensor_tensor(k.newton2[:, :], k.newton[:, :], k.rough[:, :], ALU.mult))
        chain.settle()
        chain.mark(v.tensor_scalar(k.newton[:, :], k.newton2[:, :], -0.5, 1.5, ALU.mult, ALU.add))
        chain.settle()
        chain.mark(v.tensor_tensor(k.rstd[:, :], k.newton[:, :], k.rough[:, :], ALU.mult))
        chain.settle()
        for t in range(NT):
            v.tensor_scalar(k.normed[:, t, :], k.resid[:, t, :], k.moments[:, t, 0:1],
                            k.rstd[:, t:t + 1], ALU.subtract, ALU.mult).then_inc(self.tile, 1)

    def scalar(self, a):
        k = self.k
        a.wait_ge(self.stats, self.norms)
        a.activation(k.log_var[:, :], k.var_eps[:, :], ACT.Ln).then_inc(self.log_done, 1)
        a.wait_ge(self.log_done, self.norms)
        a.activation(k.rough[:, :], k.log_var[:, :], ACT.Exp, scale=-0.5).then_inc(self.rough, 1)



def layer0_memory(k, s):
    sb = lambda name, shape, dt=F32: k.sbuf(s, name, shape, dt)
    k.wk = sb("wk", [DC, D])
    k.wkv_d = sb("wkv_d", [DC, 2 * D])
    k.wv = sb("wv", [DC, D])
    k.wo_par = sb("wo_par", [P, 2, D])
    k.wmean = sb("wmean", [P, 4, HEADS])
    k.same_head = sb("same_head", [P, P])
    k.row_parity3 = sb("row_parity3", [PARTS, 3, 2])
    k.row_parity = sb("row_parity", [PARTS, 2])
    k.col_parity = sb("col_parity", [TT, 2])
    k.rep16 = sb("rep16", [HD0, P])
    k.small16 = sb("small16", [HD0, 6])
    k.lnwb = sb("lnwb", [P, 6])
    k.bias_in = sb("bias_in", [P, 6])
    k.bias_c = sb("bias_c", [P, 6])
    k.bv_in = sb("bv_in", [P, 4])
    k.bv_sum = sb("bv_sum", [P, 2])
    k.bo_row = sb("bo_row", [1, D])
    k.bo_b = sb("bo_b", [TT, D])
    k.q_stack = sb("q_stack", [PARTS, HPAIRS, TOK], F16)
    k.q_diag = [sb(f"q_diag{i}", [P, HPAIRS, 2, SEQ], F16) for i in range(2)]
    k.key_stack = [sb(f"key_stack{i}", [P, HPAIRS, 3, BANK], F16) for i in range(2)]
    k.key_hi = sb("key_hi", [P, 2, 3, BANK], F16)
    k.key_lo = sb("key_lo", [P, 2, 3, BANK], F16)
    with ExitStack() as tmp:
        k.wq = k.sbuf(tmp, "wq", [P, DK, D])
        k.wo0 = k.sbuf(tmp, "wo0", [P, DK, D])
        k.bv_cols = k.sbuf(tmp, "bv_cols", [P, 2, TT])
        k.q_all = k.sbuf(tmp, "q_all", [P, 2, TOK])
        k.q_hi = k.sbuf(tmp, "q_hi", [P, 2, TOK], F16)
        k.q_lo = k.sbuf(tmp, "q_lo", [P, 2, TOK], F16)
        k.qtmp, k.qsq, k.qlog, k.qrs, k.qhat = (k.sbuf(tmp, name, [P, 2, 4 * TT]) for name in (
            "qtmp", "qsq", "qlog", "qrs", "qhat"))
    k.values = [k.values_a, sb("values_b", [CH0, CHUNKS, HPAIRS * PW])]
    k.kc = sb("kc", [P, 2, 3, BANK])
    k.ksq = sb("ksq", [P, 3, BANK])
    k.krs = sb("krs", [P, 3, BANK])
    k.values_d = [sb(f"values_d{i}", [DCA, HPAIRS * PW]) for i in range(2)]
    k.rows_d = sb("rows_d", [DCA, DC])
    k.ctx_t = sb("ctx_t", [DC, 3, BANK])
    k.maxima = sb("maxima", [TT, HPAIRS, 4])
    k.shift_col = sb("shift_col", [TT, 2, HPAIRS], BF16)
    k.probs_d = sb("probs_d", [DCA, 2, HALF])
    k.rsum, k.rpar, k.rsum_d, k.rpar_d = (sb(n, [TT, HPAIRS, 2]) for n in ("rsum", "rpar", "rsum_d", "rpar_d"))
    k.parts, k.parts_d = (sb(n, [TT, HPAIRS, 2, HD0]) for n in ("parts", "parts_d"))
    k.att_d, k.att_half, k.att = (sb(n, [TT, HPAIRS, HD0]) for n in ("att_d", "att_half", "att"))
    k.att_t = sb("att_t", [P, 2, 2, SEQ])
    k.ytmp = sb("ytmp", [TT, D])


def setup(k):
    nc, i = k.nc, k.i
    norm = k.norm.start()
    (ld_x, ld_small, ld_w, consts, pool_own, w_ready, pe_small, small_ready, q_full, q_cen, q_log,
     q_rstd, q_var, q_hat, q_done, vec, gates_rd, stacked, act_own, q_read) = k.sems(
        "ld_x", "ld_small", "ld_w", "consts", "pool_own", "w_ready", "pe_small", "small_ready",
        "q_full", "q_cen", "q_log", "q_rstd", "q_var", "q_hat", "q_done", "vec", "gates_rd",
        "stacked", "act_own", "q_read")
    GROUP = 4 * TT

    with nc.Block() as block:
        @block.sync
        def _(sp):
            x_tiles = i["x"].rearrange("(t b) s d -> (b s) t d", b=2)
            sp.dma_start(k.resid[:, 0:8, :], x_tiles[:, 0:8, :]).then_inc(ld_x, 16)
            sp.dma_start(k.resid[:, 8:16, :], x_tiles[:, 8:16, :]).then_inc(ld_x, 16)
            sp.dma_start(k.wq[:, :, :], i["L0_xattn_Wq"].rearrange("(c p) n -> p c n", p=P)).then_inc(ld_w, 16)
            sp.dma_start(k.wk[:, :], i["L0_xattn_Wk"]).then_inc(ld_w, 16)
            sp.dma_start(k.wkv_d[:, :], i["L0_xattn_Wkv_dca"]).then_inc(ld_w, 16)
            sp.dma_start(k.wv[:, :], i["L0_xattn_Wv"]).then_inc(ld_w, 16)
            sp.dma_start(k.wo0[:, :, :], i["L0_xattn_Wo"].rearrange("(c p) n -> p c n", p=P)).then_inc(ld_w, 16)
            for m in range(HPAIRS):
                sp.dma_start(k.wo_par[HD0 * m:HD0 * (m + 1), :, :], i["L0_xattn_Wo"][
                    2 * HD0 * m:2 * HD0 * (m + 1), :].rearrange("(e d) n -> d e n", d=HD0)).then_inc(ld_w, 16)
            for h in range(2):
                sp.wait_ge(q_read, 4 * (h + 1))
                for p in range(4):
                    for part, src in enumerate((k.q_hi, k.q_hi, k.q_lo)):
                        sp.dma_start(k.q_stack[32 * part:32 * part + 32, 4 * h + p, :],
                                     src[32 * p:32 * p + 32, h, :]).then_inc(stacked, 16)
            sp.wait_ge(stacked, 16 * 3 * HPAIRS)

        @block.gpsimd
        def _(g):
            g.memset(k.ident[:, :], 0.0).then_inc(pool_own, 1)
            g.memset(k.same_head[:, :], 1.0 / HD0).then_inc(pool_own, 1)
            g.memset(k.row_parity3[:, :, :], 1.0).then_inc(pool_own, 1)
            g.memset(k.col_parity[:, :], 1.0).then_inc(pool_own, 1)
            g.memset(k.rep16[:, :], 0.0).then_inc(pool_own, 1)
            g.wait_ge(pool_own, 5)
            g.affine_select(out=k.ident[:, :], in_=k.ident[:, :], compare_op=ALU.not_equal, fill=1.0,
                            base=0, pattern=[[-1, P]], channel_multiplier=1).then_inc(pool_own, 1)
            heads = k.same_head[:, :].rearrange("p (e d) -> p e d", d=HD0)
            blocks = ((heads, HD0, [[-HD0, 8], [0, HD0]]), (k.row_parity3[:, :, :], HD0, [[-2 * HD0, 3], [-HD0, 2]]),
                      (k.col_parity[:, :], SEQ, [[-SEQ, 2]]))
            for ap, _height, first in blocks:
                g.affine_select(out=ap, in_=ap, compare_op=ALU.is_ge, fill=0.0, base=0, pattern=first,
                                channel_multiplier=1).then_inc(pool_own, 1)
            rep = k.rep16[:, :].rearrange("p (e d) -> p e d", d=HD0)
            g.affine_select(out=rep, in_=rep, compare_op=ALU.not_equal, fill=1.0, base=0,
                            pattern=[[0, 8], [-1, HD0]], channel_multiplier=1).then_inc(pool_own, 1)
            g.wait_ge(pool_own, 10)
            for ap, height, first in blocks:
                g.affine_select(out=ap, in_=ap, compare_op=ALU.is_ge, fill=0.0, base=height - 1,
                                pattern=[[-step, n] for step, n in first], channel_multiplier=-1
                                ).then_inc(pool_own, 1)
            g.tensor_copy(k.ident_bf[:, :], k.ident[:, :]).then_inc(pool_own, 1)
            g.memset(k.ones_row[:, :], 1.0).then_inc(pool_own, 1)
            g.memset(k.eps_ln[:, :], LN_EPS).then_inc(pool_own, 1)
            g.memset(k.eps_qk[:, :], QK_EPS).then_inc(pool_own, 1)
            g.wait_ge(pool_own, 17)
            for n, name in enumerate(("qn_w", "qn_b", "kn_w", "kn_b", "kn_dca_w", "kn_dca_b")):
                g.dma_start(k.small16[:, n:n + 1],
                            i["L0_xattn_" + name].rearrange("(d o) -> d o", o=1)).then_inc(ld_small, 16)
            rows = lambda v: v.rearrange("(c p) -> p c", p=P)
            g.dma_start(k.bias_in[:, 0:2], rows(i["L0_xattn_bq"]), allow_slow_non_contiguous=True).then_inc(ld_small, 16)
            g.dma_start(k.bias_in[:, 2:4], rows(i["L0_xattn_bk"]), allow_slow_non_contiguous=True).then_inc(ld_small, 16)
            g.dma_start(k.bias_in[:, 4:6], rows(i["L0_xattn_bkv_dca"][0:D]), allow_slow_non_contiguous=True).then_inc(ld_small, 16)
            g.dma_start(k.bv_in[:, 0:2], rows(i["L0_xattn_bv"]), allow_slow_non_contiguous=True).then_inc(ld_small, 16)
            g.dma_start(k.bv_in[:, 2:4], rows(i["L0_xattn_bkv_dca"][D:2 * D]), allow_slow_non_contiguous=True).then_inc(ld_small, 16)
            g.dma_start(k.bo_row[:, :], i["L0_xattn_bo"].rearrange("(o d) -> o d", o=1)).then_inc(ld_small, 16)
            g.dma_start(k.gates_raw[:, 0:2], i["g_xattn"].rearrange("(o d) -> o d", o=1)).then_inc(ld_small, 16)
            g.dma_start(k.gates_raw[:, 2:4], i["g_ffn"].rearrange("(o d) -> o d", o=1)).then_inc(ld_small, 16)
            for n in range(2):
                tail = k.key_stack[n][PARTS:P, :, :, :]
                g.memset(tail, 0.0).then_inc(consts, 1)
                g.memset(k.q_diag[n][PARTS:P, :, :, :], 0.0).then_inc(consts, 1)
                g.wait_ge(consts, 2 + 5 * n)
                g.memset(k.key_stack[n][PARTS:PARTS + 2, :, 2, SPAN0:BANK], UP * UP).then_inc(consts, 1)
                g.wait_ge(consts, 3 + 5 * n)
                g.memset(k.key_stack[n][PARTS:PARTS + 1, :, 2, SPAN0:BANK], 0.0).then_inc(consts, 1)
                g.memset(k.key_stack[n][PARTS:PARTS + 1, :, :, 0:SPAN0], UP * UP).then_inc(consts, 1)
            g.wait_ge(consts, 10)

        @block.vector
        def _(v):
            chain = Chain(v, vec)
            v.wait_ge(ld_w, 16 * (5 + HPAIRS))
            groups = ((k.wq[:, 0, :], 0), (k.wq[:, 1, :], 1), (k.wk[:, :], 2), (k.wkv_d[:, 0:D], 3))
            for w, n in groups:
                chain.mark(v.tensor_reduce(k.wmean[:, n, :], w.rearrange("p (h d) -> p h d", d=HD0),
                                           AX.X, ALU.add))
            chain.settle()
            chain.mark(v.tensor_scalar(k.wmean[:, :, :], k.wmean[:, :, :], 1.0 / HD0, None, ALU.mult))
            chain.settle()
            for w, n in groups:
                w3 = w.rearrange("p (h d) -> p h d", d=HD0)
                v.tensor_tensor(w3, w3, k.wmean[:, n, :].unsqueeze(2).to_broadcast([P, HEADS, HD0]),
                                ALU.subtract).then_inc(w_ready, 1)
            v.wait_ge(pool_own, 17)
            chain.mark(v.tensor_tensor(k.row_parity[:, :], k.row_parity3[:, 0, :], k.row_parity3[:, 1, :], ALU.add))
            chain.settle()
            chain.mark(v.tensor_tensor(k.row_parity[:, :], k.row_parity[:, :], k.row_parity3[:, 2, :], ALU.add))
            v.wait_ge(ld_small, 16 * 14)
            chain.mark(v.tensor_tensor(k.bv_sum[:, :], k.bv_in[:, 0:2], k.bv_in[:, 2:4], ALU.add))
            chain.settle()
            v.tensor_copy(k.bv_cols[:, :, :], k.bv_sum[:, :].unsqueeze(2).to_broadcast([P, 2, TT])
                          ).then_inc(small_ready, 1)
            v.wait_ge(ld_x, 32)
            norm.vector(v, chain)
            v.wait_ge(ld_small, 16 * 14)
            v.wait_ge(pe_small, 1)
            v.tensor_scalar(k.lnwb[:, :], k.bank(4, (0, P), 6), UP, None, ALU.mult).then_inc(small_ready, 1)
            v.tensor_tensor(k.bias_c[:, :], k.bias_in[:, :], k.bank(4, (0, P), 6, 8), ALU.subtract
                            ).then_inc(small_ready, 1)
            v.tensor_copy(k.bo_b[:, :], k.bank(5, (0, TT), D)).then_inc(small_ready, 1)
            v.tensor_copy(k.gates[:, :], k.bank(4, (0, P), 4, 16)).then_inc(small_ready, 1)
            norm.copy_vector(v)
            for n in range(8):
                h, g = divmod(n, 4)
                v.wait_ge(q_rstd, n + 1)
                v.wait_ge(small_ready, 5)
                v.tensor_tensor(k.qhat[:, n % 2, :], k.qtmp[:, n % 2, :], k.qrs[:, n % 2, :],
                                ALU.mult).then_inc(q_hat, 1)
                v.wait_ge(q_hat, n + 1)
                v.tensor_scalar(k.q_all[:, h, g * GROUP:(g + 1) * GROUP], k.qhat[:, n % 2, :],
                                k.lnwb[:, 0:1], k.lnwb[:, 1:2], ALU.mult, ALU.add).then_inc(q_done, 1)
                v.wait_ge(q_done, n + 1)
                part = (slice(None), h, slice(g * GROUP, (g + 1) * GROUP))
                chain.mark(v.tensor_copy(k.q_hi[part], k.q_all[part]))
                chain.settle()
                v.tensor_tensor(k.q_lo[part], k.q_all[part], k.q_hi[part], ALU.subtract).then_inc(q_read, 1)
            v.wait_ge(w_ready, 4)

        @block.tensor
        def _(pe):
            pe.wait_ge(pool_own, 17)
            pe.wait_ge(ld_small, 16 * 14)
            pe.wait_ge(gates_rd, 1)
            pe.matmul(k.bank(4, (0, P), 6), k.rep16[:, :], k.small16[:, :], start=True, stop=True)
            pe.matmul(k.bank(4, (0, P), 6, 8), k.same_head[:, :], k.bias_in[:, :], start=True, stop=True)
            pe.matmul(k.bank(4, (0, P), 4, 16), k.ones_row[:, :], k.gates_th[:, :], start=True, stop=True)
            pe.wait_ge(ld_w, 16 * (5 + HPAIRS))
            pe.wait_ge(small_ready, 1)
            for h in range(2):
                pe.matmul(k.bank(5, (0, TT), D), k.bv_cols[:, h, :], k.wo0[:, h, :], start=(h == 0), stop=False)
            pe.matmul(k.bank(5, (0, TT), D), k.ones_row[:, 0:TT], k.bo_row[:, :], start=False,
                      stop=True).then_inc(pe_small, 1)
            norm.tensor(pe)
            norm.wait_all(pe)
            pe.wait_ge(w_ready, 4)
            for n in range(9):
                if n < 8:
                    h, g = divmod(n, 4)
                    q = k.bank(n % 2, (0, P), GROUP)
                    if n >= 2:
                        pe.wait_ge(q_cen, n - 1)
                    for c in range(DK):
                        last = pe.matmul(q, k.wq[:, c, h * P:(h + 1) * P],
                                         k.normed_t[:, c, g * GROUP:(g + 1) * GROUP],
                                         start=(c == 0), stop=(c == DK - 1))
                    last.then_inc(q_full, 1)
                if n >= 1:
                    m = n - 1
                    pe.wait_ge(q_cen, m + 1)
                    if m >= 2:
                        pe.wait_ge(q_log, m - 1)
                    pe.matmul(k.bank(2 + m % 2, (0, P), GROUP), k.same_head[:, :], k.qsq[:, m % 2, :],
                              start=True, stop=True).then_inc(q_var, 1)

        @block.scalar
        def _(a):
            a.wait_ge(ld_small, 16 * 14)
            a.activation(k.gates_th[:, :], k.gates_raw[:, :], ACT.Tanh).then_inc(gates_rd, 1)
            a.preload_act_table_set("natural_log_exp_and_others")
            norm.scalar(a)
            norm.copy_scalar(a)
            a.wait_ge(small_ready, 5)
            a.wait_ge(pool_own, 17)
            for n in range(9):
                if n < 8:
                    h, buf = n // 4, n % 2
                    a.wait_ge(q_full, n + 1)
                    if n >= 2:
                        a.wait_ge(q_hat, n - 1)
                        a.wait_ge(q_var, n - 1)
                    src = k.bank(n % 2, (0, P), GROUP)
                    a.activation(k.qtmp[:, buf, :], src, ACT.Identity, bias=k.bias_c[:, h:h + 1]
                                 ).then_inc(act_own, 1)
                    a.activation(k.qsq[:, buf, :], src, ACT.Square, bias=k.bias_c[:, h:h + 1]
                                 ).then_inc(q_cen, 1)
                if n >= 1:
                    m = n - 1
                    a.wait_ge(q_var, m + 1)
                    a.activation(k.qlog[:, m % 2, :], k.bank(2 + m % 2, (0, P), GROUP), ACT.Ln,
                                 bias=k.eps_qk[:, 0:1]).then_inc(q_log, 1)
                    a.wait_ge(q_log, m + 1)
                    if m >= 2:
                        a.wait_ge(q_hat, m - 1)
                    a.activation(k.qrs[:, m % 2, :], k.qlog[:, m % 2, :], ACT.Exp, scale=-0.5
                                 ).then_inc(q_rstd, 1)


PREP0 = ["T", "K0", "V0", "K1", "V1", "W0", "W1", "WD"] + [f"M{m}" for m in range(HPAIRS)] + ["R"]
SLOTS0 = {0: (["SD"], ["T"]), 1: (["PD"], ["OT"]), 2: (["K0"], ["ODT"]), 3: (["V0"], ["K1"]),
          4: (["C"], ["V1"]), 5: (["Y"], ["W0"]), 6: (["W1"], ["WD"]), 7: (["M0"], ["M1"]),
          8: (["M2"], ["M3"]), 9: (["M4"], ["M5"]), 10: (["M6"], ["M7"]), 11: (["R"], [])}


def runs0(part, odd, unit):
    if unit == "Y" and odd:
        return False
    if part == "first" and not odd and unit in ("OT", "C", "Y"):
        return False
    return not (part == "last" and odd and unit in PREP0)


def pieces0(unit):
    if unit in ("PD", "OT", "ODT", "Y"):
        return 1, "v"
    if unit in ("C", "WD"):
        return 1, "a"
    if unit in ("SD", "R"):
        return 2, "a" if unit == "SD" else "v"
    return 3, "v" if unit[0] == "M" else "a"


def expand0(units):
    return [((odd, u, n), pieces0(u)[1]) for odd, u in units for n in range(pieces0(u)[0])]


def order0(part):
    return expand0([(odd, u) for odd in range(2) for j in range(CHUNKS) for side in SLOTS0[j] for u in side
                    if runs0(part, odd, u)])


def pair_loop(eng, body):
    body("first", 0)
    with eng.Fori(1, PAIRS - 1) as pair:
        body("mid", pair)
    body("last", PAIRS - 1)


def layer0_attention(k):
    nc, i = k.nc, k.i
    (full, free_a, free_v, s_full, shift_done, exp_done, pv_done, rstd, khat, keys_fin, hi_done, lo_done, q_ready, dup_rows, row_ready,
     o_read, rs_own, rsd_own, att_ready, resid_done, loaded, consts) = k.sems(*("a0_" + n for n in (
         "shared_full", "shared_free_a", "shared_free_v", "scores_full", "shift_done", "exp_done", "pv_done", "rstd", "khat", "keys_fin", "hi_done",
         "lo_done", "q_ready", "dup_rows", "row_ready", "o_read", "rs_own", "rsd_own", "att_ready", "resid_done",
         "loaded", "consts")))
    ring = Ring(full, {"a": free_a, "v": free_v}, pro=expand0([(1, u) for u in PREP0]), first=order0("first"),
                mid=order0("mid"), last=order0("last"), epi=expand0([(0, u) for u in ("OT", "C", "Y")]))
    stacked = k.sems("a0_stacked0", "a0_stacked1")
    LOADS = 4
    STACKS = 12
    CONSTS = 8
    S, O, SHARED = 0, 4, 5

    def spans(b):
        return [(0, SPAN0, 0)] + ([(SPAN0, BANK, 1)] if b == 2 else [])

    def scores_bank(j, rows):
        return k.banks(S + 2 * (j % 2), 2, rows, HALF)

    def chunk_cols(j):
        return j // 4, (j % 4) * CH0

    def pair_block(bank, m):
        at = 64 * (m % 2)
        return k.bank(bank, (at, at + PW), TT, (m // 2) * TT)

    with nc.Block() as block:
        @block.sync
        def _(sp):
            def load(batch):
                for b in range(3):
                    sp.dma_start(
                        k.rows_raw[:, 4 * b:4 * b + 4, :],
                        i["ctx"][bass.ds(batch, 1), b * STEP0:b * STEP0 + SPAN0, :].rearrange(
                            "o (c p) d -> p (o c) d", p=CH0)).then_inc(loaded, 16)
                sp.dma_start(k.rows_d[:, :],
                             i["ctx"][bass.ds(batch, 1), MAIN:KEYS, :].rearrange("o p d -> p (o d)")
                             ).then_inc(loaded, 16)

            def stack(nb, nxt):
                for h in range(2):
                    wait_alone(k, sp, hi_done, 2 * nb + h + 1)
                    for part in (0, 2):
                        for p in range(4):
                            sp.dma_start(k.key_stack[nxt][32 * part:32 * part + 32, 4 * h + p, :, :],
                                         k.key_hi[32 * p:32 * p + 32, h, :, :]).then_inc(stacked[h], 16)
                    wait_alone(k, sp, lo_done, 2 * nb + h + 1)
                    for p in range(4):
                        sp.dma_start(k.key_stack[nxt][32:64, 4 * h + p, :, :],
                                     k.key_lo[32 * p:32 * p + 32, h, :, :]).then_inc(stacked[h], 16)

            def body(part, pair):
                for odd in range(2):
                    batch = 2 * pair + odd
                    if part == "last" and odd:
                        continue
                    if part != "last":
                        wait_alone(k, sp, full, ring.written(part, pair, (odd, "T", 2)))
                        load(batch + 2)
                    wait_alone(k, sp, s_full, CHUNKS * batch + 1)
                    stack(batch + 1, 1 - odd)

            load(0)
            sp.wait_ge(full, ring.written("pro", 0, (1, "T", 2)))
            load(1)
            stack(0, 0)
            pair_loop(sp, body)

        @block.tensor
        def _(pe):
            def weighted(bank, values, probs, n, start, stop):
                flat = probs[0:n, :, :].rearrange("p h c -> p (h c)")
                for m in range(HPAIRS):
                    last = pe.matmul(pair_block(bank, m), values[:, m * PW:(m + 1) * PW],
                                     flat[:, m * TT:(m + 1) * TT], start=start and m < 2, stop=stop,
                                     skip_group_check=True)
                return last

            def scored(dst, half, odd, b, cols):
                for m in range(4 * half, 4 * half + 4):
                    last = pe.matmul(dst[:, (m % 4) * TT:(m % 4 + 1) * TT],
                                     k.key_stack[odd][:, m, b, cols], k.q_diag[odd][:, m, :, :],
                                     start=True, stop=True)
                return last

            def piece(part, pair, key, batch):
                odd, name, b = key
                ring.wait_bank(pe, part, pair, key)
                nxt = 1 - odd
                at = SHARED + ring.bank(part, key)
                if name == "T":
                    pe.wait_ge(loaded, 16 * LOADS * (batch + 2))
                    for n in range(4):
                        last = pe.transpose(k.bank(at, (0, P), CH0, n * CH0), k.rows_raw[:, 4 * b + n, :],
                                            k.ident[0:CH0, 0:CH0])
                    if b == 2:
                        last = pe.transpose(k.bank(at, (0, P), DCA, SPAN0), k.rows_d[:, :],
                                            k.ident[0:DCA, 0:DCA])
                elif name[0] == "K":
                    h = int(name[1])
                    for lo, hi, dca in spans(b):
                        w = k.wkv_d if dca else k.wk
                        last = pe.matmul(k.bank(at, (0, P), hi - lo, lo), w[:, h * P:(h + 1) * P],
                                         k.ctx_t[:, b, lo:hi], start=True, stop=True)
                elif name[0] == "V":
                    last = pe.matmul(k.bank(at, (0, P), BANK), k.same_head[:, :], k.ksq[:, b, :],
                                     start=True, stop=True)
                elif name == "WD":
                    last = pe.matmul(k.bank(at, (0, DCA), D), k.ctx_t[:, 2, SPAN0:BANK],
                                     k.wkv_d[:, D:2 * D], start=True, stop=True)
                elif name[0] == "W":
                    for n in range(2):
                        cb, c = chunk_cols(6 * int(name[1]) + 2 * b + n)
                        last = pe.matmul(k.bank(at, (0, CH0), D, n * D), k.ctx_t[:, cb, c:c + CH0],
                                         k.wv[:, :], start=True, stop=True)
                elif name[0] == "M":
                    m = int(name[1])
                    pe.wait_ge(stacked[m // 4], 16 * STACKS * (batch + 2))
                    pe.wait_ge(q_ready, batch + 2)
                    n = spans(b)[-1][1]
                    last = pe.matmul(k.bank(at, (0, TT), n), k.q_diag[nxt][0:PARTS, m, :, :],
                                     k.key_stack[nxt][0:PARTS, m, b, 0:n], start=True, stop=True)
                elif name == "R":
                    pe.wait_ge(shift_done, batch + 2)
                    for m in range(4 * b, 4 * b + 4):
                        last = pe.matmul(k.bank(at, (PARTS, PARTS + 2), TT, (m % 4) * TT),
                                         k.shift_col[:, :, m], k.ident_bf[0:TT, 0:TT], start=True, stop=True)
                elif name == "SD":
                    last = scored(k.bank(at, (0, DCA), HALF), b, odd, 2, slice(SPAN0, BANK))
                elif name == "PD":
                    pe.wait_ge(free_a, ring.was_read(part, pair, (odd, "SD", 1)))
                    last = weighted(at, k.values_d[odd], k.probs_d, DCA, True, True)
                elif name in ("OT", "ODT"):
                    src = k.sums_t if name == "OT" else k.sums_dt
                    if name == "OT":
                        pe.wait_ge(o_read, batch)
                    else:
                        pe.wait_ge(free_v, ring.was_read(part, pair, (odd, "PD", 0)))
                    for n in range(HPAIRS // 2):
                        last = pe.transpose(k.bank(at, (0, TT), PSPAN, n * P), src[0:PSPAN, n * TT:(n + 1) * TT],
                                            k.ident[0:PSPAN, 0:PSPAN])
                elif name == "C":
                    pe.wait_ge(att_ready, batch)
                    last = pe.transpose(k.bank(at, (0, P), TT), k.att[:, :, :].rearrange("p m d -> p (m d)"),
                                        k.ident[0:TT, 0:TT])
                else:
                    pe.wait_ge(free_a, ring.was_read(part, pair, (odd, "C", 0)))
                    for e in range(2):
                        last = pe.matmul(k.bank(at, (0, TT), D), k.att_t[:, e, :, :], k.wo_par[:, e, :],
                                         start=(e == 0), stop=(e == 1))
                last.then_inc(full, 1)

            def unit(part, pair, odd, name, batch):
                if name[0] == "K":
                    pe.wait_ge(free_a, ring.was_read(part, pair, (odd, "T", 2)))
                if name[0] == "V":
                    pe.wait_ge(free_a, ring.was_read(part, pair, (odd, "K" + name[1], 2)))
                for b in range(pieces0(name)[0]):
                    piece(part, pair, (odd, name, b), batch)

            def scores(part, batch, odd, j):
                if j == 0:
                    pe.wait_ge(row_ready, batch + 1)
                if not (part == "first" and odd == 0 and j < 2):
                    pe.wait_ge(exp_done, CHUNKS * batch + j - 1)
                b, c = chunk_cols(j)
                for half in range(2):
                    last = scored(scores_bank(j, (0, CH0))[:, half, :], half, odd, b, slice(c, c + CH0))
                last.then_inc(s_full, 1)

            def values(batch, odd, j):
                pe.wait_ge(exp_done, CHUNKS * batch + j + 1)
                if j == 0:
                    pe.wait_ge(dup_rows, batch + 1)
                    at_least(pe, o_read, batch)
                weighted(O, k.values[odd][:, j, :], k.probs[j % 2], CH0, j == 0, j == CHUNKS - 1
                         ).then_inc(pv_done, 1)

            def body(part, pair):
                for odd in range(2):
                    batch = 2 * pair + odd
                    for j in range(CHUNKS):
                        scores(part, batch, odd, j)
                        before, after = SLOTS0[j]
                        for name in before:
                            if runs0(part, odd, name):
                                unit(part, pair, odd, name, batch)
                        if j > 0:
                            values(batch, odd, j - 1)
                        elif not (part == "first" and odd == 0):
                            values(batch - 1, 1 - odd, CHUNKS - 1)
                        for name in after:
                            if runs0(part, odd, name):
                                unit(part, pair, odd, name, batch)

            pe.wait_ge(consts, CONSTS)
            for name in PREP0:
                unit("pro", 0, 1, name, -1)
            pair_loop(pe, body)
            values(BATCH - 1, 1, CHUNKS - 1)
            for name in ("OT", "C", "Y"):
                unit("epi", PAIRS, 0, name, BATCH)

        def read_values(copy, name, b, nxt, at):
            if name == "WD":
                dst, src = k.values_d[nxt][:, :], k.bank(at, (0, DCA), D)
                return copy(dst.rearrange("p (h s) -> p h s", s=VW)[:, :, 0:HD0],
                            src.rearrange("p (h d) -> p h d", d=HD0))
            j = 6 * int(name[1]) + 2 * b
            dst, src = k.values[nxt][:, j:j + 2, :], k.bank(at, (0, CH0), 2 * D)
            return copy(dst.rearrange("p j (h s) -> p (j h) s", s=VW)[:, :, 0:HD0],
                        src.rearrange("p (g d) -> p g d", d=HD0))

        @block.scalar
        def _(a):
            def unit(part, pair, odd, name, batch):
                for b in range(pieces0(name)[0]):
                    key = (odd, name, b)
                    at = SHARED + ring.bank(part, key)
                    ring.wait_full(a, part, pair, key)
                    if name == "T":
                        n = spans(b)[-1][1]
                        last = a.activation(k.ctx_t[:, b, 0:n], k.bank(at, (0, P), n), ACT.Identity)
                    elif name[0] == "K":
                        h = int(name[1])
                        for dst, f in ((k.kc[:, h, b, :], ACT.Identity), (k.ksq[:, b, :], ACT.Square)):
                            for lo, hi, dca in spans(b):
                                c = (4 if dca else 2) + h
                                last = a.activation(dst[:, lo:hi], k.bank(at, (0, P), hi - lo, lo), f,
                                                    bias=k.bias_c[:, c:c + 1])
                    elif name[0] == "V":
                        if b == 0:
                            at_least(a, khat, 2 * (batch + 1) + int(name[1]))
                        last = a.activation(k.krs[:, b, :], k.bank(at, (0, P), BANK), ACT.Ln,
                                            bias=k.eps_qk[:, 0:1])
                    elif name[0] == "W":
                        last = read_values(lambda o, s: a.activation(o, s, ACT.Identity), name, b, 1 - odd, at)
                    elif name == "SD":
                        last = a.activation(k.probs_d[:, b, :], k.bank(at, (0, DCA), HALF), ACT.Exp, scale=SCALE0 / (UP * UP))
                    elif name == "C":
                        last = a.activation(k.att_t[:, :, 1 - odd, :],
                                            k.bank(at, (0, P), TT).rearrange("p (e q) -> p e q", q=SEQ),
                                            ACT.Identity)
                    last.then_inc(free_a, 1)
                if name[0] == "V":
                    a.wait_ge(free_a, ring.was_read(part, pair, (odd, name, 2)))
                    a.activation(k.krs[:, :, :], k.krs[:, :, :], ACT.Exp, scale=-0.5).then_inc(rstd, 1)

            def body(part, pair):
                for odd in range(2):
                    batch = 2 * pair + odd
                    for j in range(CHUNKS):
                        n = CHUNKS * batch + j
                        a.wait_ge(s_full, n + 1)
                        if not (part == "first" and odd == 0 and j < 2):
                            a.wait_ge(pv_done, n - 1)
                        a.activation(k.probs[j % 2][0:CH0, :, :], scores_bank(j, (0, CH0)), ACT.Exp,
                                     scale=SCALE0 / (UP * UP)).then_inc(exp_done, 1)
                        for side in SLOTS0[j]:
                            for name in side:
                                if pieces0(name)[1] == "a" and runs0(part, odd, name):
                                    unit(part, pair, odd, name, batch)

            a.preload_act_table_set("natural_log_exp_and_others")
            a.wait_ge(consts, CONSTS)
            for name in PREP0:
                if pieces0(name)[1] == "a":
                    unit("pro", 0, 1, name, -1)
            pair_loop(a, body)
            unit("epi", PAIRS, 0, "C", BATCH)

        @block.vector
        def _(v):
            def copy_sums(dst, bank):
                for at in (0, 64):
                    last = v.tensor_copy(dst[at:at + PW, :], k.bank(bank, (at, at + PW), HALF))
                return last

            def read_sums(batch):
                v.wait_ge(pv_done, CHUNKS * batch + CHUNKS)
                copy_sums(k.sums_t, O).then_inc(o_read, 1)

            def divided(at, read, count, own, rsum, rpar, parts):
                tiles = k.bank(at, (0, TT), BANK).rearrange("p (m c) -> p m c", c=64)[:, :, 0:PW].rearrange(
                    "p m (e s) -> p m e s", s=VW)
                v.reciprocal(rsum[:, :, :], tiles[:, :, :, HD0]).then_inc(own, 1)
                v.wait_ge(own, 3 * count + 1)
                v.tensor_tensor(rpar[:, :, :], rsum[:, :, :],
                                k.col_parity[:, :].unsqueeze(1).to_broadcast([TT, HPAIRS, 2]), ALU.mult
                                ).then_inc(own, 1)
                v.wait_ge(own, 3 * count + 2)
                v.tensor_tensor(parts[:, :, :, :], tiles[:, :, :, 0:HD0],
                                rpar[:, :, :].unsqueeze(3).to_broadcast([TT, HPAIRS, 2, HD0]), ALU.mult
                                ).then_inc(free_v, 1)
                v.wait_ge(free_v, read)

            def normalise_keys(nb, h):
                v.wait_ge(rstd, 2 * nb + h + 1)
                v.tensor_tensor(k.kc[:, h, :, :], k.kc[:, h, :, :], k.krs[:, :, :], ALU.mult
                                ).then_inc(khat, 1)
                v.wait_ge(khat, 2 * nb + h + 1)
                v.tensor_scalar(k.kc[:, h, :, 0:SPAN0], k.kc[:, h, :, 0:SPAN0],
                                k.lnwb[:, 2:3], k.lnwb[:, 3:4], ALU.mult, ALU.add)
                v.tensor_scalar(k.kc[:, h, 2, SPAN0:BANK], k.kc[:, h, 2, SPAN0:BANK],
                                k.lnwb[:, 4:5], k.lnwb[:, 5:6], ALU.mult, ALU.add).then_inc(keys_fin, 1)

                v.wait_ge(keys_fin, 2 * nb + h + 1)
                v.tensor_copy(k.key_hi[:, h, :, :], k.kc[:, h, :, :]).then_inc(hi_done, 1)
                v.wait_ge(hi_done, 2 * nb + h + 1)
                v.tensor_tensor(k.key_lo[:, h, :, :], k.kc[:, h, :, :], k.key_hi[:, h, :, :], ALU.subtract
                                ).then_inc(lo_done, 1)

            def unit(part, pair, odd, name, batch):
                for b in range(pieces0(name)[0]):
                    piece(part, pair, odd, name, b, batch)
                if name == f"M{HPAIRS - 1}":
                    v.wait_ge(free_v, ring.was_read(part, pair, (odd, name, 2)))
                    v.tensor_reduce(k.shift_col[:, 0, :], k.maxima[:, :, 0:3], AX.X, ALU.max, negate=True)
                    v.tensor_reduce(k.shift_col[:, 1, :], k.maxima[:, :, 3:4], AX.X, ALU.max, negate=True
                                    ).then_inc(shift_done, 1)
                elif name == "R":
                    v.wait_ge(free_v, ring.was_read(part, pair, (odd, "R", 1))).then_inc(row_ready, 1)

            def piece(part, pair, odd, name, b, batch):
                key = (odd, name, b)
                at, read = SHARED + ring.bank(part, key), ring.was_read(part, pair, key)
                ring.wait_full(v, part, pair, key)
                if name == "PD":
                    last = copy_sums(k.sums_dt, at)
                elif name == "ODT":
                    divided(at, read, batch, rsd_own, k.rsum_d, k.rpar_d, k.parts_d)
                    v.tensor_tensor(k.att_d[:, :, :], k.parts_d[:, :, 0, :], k.parts_d[:, :, 1, :], ALU.add
                                    ).then_inc(rsd_own, 1)
                    return
                elif name == "OT":
                    prev = batch - 1
                    at_least(v, att_ready, prev)
                    divided(at, read, prev, rs_own, k.rsum, k.rpar, k.parts)
                    v.wait_ge(rsd_own, 3 * prev + 3)
                    v.tensor_tensor(k.att_half[:, :, :], k.parts[:, :, 0, :], k.att_d[:, :, :], ALU.add
                                    ).then_inc(rs_own, 1)
                    v.wait_ge(rs_own, 3 * prev + 3)
                    v.tensor_tensor(k.att[:, :, :], k.parts[:, :, 1, :], k.att_half[:, :, :], ALU.add
                                    ).then_inc(att_ready, 1)
                    return
                elif name[0] == "M":
                    m = int(name[1])
                    for lo, hi, dca in spans(b):
                        c = 3 if dca else b
                        last = v.tensor_reduce(k.maxima[:, m, c:c + 1], k.bank(at, (0, TT), hi - lo, lo),
                                               AX.X, ALU.max)
                elif name == "R":
                    last = v.tensor_scalar(
                        k.q_diag[1 - odd][PARTS:PARTS + 2, 4 * b:4 * b + 4, :, :].rearrange(
                            "p m e q -> p (m e q)"), k.bank(at, (PARTS, PARTS + 2), HALF),
                        1.0 / (UP * UP), None, ALU.mult)
                elif name == "Y":
                    v.tensor_tensor(k.ytmp[:, :], k.bank(at, (0, TT), D), k.bo_b[:, :], ALU.add
                                    ).then_inc(free_v, 1)
                    v.wait_ge(free_v, read)
                    row = k.resid[:, bass.ds(pair - 1, 1), :].rearrange("p o d -> p (o d)")
                    v.scalar_tensor_tensor(out=row, in0=k.ytmp[:, :], scalar=k.gates[0:TT, 0:1],
                                           in1=row, op0=ALU.mult, op1=ALU.add).then_inc(resid_done, 1)
                    return
                last.then_inc(free_v, 1)

            def body(part, pair):
                for odd in range(2):
                    batch = 2 * pair + odd
                    if not (part == "first" and odd == 0):
                        read_sums(batch - 1)
                    for j in range(CHUNKS):
                        for side in SLOTS0[j]:
                            for name in side:
                                if pieces0(name)[1] == "v":
                                    if runs0(part, odd, name):
                                        unit(part, pair, odd, name, batch)
                        if not (part == "last" and odd):
                            if j in (3, 5):
                                normalise_keys(batch + 1, (j - 3) // 2)

            v.memset(k.sums_t[32:64, :], 0.0).then_inc(consts, 1)
            v.memset(k.sums_dt[32:64, :], 0.0).then_inc(consts, 1)
            v.wait_ge(consts, CONSTS)
            for h in range(2):
                normalise_keys(0, h)
            for name in PREP0:
                if pieces0(name)[1] == "v":
                    unit("pro", 0, 1, name, -1)
            pair_loop(v, body)
            read_sums(BATCH - 1)
            for name in ("OT", "Y"):
                unit("epi", PAIRS, 0, name, BATCH)
            v.wait_ge(resid_done, PAIRS)

        @block.gpsimd
        def _(g):
            g.memset(k.kc[:, :, 0:2, SPAN0:BANK], 0.0).then_inc(consts, 1)
            g.memset(k.ksq[:, 0:2, SPAN0:BANK], 0.0).then_inc(consts, 1)
            for n in range(2):
                g.memset(k.values[n][:, :, :].rearrange("p j (h s) -> p (j h) s", s=VW)[:, :, HD0:VW], 1.0
                         ).then_inc(consts, 1)
                g.memset(k.values_d[n][:, :].rearrange("p (h s) -> p h s", s=VW)[:, :, HD0:VW], 1.0
                         ).then_inc(consts, 1)
            g.wait_ge(consts, CONSTS)

            def values_read(part, pair, odd):
                return [ring.was_read(part, pair, (odd, *key)) for key in (("W0", 2), ("WD", 0), ("W1", 2))]

            def prepare(nb, nxt, used, values_read):
                if not (isinstance(nb, int) and nb == 0):
                    g.wait_ge(s_full, used + 1)
                g.tensor_tensor(
                    k.q_diag[nxt][0:PARTS, :, :, :],
                    k.q_stack[:, :, bass.ds(nb * SEQ, SEQ)].unsqueeze(2).to_broadcast([PARTS, HPAIRS, 2, SEQ]),
                    k.row_parity[:, :].unsqueeze(1).unsqueeze(3).to_broadcast([PARTS, HPAIRS, 2, SEQ]),
                    ALU.mult).then_inc(q_ready, 1)
                for count in values_read:
                    wait_alone(k, g, free_a, count)
                g.memset(k.values[nxt][0:DUP0, 4:12:4, :], 0.0).then_inc(dup_rows, 1)

            def body(part, pair):
                for odd in range(2):
                    batch = 2 * pair + odd
                    if not (part == "last" and odd):
                        prepare(batch + 1, 1 - odd, CHUNKS * batch, values_read(part, pair, odd))

            prepare(0, 0, 0, values_read("pro", 0, 1))
            pair_loop(g, body)



INNER = 704
IC = 6
ITAIL = INNER - 5 * P
IPAD = IC * P
IHALF = INNER // 2
FP8_MAX = 448.0
EXP_BITS = 0x7F800000
FP8_LEAST = 2.0 ** -6
FP8_MAGIC = 1.5 * 2.0 ** 20


def ffn_memory(k, s):
    sb = lambda name, shape, dt=F32: k.sbuf(s, name, shape, dt)
    k.up_row_i = sb("up_row_i", [1, D], I32)
    k.down_row_i = sb("down_row_i", [1, INNER], I32)
    k.up_row = sb("up_row", [1, D])
    k.down_row = sb("down_row", [1, INNER])
    k.down_col = sb("down_col", [P, IC], I32)
    k.ones = sb("ones", [P, P])
    k.feature_i = sb("feature_i", [P, IC], I32)
    k.feature = sb("feature", [P, IC])
    k.up_count = sb("up_count", [P, DK])
    k.down_count = sb("down_count", [P, IC])
    k.diag = sb("diag", [P, 2, P])
    k.up_mask = sb("up_mask", [P, D])
    k.down_mask = sb("down_mask", [P, IPAD])
    k.amax_w = sb("amax_w", [P, 2 * IC + DK])
    k.inv_w = sb("inv_w", [P, 2 * IC + DK])
    k.gate_scale = sb("gate_scale", [TT, IPAD])
    k.up_scale = sb("up_scale", [TT, IPAD])
    k.down_scale = sb("down_scale", [TT, D])
    k.qg_t = sb("qg_t", [P, DK, INNER], BF16)
    k.qu_t = sb("qu_t", [P, DK, INNER], BF16)
    k.qd_t = sb("qd_t", [P, IC, D], BF16)
    k.amax_x = sb("amax_x", [TT, NT])
    k.inv_x = sb("inv_x", [TT, NT])
    k.scale_x = sb("scale_x", [TT, NT])
    k.amax_t = sb("amax_t", [TT, NT])
    k.inv_t = sb("inv_t", [TT, NT])
    k.scale_t = sb("scale_t", [TT, NT])
    k.qx_t = sb("qx_t", [P, DK, TOK], BF16)
    with ExitStack() as prep:
        k.wg = k.sbuf(prep, "wg", [P, IC, D])
        k.wu = k.sbuf(prep, "wu", [P, IC, D])
        k.wd = k.sbuf(prep, "wd", [P, DK, INNER])
        k.wtmp = k.sbuf(prep, "wtmp", [P, IC * D])
        k.equal = k.sbuf(prep, "equal", [P, INNER])
        k.idx_b = k.sbuf(prep, "idx_b", [P, INNER])
        k.qg = k.sbuf(prep, "qg", [P, IC, D], BF16)
        k.qu = k.sbuf(prep, "qu", [P, IC, D], BF16)
        k.qd = k.sbuf(prep, "qd", [P, DK, IPAD], BF16)
        k.xs = k.sbuf(prep, "xs", [TT, NT, D])
        k.xm = k.sbuf(prep, "xm", [TT, NT, D])
        k.qx = k.sbuf(prep, "qx", [TT, NT, D], BF16)
    k.gate = sb("gate", [TT, NT, INNER])
    k.hidden = sb("hidden", [TT, NT, INNER])
    k.q_hidden = sb("q_hidden", [TT, 2, IPAD], BF16)
    k.qh_t = sb("qh_t", [P, 2, IC, TT], BF16)
    k.down_tmp = sb("down_tmp", [TT, 2, D])


def round_fp8(v, chain, value, magic, out):
    chain.mark(v.tensor_scalar(magic.bitcast(U32), value.bitcast(U32), EXP_BITS, None, ALU.bitwise_and))
    chain.settle()
    chain.mark(v.tensor_scalar(magic, magic, FP8_LEAST, FP8_MAGIC, ALU.max, ALU.mult))
    chain.settle()
    chain.mark(v.tensor_tensor(value, value, magic, ALU.add))
    chain.settle()
    return v.tensor_tensor(out, value, magic, ALU.subtract)


def ffn_prepare(k):
    nc, i = k.nc, k.i
    norm = k.norm.start()
    (ld, gathered, consts, own_p, casts, vec, counted, spread, wq_done, turned, turned_read, tok_read,
     x_done, scales, ld_w) = k.sems(*("f0_" + n for n in (
         "ld", "gathered", "consts", "own_p", "casts", "vec", "counted", "spread", "wq_done",
         "turned", "turned_read", "tok_read", "x_done", "scales", "ld_w")))

    def chunk(c):
        return P if c < IC - 1 else ITAIL

    with nc.Block() as block:
        @block.sync
        def _(sp):
            one = lambda v: v.rearrange("(o d) -> o d", o=1)
            up, down = i["L0_ffn_up_reorder_index"], i["L0_ffn_down_reorder_index"]
            sp.dma_start(k.down_col[:, 0:IC - 1], down[0:5 * P].rearrange("(c p) -> p c", p=P),
                         allow_slow_non_contiguous=True).then_inc(ld, 16)
            sp.dma_start(k.down_col[0:ITAIL, IC - 1:IC], down[5 * P:INNER].rearrange("(p o) -> p o", o=1)
                         ).then_inc(ld, 16)
            sp.dma_start(k.up_row_i[:, :], one(up)).then_inc(ld, 16)
            sp.dma_start(k.down_row_i[:, :], one(down)).then_inc(ld, 16)
            sp.dma_start(k.wd[:, :, :], i["L0_ffn_w_down"].rearrange("(c p) n -> p c n", p=P)
                         ).then_inc(ld_w, 16)

        @block.gpsimd
        def _(g):
            g.memset(k.ones[:, :], 1.0).then_inc(consts, 1)
            g.iota(k.feature_i[:, :], [[P, IC]], base=0, channel_multiplier=1).then_inc(consts, 1)
            for w in (k.wg, k.wu):
                g.memset(w[:, IC - 1, :], 1.0).then_inc(own_p, 1)
            g.memset(k.qd[:, :, INNER:IPAD], 0.0).then_inc(consts, 1)
            g.wait_ge(ld, 64)
            g.wait_ge(own_p, 2)
            for w, name in ((k.wg, "L0_ffn_w_gate"), (k.wu, "L0_ffn_w_up")):
                for c in range(IC):
                    n = chunk(c)
                    g.indirect_dma_start(w[0:n, c, :], None, i[name], bass.IndirectOffsetOnAxis(
                        ap=k.down_col[0:n, c:c + 1], axis=0)).then_inc(gathered, 16)
            g.wait_ge(gathered, 16 * 2 * IC)

        @block.tensor
        def _(pe):
            pe.wait_ge(casts, 3)
            pe.matmul(k.bank(0, (0, P), D), k.ones_row[:, :], k.up_row[:, :], start=True, stop=True)
            for h in range(2):
                last = pe.matmul(k.bank(1 + h, (0, P), IHALF), k.ones_row[:, :],
                                 k.down_row[:, h * IHALF:(h + 1) * IHALF], start=True, stop=True)
            last.then_inc(spread, 1)
            pe.wait_ge(consts, 3)
            n = 0
            for _name, count, _dst in spreads(k):
                for c in range(count):
                    pe.wait_ge(scales, n + 1)
                    pe.matmul(spread_bank(k, _name, c), k.ones[:, :], k.diag[:, n % 2, :],
                              start=True, stop=True).then_inc(counted, 1)
                    n += 1
            norm.tensor(pe)
            n = 0
            for src, outer, inner in ((k.qg, IC, DK), (k.qu, IC, DK), (k.qd, DK, IC)):
                pe.wait_ge(wq_done, (k.qg, k.qu, k.qd).index(src) + 1)
                for c in range(inner):
                    if n >= 2:
                        pe.wait_ge(turned_read, n - 1)
                    for o in range(outer):
                        rows = chunk(o) if outer == IC else P
                        last = pe.transpose(turn_bank(k, n)[:, o * P:o * P + rows],
                                            src[0:rows, o, c * P:(c + 1) * P], k.ident_bf[0:rows, 0:rows])
                    last.then_inc(turned, 1)
                    n += 1
            for q in range(NT // 4):
                pe.wait_ge(x_done, q + 1)
                for c in range(DK):
                    pe.wait_ge(turned_read, 2 * DK + IC)
                    at_least(pe, tok_read, n - (2 * DK + IC) - 1)
                    for t in range(4):
                        last = pe.transpose(turn_bank(k, n)[:, t * TT:(t + 1) * TT],
                                            k.qx[:, 4 * q + t, c * P:(c + 1) * P], k.ident_bf[0:TT, 0:TT])
                    last.then_inc(turned, 1)
                    n += 1

        @block.scalar
        def _(a):
            norm.scalar(a)
            norm.copy_scalar(a)
            n = 2 * DK + IC
            for q in range(NT // 4):
                for c in range(DK):
                    a.wait_ge(turned, n + 1)
                    a.activation(k.qx_t[:, c, q * 4 * TT:(q + 1) * 4 * TT], turn_bank(k, n)[:, 0:4 * TT],
                                 ACT.Identity).then_inc(tok_read, 1)
                    n += 1

        @block.vector
        def _(v):
            chain = Chain(v, vec)
            v.wait_ge(ld, 64)
            v.wait_ge(consts, 3)
            v.tensor_copy(k.up_row[:, :], k.up_row_i[:, :]).then_inc(casts, 1)
            v.tensor_copy(k.down_row[:, :], k.down_row_i[:, :]).then_inc(casts, 1)
            v.tensor_copy(k.feature[:, :], k.feature_i[:, :]).then_inc(casts, 1)
            v.wait_ge(casts, 3)
            v.wait_ge(spread, 1)
            for size, pieces, count in ((D, DK, k.up_count), (INNER, IC, k.down_count)):
                if size == D:
                    src = k.bank(0, (0, P), D)
                    chain.mark(v.tensor_copy(k.idx_b[:, 0:D], src))
                else:
                    for h in range(2):
                        chain.mark(v.tensor_copy(k.idx_b[:, h * IHALF:(h + 1) * IHALF],
                                                 k.bank(1 + h, (0, P), IHALF)))
                chain.settle()
                for c in range(pieces):
                    chain.mark(v.tensor_scalar(k.equal[:, 0:size], k.idx_b[:, 0:size],
                                               k.feature[:, c:c + 1], None, ALU.is_equal))
                    chain.settle()
                    chain.mark(v.tensor_reduce(count[:, c:c + 1], k.equal[:, 0:size], AX.X, ALU.add))
                    chain.settle()
            n = 0

            def spread_column(name, column, pieces, dst, rows):
                nonlocal n
                for c in range(pieces):
                    if n >= 2:
                        v.wait_ge(counted, n - 1)
                    v.tensor_scalar(k.diag[:, n % 2, :], k.ident[:, :], column[:, c:c + 1], None,
                                    ALU.mult).then_inc(scales, 1)
                    n += 1
                v.wait_ge(counted, n)
                chain.mark(v.tensor_copy(dst[:, 0:pieces * P],
                                         spread_bank(k, name, 0, pieces * P)[0:rows, :]))
                chain.settle()

            spread_column("up_count", k.up_count, DK, k.up_mask, P)
            chain.mark(v.tensor_scalar(k.up_mask[:, :], k.up_mask[:, :], 1.0, None, ALU.min))
            chain.settle()
            spread_column("down_count", k.down_count, IC, k.down_mask, P)
            chain.mark(v.tensor_scalar(k.down_mask[:, :], k.down_mask[:, :], 1.0, None, ALU.min))
            chain.settle()
            v.wait_ge(gathered, 16 * 2 * IC)
            v.wait_ge(ld_w, 16)
            for m, (w, q, mask, pieces, size, at) in enumerate((
                    (k.wg, k.qg, k.up_mask, IC, D, 0), (k.wu, k.qu, k.up_mask, IC, D, IC),
                    (k.wd, k.qd, k.down_mask, DK, INNER, 2 * IC))):
                tmp = k.wtmp[:, 0:pieces * size].rearrange("p (c n) -> p c n", n=size)
                mb = mask[:, 0:size].unsqueeze(1).to_broadcast([P, pieces, size])
                at_least(v, wq_done, m)
                chain.mark(v.tensor_tensor(tmp, w[:, :, :], mb, ALU.mult))
                chain.settle()
                chain.mark(v.tensor_reduce(k.amax_w[:, at:at + pieces], tmp, AX.X, ALU.max,
                                           apply_absolute_value=True))
                chain.settle()
                chain.mark(v.reciprocal(k.inv_w[:, at:at + pieces], k.amax_w[:, at:at + pieces]))
                chain.mark(v.tensor_scalar(k.amax_w[:, at:at + pieces], k.amax_w[:, at:at + pieces],
                                           1.0 / FP8_MAX, None, ALU.mult))
                chain.settle()
                for c in range(pieces):
                    chain.mark(v.tensor_scalar(w[:, c, :], w[:, c, :], k.inv_w[:, at + c:at + c + 1],
                                               FP8_MAX, ALU.mult, ALU.mult))
                chain.settle()
                round_fp8(v, chain, w[:, :, :], tmp, q[:, :, 0:size]).then_inc(wq_done, 1)
            v.wait_ge(wq_done, 3)
            spread_column("gate_scale", k.amax_w[:, 0:IC], IC, k.gate_scale, TT)
            spread_column("up_scale", k.amax_w[:, IC:2 * IC], IC, k.up_scale, TT)
            chain.mark(v.tensor_tensor(k.up_scale[:, :], k.up_scale[:, :], k.down_mask[0:TT, :], ALU.mult))
            spread_column("down_scale", k.amax_w[:, 2 * IC:], DK, k.down_scale, TT)
            chain.mark(v.tensor_scalar(k.down_scale[:, :], k.down_scale[:, :], k.gates[0:TT, 2:3], None,
                                       ALU.mult))
            norm.vector(v, chain)
            norm.copy_vector(v)
            norm.wait_tiles(v, NT)
            m = 0
            for dst, counts, pieces, width in ((k.qg_t, k.up_count, DK, INNER), (k.qu_t, k.up_count, DK, INNER),
                                               (k.qd_t, k.down_count, IC, D)):
                for c in range(pieces):
                    v.wait_ge(turned, m + 1)
                    v.tensor_scalar(dst[:, c, :], turn_bank(k, m)[:, 0:width], counts[:, c:c + 1], None,
                                    ALU.mult).then_inc(turned_read, 1)
                    m += 1
            for q in range(NT // 4):
                ts = slice(4 * q, 4 * q + 4)
                mb = k.up_mask[0:TT, :].unsqueeze(1).to_broadcast([TT, 4, D])
                chain.mark(v.tensor_tensor(k.xm[:, ts, :], k.normed[:, ts, :], mb, ALU.mult))
                chain.settle()
                chain.mark(v.tensor_reduce(k.amax_x[:, ts], k.xm[:, ts, :], AX.X, ALU.max,
                                           apply_absolute_value=True))
                chain.settle()
                chain.mark(v.reciprocal(k.inv_x[:, ts], k.amax_x[:, ts]))
                chain.mark(v.tensor_scalar(k.scale_x[:, ts], k.amax_x[:, ts], 1.0 / FP8_MAX, None, ALU.mult))
                chain.settle()
                for t in range(4 * q, 4 * q + 4):
                    chain.mark(v.tensor_scalar(k.xs[:, t, :], k.normed[:, t, :], k.inv_x[:, t:t + 1], FP8_MAX,
                                               ALU.mult, ALU.mult))
                chain.settle()
                round_fp8(v, chain, k.xs[:, ts, :], k.xm[:, ts, :], k.qx[:, ts, :]).then_inc(x_done, 1)
            v.wait_ge(x_done, 4)


def spreads(k):
    return (("up_count", DK, None), ("down_count", IC, None), ("gate_scale", IC, None),
            ("up_scale", IC, None), ("down_scale", DK, None))


def spread_bank(k, name, c, cols=P):
    n = [s[0] for s in spreads(k)].index(name)
    return k.bank(3 + 2 * (n % 2), (0, P), cols, c * P)


def turn_bank(k, n):
    return k.bank(n % 2 + 6, (0, P), BANK).bitcast(BF16)


def ffn_run(k):
    nc = k.nc
    (g_full, u_full, g_read, u_read, silu_done, hid_done, amax_done, scaled, rounding, rounded, turned,
     turned_read, y_full, y_read, resid_done, vec, consts) = k.sems(*("f1_" + n for n in (
         "g_full", "u_full", "g_read", "u_read", "silu_done", "hid_done", "amax_done", "scaled", "rounding",
         "rounded", "turned", "turned_read", "y_full", "y_read", "resid_done", "vec", "consts")))
    HALVES = NT // 2

    def gu_banks(which):
        return k.banks(2 * which, 2, (0, TT), IHALF)

    def halves(ap):
        return ap.rearrange("p (h n) -> p h n", n=IHALF)

    def tile(ap, t):
        return ap[:, bass.ds(t, 1), :].rearrange("p o n -> p (o n)")

    def turned_bank(par):
        return k.bank(4 + par, (0, P), BANK).bitcast(BF16)

    with nc.Block() as block:
        @block.tensor
        def _(pe):
            with pe.Fori(0, NT) as t:
                for which, w, read, full in ((0, k.qg_t, g_read, g_full), (1, k.qu_t, u_read, u_full)):
                    pe.wait_ge(read, t + 1)
                    for h in range(2):
                        for c in range(DK):
                            last = pe.matmul(gu_banks(which)[:, h, :], k.qx_t[:, c, bass.ds(t * TT, TT)],
                                             w[:, c, h * IHALF:(h + 1) * IHALF],
                                             start=(c == 0), stop=(c == DK - 1))
                    last.then_inc(full, 1)

            def turn(t, par):
                pe.wait_ge(rounded, t + 1)
                pe.wait_ge(turned_read, t + 1)
                for c in range(IC):
                    last = pe.transpose(turned_bank(par)[:, c * TT:(c + 1) * TT],
                                        k.q_hidden[:, par, c * P:(c + 1) * P], k.ident_bf[0:TT, 0:TT])
                last.then_inc(turned, 1)

            def down(t, par):
                pe.wait_ge(turned_read, t + 3)
                pe.wait_ge(y_read, t + 1)
                for c in range(IC):
                    last = pe.matmul(k.bank(6 + par, (0, TT), D), k.qh_t[:, par, c, :], k.qd_t[:, c, :],
                                     start=(c == 0), stop=(c == IC - 1))
                last.then_inc(y_full, 1)

            turn(0, 0)
            with pe.Fori(0, HALVES - 1) as u:
                for par in range(2):
                    turn(2 * u + par + 1, 1 - par)
                    down(2 * u + par, par)
            turn(NT - 1, 1)
            down(NT - 2, 0)
            down(NT - 1, 1)

        @block.vector
        def _(v):
            v.engine_nop().then_inc(g_read, 1)
            v.engine_nop().then_inc(u_read, 1)
            for _n in range(2):
                v.engine_nop().then_inc(y_read, 1)
            with v.Fori(0, NT) as t:
                for which, src, dst, full, read in ((0, k.gate_scale, k.gate, g_full, g_read),
                                                    (1, k.up_scale, k.hidden, u_full, u_read)):
                    v.wait_ge(full, t + 1)
                    v.scalar_tensor_tensor(out=halves(tile(dst, t)), in0=gu_banks(which),
                                           scalar=k.scale_x[:, bass.ds(t, 1)], in1=halves(src[:, 0:INNER]),
                                           op0=ALU.mult, op1=ALU.mult).then_inc(read, 1)
            chain = Chain(v, vec)

            def find_scales(q):
                ts = slice(4 * q, 4 * q + 4)
                v.wait_ge(hid_done, 4 * q + 4)
                chain.mark(v.tensor_reduce(k.amax_t[:, ts], k.hidden[:, ts, :], AX.X, ALU.max,
                                           apply_absolute_value=True))
                chain.settle()
                chain.mark(v.reciprocal(k.inv_t[:, ts], k.amax_t[:, ts]))
                chain.mark(v.tensor_scalar(k.scale_t[:, ts], k.amax_t[:, ts], 1.0 / FP8_MAX, None, ALU.mult))
                chain.settle()
                v.tensor_scalar(k.inv_t[:, ts], k.inv_t[:, ts], FP8_MAX, None, ALU.mult).then_inc(amax_done, 1)

            def round_tiles(q):
                ts = slice(4 * q, 4 * q + 4)
                v.wait_ge(scaled, 4 * q + 4)
                value, magic = k.hidden[:, ts, :], k.gate[:, ts, :]
                chain.mark(v.tensor_scalar(magic.bitcast(U32), value.bitcast(U32), EXP_BITS, None,
                                           ALU.bitwise_and))
                chain.settle()
                chain.mark(v.tensor_scalar(magic, magic, FP8_LEAST, FP8_MAGIC, ALU.max, ALU.mult))
                chain.settle()
                v.tensor_tensor(value, value, magic, ALU.add).then_inc(rounding, 1)

            def add_tiles(q):
                with v.Fori(2 * q, 2 * q + 2) as u:
                    for par in range(2):
                        t = 2 * u + par
                        v.wait_ge(y_full, t + 1)
                        v.scalar_tensor_tensor(out=k.down_tmp[:, par, :], in0=k.bank(6 + par, (0, TT), D),
                                               scalar=k.scale_t[:, bass.ds(t, 1)], in1=k.down_scale[:, :],
                                               op0=ALU.mult, op1=ALU.mult).then_inc(y_read, 1)
                        v.wait_ge(y_read, t + 3)
                        v.tensor_tensor(tile(k.resid, t), tile(k.resid, t), k.down_tmp[:, par, :], ALU.add
                                        ).then_inc(resid_done, 1)

            find_scales(0)
            for q in range(NT // 4):
                if q + 1 < NT // 4:
                    find_scales(q + 1)
                round_tiles(q)
                if q >= 1:
                    add_tiles(q - 1)
            add_tiles(NT // 4 - 1)
            v.wait_ge(resid_done, NT)

        @block.scalar
        def _(a):
            for _n in range(2):
                a.nop().then_inc(turned_read, 1)
            a.preload_act_table_set("silu_and_others")
            with a.Fori(0, NT) as t:
                a.wait_ge(g_read, t + 2)
                a.activation(tile(k.gate, t), tile(k.gate, t), ACT.Silu).then_inc(silu_done, 1)

            def scale_tiles(q):
                a.wait_ge(amax_done, q + 1)
                for t in range(4 * q, 4 * q + 4):
                    a.activation(k.hidden[:, t, :], k.hidden[:, t, :], ACT.Identity,
                                 scale=k.inv_t[:, t:t + 1]).then_inc(scaled, 1)

            def copy_turned(q):
                with a.Fori(2 * q, 2 * q + 2) as u:
                    for par in range(2):
                        t = 2 * u + par
                        a.wait_ge(turned, t + 1)
                        a.wait_ge(y_read, t + 1)
                        a.activation(k.qh_t[:, par, :, :].rearrange("p c n -> p (c n)"),
                                     turned_bank(par)[:, 0:IC * TT], ACT.Identity).then_inc(turned_read, 1)

            scale_tiles(0)
            for q in range(NT // 4):
                if q + 1 < NT // 4:
                    scale_tiles(q + 1)
                copy_turned(q)

        @block.gpsimd
        def _(g):
            g.memset(k.q_hidden[:, :, INNER:IPAD], 0.0).then_inc(consts, 1)
            with g.Fori(0, NT) as t:
                g.wait_ge(silu_done, t + 1)
                g.wait_ge(u_read, t + 2)
                g.tensor_tensor(tile(k.hidden, t), tile(k.gate, t), tile(k.hidden, t), ALU.mult
                                ).then_inc(hid_done, 1)
            g.wait_ge(consts, 1)
            with g.Fori(0, NT // 4) as q:
                g.wait_ge(rounding, q + 1)
                for n in range(4):
                    t = 4 * q + n
                    g.wait_ge(turned_read, t + 1)
                    g.tensor_tensor(k.q_hidden[:, n % 2, 0:INNER], tile(k.hidden, t), tile(k.gate, t),
                                    ALU.subtract).then_inc(rounded, 1)



HD1 = 128
KV = 8
CH1 = KEYS // CHUNKS
SPAN1 = 4 * CH1
SCALE1 = HD1 ** -0.5
MASKED = -1e30

PREP1 = ["T", "B"] + [f"M{m}" for m in range(QT)] + ["R"]
SLOTS1 = {0: ([], []), 1: (["OT"], ["B"]), 2: (["Y"], []), 3: (["T"], []), 4: (["M0"], []),
          5: (["M1"], []), 6: (["M2"], []), 7: (["M3"], []), 8: (["M4"], []), 9: (["M5"], []),
          10: (["M6"], []), 11: (["R"], [])}
PREP1_ORDER = ["B", "T"] + PREP1[2:]


def runs1(part, odd, unit):
    if unit == "Y" and odd:
        return False
    if part == "first" and not odd and unit in ("OT", "Y"):
        return False
    return not (part == "last" and odd and unit in PREP1)


def order1(part):
    return [(odd, u) for odd in range(2) for j in range(CHUNKS) for side in SLOTS1[j] for u in side
            if runs1(part, odd, u)]


def layer1_memory(k, s):
    sb = lambda name, shape, dt=F32: k.sbuf(s, name, shape, dt)
    k.qk_w = sb("qk_w", [P, DK, HEADS, DC])
    k.vo_w = sb("vo_w", [DC, HEADS, D])
    k.mask_col8 = sb("mask_col8", [CH1, BATCH, CHUNKS], U8)
    k.mask_row8 = sb("mask_row8", [BATCH, KEYS], U8)
    k.mask_row = sb("mask_row", [BATCH, KEYS])
    k.any_col = sb("any_col", [BATCH, 1])
    k.any_diag = sb("any_diag", [BATCH, BATCH])
    k.ones_bc = sb("ones_bc", [BATCH, P])
    k.any_key = sb("any_key", [P, BATCH])
    k.mask_bias = sb("mask_bias", [CH1, BATCH, CHUNKS])
    with ExitStack() as prep:
        k.wq1 = k.sbuf(prep, "wq1", [P, DK, HEADS * HD1])
        k.wk1 = k.sbuf(prep, "wk1", [DC, KV, HD1])
        k.wv1 = k.sbuf(prep, "wv1", [DC, KV, HD1])
        k.wo1 = k.sbuf(prep, "wo1", [HD1, HEADS, D])
        k.wk1_t = k.sbuf(prep, "wk1_t", [HD1, KV, DC])
        k.wv1_t = k.sbuf(prep, "wv1_t", [HD1, KV, DC])
        k.wq1_t = k.sbuf(prep, "wq1_t", [HD1, 2, D])
        k.q_stage = [[k.sbuf(prep, f"q_stage_{x}{n}", [DC, 8, HEADS, SEQ], F16) for x in ("hi", "lo")]
                     for n in range(2)]
    k.rows1 = [sb(f"rows1_{n}", [CH1, CHUNKS, DC + 1]) for n in range(2)]
    k.ctx_hi = [sb(f"ctx_hi{n}", [DC, 3, SPAN1], F16) for n in range(2)]
    k.ctx_lo = [sb(f"ctx_lo{n}", [DC, 3, SPAN1], F16) for n in range(2)]
    k.q1_hi = [sb(f"q1_hi{n}", [DC, HQ], F16) for n in range(2)]
    k.q1_lo = [sb(f"q1_lo{n}", [DC, HQ], F16) for n in range(2)]
    k.bias_bc = sb("bias_bc", [CH1, CHUNKS, P], BF16)
    k.bias_row = sb("bias_row", [P, 3, SPAN1])
    k.masked = sb("masked", [P, 3, SPAN1], BF16)
    k.max_f = sb("max_f", [P, QT])
    k.max_col = sb("max_col", [P, QT], BF16)
    k.shift1 = [sb(f"shift1_{n}", [P, HQ]) for n in range(2)]
    k.shifted = [sb(f"shifted{n}", [CH1, 2, HALF]) for n in range(2)]
    k.rsum1 = sb("rsum1", [P, QT])
    k.rinv1 = sb("rinv1", [P, QT])


def layer1_prepare(k):
    nc, i = k.nc, k.i
    norm = k.norm.start()
    k.q1_dram = [nc.dram_tensor(f"q1_{x}_scratch", (P, BATCH, HQ), F16, kind="Internal").ap()
                 for x in ("hi", "lo")]
    (ld_w, ld_m, consts, own_p, kv_turned, kv_read, q_turned, q_read, w_full, w_read, mask_v, any_full,
     q_full, stage_a, stage_v, vec, own_a) = k.sems(*("p1_" + n for n in (
         "ld_w", "ld_m", "consts", "own_p", "kv_turned", "kv_read", "q_turned", "q_read", "w_full", "w_read",
         "mask_v", "any_full", "q_full", "stage_a", "stage_v", "vec", "own_a")))
    stored = k.sems("p1_stored0", "p1_stored1")
    GROUPS, GC = 4, 4 * TT

    with nc.Block() as block:
        @block.sync
        def _(sp):
            sp.dma_start(k.wk1[:, :, :], i["L1_xattn_Wk"].rearrange("p (g d) -> p g d", d=HD1)).then_inc(ld_w, 16)
            sp.dma_start(k.wv1[:, :, :], i["L1_xattn_Wv"].rearrange("p (g d) -> p g d", d=HD1)).then_inc(ld_w, 16)
            sp.dma_start(k.wq1[:, :, :], i["L1_xattn_Wq"].rearrange("(c p) n -> p c n", p=P)).then_inc(ld_w, 16)
            sp.dma_start(k.wo1[:, :, :], i["L1_xattn_Wo"].rearrange("(h p) n -> p h n", p=P)).then_inc(ld_w, 16)
            sp.dma_start(k.mask_row8[:, :], i["mask"]).then_inc(ld_m, 16)
            sp.dma_start(k.mask_col8[:, :, :], i["mask"].rearrange("b (p j) -> p b j", j=CHUNKS)
                         ).then_inc(ld_m, 16)
            for g in range(GROUPS):
                for x, staged in enumerate((stage_a, stage_v)):
                    sp.wait_ge(staged, HEADS * (g + 1))
                    sp.dma_start(k.q1_dram[x][:, 8 * g:8 * g + 8, :],
                                 k.q_stage[g % 2][x][:, :, :, :].rearrange("p b h q -> p b (h q)")
                                 ).then_inc(stored[g % 2], 16)
            for n in range(2):
                sp.wait_ge(stored[n], 32 * (GROUPS // 2))

        @block.gpsimd
        def _(g):
            g.memset(k.ones_bc[:, :], 1.0).then_inc(consts, 1)
            g.wait_ge(ld_m, 32)
            g.tensor_scalar(k.mask_bias[:, :, :], k.mask_col8[:, :, :], -MASKED, MASKED, ALU.mult, ALU.add
                            ).then_inc(own_p, 1)
            g.wait_ge(own_p, 1)
            g.wait_ge(mask_v, 2)
            g.tensor_tensor(k.mask_bias[:, :, :], k.mask_bias[:, :, :],
                            k.any_key[0:CH1, :].unsqueeze(2).to_broadcast([CH1, BATCH, CHUNKS]), ALU.mult
                            ).then_inc(own_p, 1)
            g.wait_ge(own_p, 2)

        @block.tensor
        def _(pe):
            pe.wait_ge(ld_w, 64)
            for g in range(KV):
                if g >= 2:
                    pe.wait_ge(kv_read, g - 1)
                pe.transpose(k.bank(g % 2, (0, P), P), k.wk1[:, g, :], k.ident[:, :])
                pe.transpose(k.bank(g % 2, (0, P), P, P), k.wv1[:, g, :], k.ident[:, :]).then_inc(kv_turned, 1)
            for h in range(HEADS + 1):
                if h < HEADS:
                    if h >= 2:
                        pe.wait_ge(q_read, h - 1)
                    for c in range(DK):
                        last = pe.transpose(k.bank(2 + h % 2, (0, P), P, c * P),
                                            k.wq1[:, c, h * P:(h + 1) * P], k.ident[:, :])
                    last.then_inc(q_turned, 1)
                if h >= 1:
                    m = h - 1
                    pe.wait_ge(q_read, m + 1)
                    pe.wait_ge(kv_read, m // 2 + 1)
                    if m >= 2:
                        pe.wait_ge(w_read, m - 1)
                    for c in range(DK):
                        pe.matmul(k.bank(4 + m % 2, (0, P), P, c * P), k.wq1_t[:, m % 2, c * P:(c + 1) * P],
                                  k.wk1_t[:, m // 2, :], start=True, stop=True)
                    pe.matmul(k.bank(4 + m % 2, (0, P), D, D), k.wv1_t[:, m // 2, :], k.wo1[:, m, :],
                              start=True, stop=True).then_inc(w_full, 1)
            pe.wait_ge(mask_v, 1)
            pe.wait_ge(consts, 1)
            pe.matmul(k.bank(6, (0, P), BATCH), k.ones_bc[:, :], k.any_diag[:, :], start=True, stop=True
                      ).then_inc(any_full, 1)
            norm.tensor(pe)
            norm.wait_all(pe)
            pe.wait_ge(w_read, HEADS)
            n = 0
            for g in range(GROUPS):
                for h in range(HEADS):
                    if n >= 4:
                        pe.wait_ge(stage_v, n - 3)
                    for c in range(DK):
                        last = pe.matmul(k.bank(4 + n % 4, (0, P), GC), k.qk_w[:, c, h, :],
                                         k.normed_t[:, c, g * GC:(g + 1) * GC], start=(c == 0), stop=(c == DK - 1))
                    last.then_inc(q_full, 1)
                    n += 1

        def staged(n):
            g, h = divmod(n, HEADS)
            return (k.q_stage[g % 2][0][:, :, h, :], k.q_stage[g % 2][1][:, :, h, :],
                    k.bank(4 + n % 4, (0, P), GC).rearrange("p (b q) -> p b q", q=SEQ))

        @block.scalar
        def _(a):
            for m in range(HEADS):
                a.wait_ge(w_full, m + 1)
                a.activation(k.qk_w[:, :, m, :], k.bank(4 + m % 2, (0, P), D).rearrange("p (c n) -> p c n", n=P),
                             ACT.Identity).then_inc(own_a, 1)
                a.activation(k.vo_w[:, m, :], k.bank(4 + m % 2, (0, P), D, D), ACT.Identity).then_inc(w_read, 1)
            norm.scalar(a)
            norm.copy_scalar(a)
            for n in range(GROUPS * HEADS):
                a.wait_ge(q_full, n + 1)
                if n % HEADS == 0 and n // HEADS >= 2:
                    a.wait_ge(stored[n // HEADS % 2], 32 * (n // HEADS // 2))
                hi, _lo, q = staged(n)
                a.activation(hi, q, ACT.Identity, scale=UP).then_inc(stage_a, 1)

        @block.vector
        def _(v):
            chain = Chain(v, vec)
            for g in range(KV):
                v.wait_ge(kv_turned, g + 1)
                chain.mark(v.tensor_copy(k.wk1_t[:, g, :], k.bank(g % 2, (0, P), P)))
                v.tensor_copy(k.wv1_t[:, g, :], k.bank(g % 2, (0, P), P, P)).then_inc(kv_read, 1)
            for h in range(HEADS):
                v.wait_ge(q_turned, h + 1)
                if h >= 2:
                    v.wait_ge(w_full, h - 1)
                v.tensor_copy(k.wq1_t[:, h % 2, :], k.bank(2 + h % 2, (0, P), D)).then_inc(q_read, 1)
            v.wait_ge(ld_m, 32)
            chain.mark(v.tensor_copy(k.mask_row[:, :], k.mask_row8[:, :]))
            chain.settle()
            chain.mark(v.tensor_reduce(k.any_col[:, :], k.mask_row[:, :], AX.X, ALU.max))
            chain.settle()
            v.tensor_scalar(k.any_diag[:, :], k.ident[0:BATCH, 0:BATCH], k.any_col[:, 0:1], None, ALU.mult
                            ).then_inc(mask_v, 1)
            v.wait_ge(any_full, 1)
            v.tensor_copy(k.any_key[:, :], k.bank(6, (0, P), BATCH)).then_inc(mask_v, 1)
            norm.vector(v, chain)
            norm.copy_vector(v)
            for n in range(GROUPS * HEADS):
                v.wait_ge(stage_a, n + 1)
                hi, lo, q = staged(n)
                v.scalar_tensor_tensor(out=lo, in0=q, scalar=UP, in1=hi, op0=ALU.mult, op1=ALU.subtract
                                       ).then_inc(stage_v, 1)


def layer1_attention(k):
    nc, i = k.nc, k.i
    turns = Turns(PREP1_ORDER, order1("first"), order1("mid"), order1("last"), ["OT", "Y"])
    (full, free, row_ready, s_full, sub_done, exp_done, pv_done, bc_ready, hi_ready, o_read, rs_own, max_own,
     consts) = k.sems(*("a1_" + n for n in (
         "shared_full", "shared_free", "row_ready", "scores_full", "sub_done", "exp_done", "pv_done", "bc_ready", "hi_ready",
         "o_read", "rs_own", "max_own", "consts")))
    loaded = k.sems("a1_loaded0", "a1_loaded1")
    q_loaded = k.sems("a1_q_loaded0", "a1_q_loaded1")
    S, O, SHARED = 0, 2, 5

    def shared(count, rows, cols):
        return k.banks(SHARED, count, rows, cols)

    def each_unit(part, odd, j, mine):
        return [name for side in SLOTS1[j] for name in side if name in mine and runs1(part, odd, name)]

    with nc.Block() as block:
        @block.sync
        def _(sp):
            def load(par, batch):
                sp.dma_start(k.rows1[par][:, :, 0:DC],
                             i["ctx"][bass.ds(batch, 1), :, :].rearrange("o (p j) d -> p (o j) d", j=CHUNKS)
                             ).then_inc(loaded[par], 16)

            def load_q(par, batch):
                for q, src in ((k.q1_hi, k.q1_dram[0]), (k.q1_lo, k.q1_dram[1])):
                    sp.dma_start(q[par][:, :], src[:, bass.ds(batch, 1), :].rearrange("p o n -> p (o n)")
                                 ).then_inc(q_loaded[par], 16)

            def body(part, pair):
                for odd in range(2):
                    batch = 2 * pair + odd
                    if part == "last" and odd:
                        continue
                    at_least(sp, pv_done, CHUNKS * batch)
                    if not (part == "first" and odd == 0):
                        load(1 - odd, batch + 1)
                        load_q(1 - odd, batch + 1)

            load(0, 0)
            load_q(0, 0)
            load(1, 1)
            load_q(1, 1)
            pair_loop(sp, body)

        @block.tensor
        def _(pe):
            def unit(part, pair, odd, name, number, batch):
                at_least(pe, free, number)
                nxt = 1 - odd
                if name == "B":
                    pe.wait_ge(bc_ready, batch + 2)
                    for j in range(CHUNKS):
                        last = pe.matmul(shared(3, (0, P), SPAN1)[:, j // 4, (j % 4) * CH1:(j % 4 + 1) * CH1],
                                         k.bias_bc[:, j, :], k.ident_bf[0:CH1, 0:CH1], start=True, stop=True)
                elif name == "T":
                    pe.wait_ge(loaded[nxt], 16 * (pair + odd + 1))
                    for j in range(CHUNKS):
                        last = pe.transpose(shared(3, (0, P), SPAN1)[:, j // 4, (j % 4) * CH1:(j % 4 + 1) * CH1],
                                            k.rows1[nxt][:, j, 0:DC], k.ident[0:CH1, 0:CH1])
                elif name[0] == "M":
                    m = int(name[1])
                    pe.wait_ge(q_loaded[nxt], 32 * (pair + odd + 1))
                    for b in range(3):
                        last = pe.matmul(shared(3, (0, P), SPAN1)[:, b, :], k.q1_hi[nxt][:, m * P:(m + 1) * P],
                                         k.ctx_hi[nxt][:, b, :], start=True, stop=True)
                elif name == "R":
                    pe.wait_ge(max_own, batch + 2)
                    for m in range(QT):
                        last = pe.matmul(k.bank(SHARED, (0, P), P, m * P),
                                         k.max_col[:, m:m + 1].to_broadcast([P, P]), k.ident_bf[:, :],
                                         start=True, stop=True)
                elif name == "OT":
                    pe.wait_ge(o_read, batch)
                    for t in range(QT):
                        last = pe.transpose(k.bank(SHARED, (0, P), P, t * P), k.heads_n[:, t, :], k.ident[:, :])
                else:
                    for h in range(HEADS):
                        last = pe.matmul(k.bank(SHARED, (0, TT), D), k.heads_t[:, h, :, :], k.vo_w[:, h, :],
                                         start=(h == 0), stop=(h == HEADS - 1))
                last.then_inc(full, 1)

            def scores(pair, batch, odd, j):
                if j == 0:
                    pe.wait_ge(q_loaded[odd], 32 * (pair + 1))
                at_least(pe, sub_done, CHUNKS * batch + j)
                hi, lo = (c[odd][:, :, :].rearrange("p b c -> p (b c)")[:, j * CH1:(j + 1) * CH1]
                          for c in (k.ctx_hi, k.ctx_lo))
                for h in range(2):
                    dst = k.banks(S, 2, (0, CH1), HALF)[:, h, :]
                    for n, (ctx, q) in enumerate(((hi, k.q1_hi), (lo, k.q1_hi), (hi, k.q1_lo))):
                        last = pe.matmul(dst, ctx, q[odd][:, h * HALF:(h + 1) * HALF],
                                         start=(n == 0), stop=(n == 2))
                last.then_inc(s_full, 1)

            def values(batch, odd, j):
                pe.wait_ge(exp_done, CHUNKS * batch + j + 1)
                if j == 0:
                    at_least(pe, o_read, batch)
                flat = k.probs[j % 2][0:CH1, :, :].rearrange("p h c -> p (h c)")
                dst = k.banks(O, 3, (0, P), BANK)
                for t in range(QT):
                    last = pe.matmul(dst[:, t // 3, (t % 3) * (DC + 1):(t % 3 + 1) * (DC + 1)],
                                     flat[:, t * P:(t + 1) * P], k.rows1[odd][:, j, :],
                                     start=(j == 0 and t % 3 == 0), stop=(j == CHUNKS - 1),
                                     skip_group_check=True)
                last.then_inc(pv_done, 1)

            def body(part, pair):
                for odd in range(2):
                    batch = 2 * pair + odd
                    for j in range(CHUNKS):
                        scores(pair, batch, odd, j)
                        before, after = SLOTS1[j]
                        for name in before:
                            if runs1(part, odd, name):
                                unit(part, pair, odd, name, turns.number(part, pair, (odd, name)), batch)
                        if j > 0:
                            values(batch, odd, j - 1)
                        elif not (part == "first" and odd == 0):
                            values(batch - 1, 1 - odd, CHUNKS - 1)
                        for name in after:
                            if runs1(part, odd, name):
                                unit(part, pair, odd, name, turns.number(part, pair, (odd, name)), batch)

            pe.wait_ge(consts, 2)
            for name in PREP1_ORDER:
                unit("pro", -1, 1, name, turns.number("pro", 0, name), -1)
            pair_loop(pe, body)
            values(BATCH - 1, 1, CHUNKS - 1)
            for name in ("OT", "Y"):
                unit("epi", PAIRS, 0, name, turns.number("epi", 0, name), BATCH)

        @block.scalar
        def _(a):
            def unit(part, pair, odd, name, number, batch):
                a.wait_ge(full, number + 1)
                if name == "T":
                    a.activation(k.ctx_hi[1 - odd][:, :, :], shared(3, (0, P), SPAN1), ACT.Identity, scale=UP
                                 ).then_inc(hi_ready, 1)
                    return
                elif name == "B":
                    last = a.activation(k.bias_row[:, :, :], shared(3, (0, P), SPAN1), ACT.Identity)
                elif name == "OT":
                    last = a.activation(k.heads_t[:, :, 1 - odd, :],
                                        k.bank(SHARED, (0, P), HQ).rearrange("p (h q) -> p h q", q=SEQ),
                                        ACT.Identity)
                elif name == "R":
                    a.activation(k.shift1[1 - odd][:, :], k.bank(SHARED, (0, P), HQ), ACT.Identity
                                 ).then_inc(free, 1)
                    a.wait_ge(free, number + 1).then_inc(row_ready, 1)
                    return
                last.then_inc(free, 1)

            def body(part, pair):
                for odd in range(2):
                    batch = 2 * pair + odd
                    for j in range(CHUNKS):
                        n = CHUNKS * batch + j
                        a.wait_ge(sub_done, n + 1)
                        if not (part == "first" and odd == 0 and j < 2):
                            a.wait_ge(pv_done, n - 1)
                        bias = k.mask_bias[:, bass.ds(batch, 1), j]
                        a.activation(k.probs[j % 2][0:CH1, :, :], k.shifted[j % 2][:, :, :], ACT.Exp,
                                     bias=bias, scale=SCALE1 / (UP * UP)).then_inc(exp_done, 1)
                        for name in each_unit(part, odd, j, ("T", "B", "OT", "R")):
                            unit(part, pair, odd, name, turns.number(part, pair, (odd, name)), batch)

            for name in PREP1_ORDER:
                if name in ("T", "B", "R"):
                    unit("pro", -1, 1, name, turns.number("pro", 0, name), -1)
            pair_loop(a, body)
            unit("epi", PAIRS, 0, "OT", turns.number("epi", 0, "OT"), BATCH)

        @block.vector
        def _(v):
            def subtract(part, batch, odd, j):
                n = CHUNKS * batch + j
                if j == 0:
                    v.wait_ge(row_ready, batch + 1)
                v.wait_ge(s_full, n + 1)
                if not (part == "first" and odd == 0 and j < 2):
                    v.wait_ge(exp_done, n - 1)
                v.tensor_tensor(k.shifted[j % 2][:, :, :], k.banks(S, 2, (0, CH1), HALF),
                                k.shift1[odd][0:CH1, :].rearrange("p (h c) -> p h c", h=2), ALU.subtract
                                ).then_inc(sub_done, 1)

            def read_sums(batch):
                v.wait_ge(pv_done, CHUNKS * batch + CHUNKS)
                src = k.banks(O, 3, (0, P), BANK)
                tiles = src[:, :, 0:3 * (DC + 1)].rearrange("p b (t c) -> p b t c", c=DC + 1)
                v.tensor_scalar(k.rsum1[:, 0:6].rearrange("p (b t) -> p b t", t=3), tiles[:, 0:2, :, DC],
                                1e-30, None, ALU.max)
                v.tensor_scalar(k.rsum1[:, 6:7], tiles[:, 2, 0, DC:DC + 1], 1e-30, None, ALU.max
                                ).then_inc(rs_own, 1)
                v.wait_ge(rs_own, 3 * batch + 1)
                v.reciprocal(k.rinv1[:, :], k.rsum1[:, :]).then_inc(rs_own, 1)
                v.wait_ge(rs_own, 3 * batch + 2)
                v.tensor_scalar(k.rsum1[:, :], k.rinv1[:, :], k.any_key[:, bass.ds(batch, 1)], None, ALU.mult
                                ).then_inc(rs_own, 1)
                v.wait_ge(rs_own, 3 * batch + 3)
                for b in range(3):
                    m = 3 if b < 2 else 1
                    last = v.tensor_tensor(
                        k.heads_n[:, 3 * b:3 * b + m, :], tiles[:, b, 0:m, 0:DC],
                        k.rsum1[:, 3 * b:3 * b + m].unsqueeze(2).to_broadcast([P, m, DC]), ALU.mult)
                last.then_inc(o_read, 1)

            def unit(part, pair, odd, name, number, batch):
                if name == "T":
                    v.wait_ge(hi_ready, batch + 2)
                    v.scalar_tensor_tensor(out=k.ctx_lo[1 - odd][:, :, :], in0=shared(3, (0, P), SPAN1),
                                           scalar=UP, in1=k.ctx_hi[1 - odd][:, :, :],
                                           op0=ALU.mult, op1=ALU.subtract).then_inc(free, 1)
                    return
                wait_alone(k, v, full, number + 1)
                if name[0] == "M":
                    m = int(name[1])
                    if m == 0 and part != "pro":
                        wait_alone(k, v, max_own, batch + 1)
                    elif m > 0:
                        wait_alone(k, v, free, number)
                    v.tensor_tensor_reduce(k.masked[:, :, :], shared(3, (0, P), SPAN1), k.bias_row[:, :, :],
                                           1.0, -3e38, ALU.add, ALU.max, k.max_f[:, m:m + 1]).then_inc(free, 1)
                    if m == QT - 1:
                        v.wait_ge(free, number + 1)
                        v.tensor_copy(k.max_col[:, :], k.max_f[:, :]).then_inc(max_own, 1)
                else:
                    row = k.resid[:, bass.ds(pair - 1, 1), :].rearrange("p o d -> p (o d)")
                    v.scalar_tensor_tensor(out=row, in0=k.bank(SHARED, (0, TT), D), scalar=k.gates[0:TT, 1:2],
                                           in1=row, op0=ALU.mult, op1=ALU.add).then_inc(free, 1)

            def body(part, pair):
                for odd in range(2):
                    batch = 2 * pair + odd
                    for j in range(CHUNKS):
                        subtract(part, batch, odd, j)
                        if j == 0 and not (part == "first" and odd == 0):
                            read_sums(batch - 1)
                        for name in each_unit(part, odd, j, ["Y", "T"] + [f"M{m}" for m in range(QT)]):
                            unit(part, pair, odd, name, turns.number(part, pair, (odd, name)), batch)

            for name in ["T"] + [f"M{m}" for m in range(QT)]:
                unit("pro", -1, 1, name, turns.number("pro", 0, name), -1)
            pair_loop(v, body)
            read_sums(BATCH - 1)
            unit("epi", PAIRS, 0, "Y", turns.number("epi", 0, "Y"), BATCH)
            v.wait_ge(free, turns.number("epi", 0, "Y") + 1)

        @block.gpsimd
        def _(g):
            for n in range(2):
                g.memset(k.rows1[n][:, :, DC:DC + 1], 1.0).then_inc(consts, 1)

            def prepare(nb):
                if not (isinstance(nb, int) and nb == 0):
                    wait_alone(k, g, s_full, CHUNKS * (nb - 1) + 1)
                g.tensor_copy(k.bias_bc[:, :, :],
                              k.mask_bias[:, bass.ds(nb, 1), :].rearrange("p o j -> p (o j)").unsqueeze(2)
                              .to_broadcast([CH1, CHUNKS, P])).then_inc(bc_ready, 1)

            def body(part, pair):
                for odd in range(2):
                    if not (part == "last" and odd):
                        prepare(2 * pair + odd + 1)

            prepare(0)
            pair_loop(g, body)



EXPERTS = 8
FF = 1024
CAP = TOK // EXPERTS
FC = FF // P
SLOTS = EXPERTS * CAP
assert CAP == 2 * TT


def moe_memory(k, s):
    sb = lambda name, shape, dt=F32: k.sbuf(s, name, shape, dt)
    k.w1 = [sb(f"w1_{n}", [P, DK, FF]) for n in range(2)]
    k.w2 = [sb(f"w2_{n}", [P, FC, D]) for n in range(2)]
    k.ff = [sb(f"ff{n}", [P, FC, CAP]) for n in range(2)]
    k.back = sb("back", [TT, NT, D])
    k.w_router = sb("w_router", [P, DK, EXPERTS])
    k.zeros = sb("zeros", [P, D])
    k.earlier = sb("earlier", [TT, TT], BF16)
    k.ones_tt = sb("ones_tt", [TT, TT], BF16)
    k.expert_i = sb("expert_i", [TT, EXPERTS], I32)
    k.token_i = sb("token_i", [TT, NT], I32)
    k.rank = sb("rank", [TT, EXPERTS])
    k.first_slot = sb("first_slot", [TT, EXPERTS])
    k.spill = sb("spill", [TT, NT])
    k.logits, k.e_gates, k.e_eq, k.e_tmp, k.e_tmp2 = (sb(name, [TT, NT, EXPERTS]) for name in (
        "logits", "e_gates", "e_eq", "e_tmp", "e_tmp2"))
    k.chosen = sb("chosen", [TT, NT, EXPERTS], BF16)
    (k.m_max, k.m_top, k.m_sum, k.m_inv, k.m_rank, k.m_loc, k.m_kept, k.m_slot, k.m_w, k.m_diff,
     k.m_put) = (sb(name, [TT, NT]) for name in (
         "m_max", "m_top", "m_sum", "m_inv", "m_rank", "m_loc", "m_kept", "m_slot", "m_w", "m_diff", "m_put"))
    k.put_i = sb("put_i", [TT, NT], I32)
    k.get_i = sb("get_i", [TT, NT], I32)


def load_expert(k, eng, par, e, loaded1, loaded2):
    eng.dma_start(k.w1[par][:, :, :], k.i["L1_ffn_w1"][bass.ds(e, 1), :, :].rearrange(
        "o (c p) f -> p (o c) f", p=P)).then_inc(loaded1[par], 16)
    eng.dma_start(k.w2[par][:, :, :], k.i["L1_ffn_w2"][bass.ds(e, 1), :, :].rearrange(
        "o (c p) d -> p (o c) d", p=P)).then_inc(loaded2[par], 16)


def moe_route(k):
    nc, i = k.nc, k.i
    norm = k.norm.start()
    k.dispatch = nc.dram_tensor("dispatch_scratch", (SLOTS + TOK, D), F32, kind="Internal").ap()
    k.expert_out = nc.dram_tensor("expert_scratch", (SLOTS, D), F32, kind="Internal").ap()
    k.w1_loaded, k.w2_loaded = k.sems("m_w1_loaded0", "m_w1_loaded1"), k.sems("m_w2_loaded0", "m_w2_loaded1")
    (ld, consts, own_p, zeroed, logits_full, shifted, exp_done, chosen, counted, indices, scattered,
     vec, casts) = k.sems(*("m0_" + n for n in (
         "ld", "consts", "own_p", "zeroed", "logits_full", "shifted", "exp_done", "chosen", "counted", "indices",
         "scattered", "vec", "casts")))

    with nc.Block() as block:
        @block.sync
        def _(sp):
            sp.dma_start(k.w_router[:, :, :], i["L1_ffn_w_gate"].rearrange("(c p) e -> p c e", p=P)
                         ).then_inc(ld, 16)
            sp.wait_ge(consts, 1)
            sp.dma_start(k.dispatch[0:SLOTS, :].rearrange("(j p) d -> p j d", p=P),
                         k.zeros[:, :].unsqueeze(1).to_broadcast([P, SLOTS // P, D])).then_inc(zeroed, 16)
            for par in range(2):
                load_expert(k, sp, par, par, k.w1_loaded, k.w2_loaded)

        @block.gpsimd
        def _(g):
            g.memset(k.zeros[:, :], 0.0).then_inc(consts, 1)
            g.memset(k.ones_tt[:, :], 1.0).then_inc(consts, 1)
            g.memset(k.earlier[:, :], 1.0).then_inc(own_p, 1)
            g.iota(k.expert_i[:, :], [[1, EXPERTS]], base=0, channel_multiplier=0).then_inc(casts, 1)
            g.iota(k.token_i[:, :], [[TT, NT]], base=SLOTS, channel_multiplier=1).then_inc(casts, 1)
            g.wait_ge(own_p, 1)
            g.affine_select(out=k.earlier[:, :], in_=k.earlier[:, :], compare_op=ALU.is_ge, fill=0.0, base=-1,
                            pattern=[[1, TT]], channel_multiplier=-1).then_inc(consts, 1)
            norm.wait_tiles(g, NT)
            g.wait_ge(zeroed, 16)
            g.wait_ge(indices, 2)
            for t in range(NT):
                g.indirect_dma_start(k.dispatch, bass.IndirectOffsetOnAxis(ap=k.put_i[:, t:t + 1], axis=0),
                                     k.normed[:, t, :], None).then_inc(scattered, 16)
            g.wait_ge(scattered, 16 * NT)

        @block.tensor
        def _(pe):
            norm.tensor(pe)
            norm.wait_all(pe)
            pe.wait_ge(ld, 16)
            for t in range(NT):
                for c in range(DK):
                    last = pe.matmul(k.bank(4, (0, TT), EXPERTS, t * EXPERTS), k.normed_t[:, c, t * TT:(t + 1) * TT],
                                     k.w_router[:, c, :], start=(c == 0), stop=(c == DK - 1))
            last.then_inc(logits_full, 1)
            pe.wait_ge(consts, 3)
            pe.wait_ge(chosen, 1)
            counts = k.bank(5, (0, TT), NT * EXPERTS)
            pe.matmul(counts, k.earlier[:, :], k.chosen[:, :, :], start=True, stop=False, skip_group_check=True)
            for t in range(NT - 1):
                last = pe.matmul(counts[:, (t + 1) * EXPERTS:], k.ones_tt[:, :],
                                 k.chosen[:, t:t + 1, :].to_broadcast([TT, NT - 1 - t, EXPERTS]),
                                 start=False, stop=(t == NT - 2), skip_group_check=True)
            last.then_inc(counted, 1)

        @block.scalar
        def _(a):
            norm.scalar(a)
            norm.copy_scalar(a)
            a.wait_ge(shifted, 1)
            a.activation(k.e_gates[:, :, :], k.logits[:, :, :], ACT.Exp).then_inc(exp_done, 1)

        @block.vector
        def _(v):
            chain = Chain(v, vec)
            each = lambda ap: ap[:, :].unsqueeze(2).to_broadcast([TT, NT, EXPERTS])
            row = lambda ap: ap[:, :].unsqueeze(1).to_broadcast([TT, NT, EXPERTS])

            def step(ins):
                chain.mark(ins)
                chain.settle()

            v.wait_ge(casts, 2)
            v.tensor_scalar(k.rank[:, :], k.expert_i[:, :], -1.0, float(EXPERTS), ALU.mult, ALU.add
                            ).then_inc(casts, 1)
            v.tensor_scalar(k.first_slot[:, :], k.expert_i[:, :], float(CAP), None, ALU.mult).then_inc(casts, 1)
            v.tensor_copy(k.spill[:, :], k.token_i[:, :]).then_inc(casts, 1)
            v.wait_ge(casts, 5)
            norm.vector(v, chain)
            norm.copy_vector(v)
            v.wait_ge(logits_full, 1)
            step(v.tensor_copy(k.logits[:, :, :], k.bank(4, (0, TT), NT * EXPERTS).rearrange(
                "p (t e) -> p t e", e=EXPERTS)))
            step(v.tensor_reduce(k.m_max[:, :], k.logits[:, :, :], AX.X, ALU.max))
            v.tensor_tensor(k.logits[:, :, :], k.logits[:, :, :], each(k.m_max), ALU.subtract
                            ).then_inc(shifted, 1)
            v.wait_ge(exp_done, 1)
            step(v.tensor_reduce(k.m_top[:, :], k.e_gates[:, :, :], AX.X, ALU.max))
            step(v.tensor_tensor(k.e_eq[:, :, :], k.e_gates[:, :, :], each(k.m_top), ALU.is_equal))
            step(v.tensor_tensor(k.e_tmp[:, :, :], k.e_eq[:, :, :], row(k.rank), ALU.mult))
            step(v.tensor_reduce(k.m_rank[:, :], k.e_tmp[:, :, :], AX.X, ALU.max))
            v.tensor_tensor(k.chosen[:, :, :], k.e_tmp[:, :, :], each(k.m_rank), ALU.is_equal
                            ).then_inc(chosen, 1)
            v.wait_ge(chosen, 1)
            chain.mark(v.tensor_reduce(k.m_sum[:, :], k.e_gates[:, :, :], AX.X, ALU.add))
            step(v.tensor_tensor(k.e_tmp2[:, :, :], k.chosen[:, :, :], row(k.first_slot), ALU.mult))
            chain.mark(v.tensor_reduce(k.m_slot[:, :], k.e_tmp2[:, :, :], AX.X, ALU.add))
            step(v.reciprocal(k.m_inv[:, :], k.m_sum[:, :]))
            chain.mark(v.tensor_tensor(k.m_w[:, :], k.m_top[:, :], k.m_inv[:, :], ALU.mult))
            v.wait_ge(counted, 1)
            step(v.tensor_tensor(k.e_tmp[:, :, :], k.chosen[:, :, :], k.bank(5, (0, TT), NT * EXPERTS).rearrange(
                "p (t e) -> p t e", e=EXPERTS), ALU.mult))
            step(v.tensor_reduce(k.m_loc[:, :], k.e_tmp[:, :, :], AX.X, ALU.add))
            chain.mark(v.tensor_scalar(k.m_kept[:, :], k.m_loc[:, :], float(CAP), None, ALU.is_lt))
            step(v.tensor_tensor(k.m_slot[:, :], k.m_slot[:, :], k.m_loc[:, :], ALU.add))
            chain.mark(v.tensor_tensor(k.m_diff[:, :], k.m_slot[:, :], k.spill[:, :], ALU.subtract))
            chain.mark(v.tensor_tensor(k.m_slot[:, :], k.m_slot[:, :], k.m_kept[:, :], ALU.mult))
            step(v.tensor_tensor(k.m_w[:, :], k.m_w[:, :], k.m_kept[:, :], ALU.mult))
            step(v.tensor_tensor(k.m_diff[:, :], k.m_diff[:, :], k.m_kept[:, :], ALU.mult))
            step(v.tensor_tensor(k.m_put[:, :], k.m_diff[:, :], k.spill[:, :], ALU.add))
            v.tensor_copy(k.put_i[:, :], k.m_put[:, :]).then_inc(indices, 1)
            v.tensor_copy(k.get_i[:, :], k.m_slot[:, :]).then_inc(indices, 1)
            step(v.tensor_scalar(k.m_w[:, :], k.m_w[:, :], k.gates[0:TT, 3:4], None, ALU.mult))


def moe_experts(k):
    nc = k.nc
    turn = k.norm
    turn.start_turn()
    rows_in, = k.sems("m1_rows_in")
    (h_full, gelu_done, expert_done, y_read, stored) = k.sems(*("m1_" + n for n in (
        "h_full", "gelu_done", "expert_done", "y_read", "stored")))

    with nc.Block() as block:
        @block.sync
        def _(sp):
            sp.dma_start(k.normed[:, :, :], k.dispatch[0:SLOTS, :].rearrange("(t p) d -> p t d", p=TT)
                         ).then_inc(rows_in, 16)

            def store_rows(e):
                sp.wait_ge(y_read, e + 3)
                sp.dma_start(k.expert_out[bass.ds(e * CAP, CAP), :].rearrange("(h p) d -> p h d", p=TT),
                             k.normed[:, bass.ds(2 * e, 2), :]).then_inc(stored, 16)

            with sp.Fori(0, EXPERTS // 2 - 1) as u:
                for par in range(2):
                    e = 2 * u + par
                    sp.wait_ge(expert_done, e + 3)
                    load_expert(k, sp, par, e + 2, k.w1_loaded, k.w2_loaded)
                    store_rows(e)
            for par in range(2):
                store_rows(EXPERTS - 2 + par)
            sp.wait_ge(stored, 16 * EXPERTS)

        @block.tensor
        def _(pe):
            pe.wait_ge(rows_in, 16)
            turn.tensor(pe)
            turn.wait_all(pe)
            for _n in range(2):
                pe.nop().then_inc(expert_done, 1)
            with pe.Fori(0, EXPERTS // 2) as u:
                for par in range(2):
                    e = 2 * u + par
                    pe.wait_ge(k.w1_loaded[par], 16 * (u + 1))
                    for f in range(FC):
                        if f % 2 == 0:
                            pe.wait_ge(gelu_done, 4 * e + f // 2 + 1)
                        for c in range(DK):
                            last = pe.matmul(k.bank(f // 2, (0, P), CAP, (f % 2) * CAP),
                                             k.w1[par][:, c, f * P:(f + 1) * P],
                                             k.normed_t[:, c, bass.ds(e * CAP, CAP)],
                                             start=(c == 0), stop=(c == DK - 1))
                        if f % 2 == 1:
                            last.then_inc(h_full, 1)
                    pe.wait_ge(k.w2_loaded[par], 16 * (u + 1))
                    pe.wait_ge(y_read, e + 1)
                    for half in range(2):
                        for f in range(FC):
                            if half == 0 and f % 2 == 0:
                                pe.wait_ge(gelu_done, 4 * e + f // 2 + 5)
                            last = pe.matmul(k.bank(4 + par, (0, TT), D, half * D),
                                             k.ff[par][:, f, half * TT:(half + 1) * TT], k.w2[par][:, f, :],
                                             start=(f == 0), stop=(f == FC - 1))
                    last.then_inc(expert_done, 1)

        @block.scalar
        def _(a):
            turn.copy_scalar(a)
            for _n in range(4):
                a.nop().then_inc(gelu_done, 1)
            a.preload_act_table_set("gelu_apprx_tanh_and_others")
            with a.Fori(0, EXPERTS // 2) as u:
                for par in range(2):
                    e = 2 * u + par
                    a.wait_ge(expert_done, e + 1)
                    for b in range(FC // 2):
                        a.wait_ge(h_full, 4 * e + b + 1)
                        a.activation(k.ff[par][:, 2 * b:2 * b + 2, :].rearrange("p f n -> p (f n)"),
                                     k.bank(b, (0, P), 2 * CAP), ACT.Gelu_apprx_tanh).then_inc(gelu_done, 1)

        @block.vector
        def _(v):
            turn.copy_vector(v)
            for _n in range(2):
                v.engine_nop().then_inc(y_read, 1)
            with v.Fori(0, EXPERTS // 2) as u:
                for par in range(2):
                    e = 2 * u + par
                    v.wait_ge(expert_done, e + 3)
                    v.tensor_copy(k.normed[:, bass.ds(2 * e, 2), :].rearrange("p h d -> p (h d)"),
                                  k.bank(4 + par, (0, TT), 2 * D)).then_inc(y_read, 1)


def moe_combine(k):
    gathered = k.sems(*(f"m2_gathered{q}" for q in range(4)))
    added, out_done = k.sems("m2_added", "m2_out_done")
    Q = NT // 4
    with k.nc.Block() as block:
        @block.gpsimd
        def _(g):
            for t in range(NT):
                g.indirect_dma_start(k.back[:, t, :], None, k.expert_out, bass.IndirectOffsetOnAxis(
                    ap=k.get_i[:, t:t + 1], axis=0)).then_inc(gathered[t // Q], 16)

        @block.vector
        def _(v):
            for t in range(NT):
                if t % Q == 0:
                    v.wait_ge(gathered[t // Q], 16 * Q)
                v.scalar_tensor_tensor(out=k.resid[:, t, :], in0=k.back[:, t, :], scalar=k.m_w[:, t:t + 1],
                                       in1=k.resid[:, t, :], op0=ALU.mult, op1=ALU.add).then_inc(added, 1)

        @block.sync
        def _(sp):
            out = k.out.rearrange("(t b) s d -> (b s) t d", b=2)
            for q in range(4):
                sp.wait_ge(added, Q * (q + 1))
                sp.dma_start(out[:, Q * q:Q * (q + 1), :], k.resid[:, Q * q:Q * (q + 1), :]).then_inc(out_done, 16)
            sp.wait_ge(out_done, 64)


def build(nc, inputs, out, upto=4):
    k = Kit(nc, inputs, out)
    with k.keep:
        make_persistent(k)
        with ExitStack() as s:
            layer0_memory(k, s)
        setup(k)
        layer0_attention(k)
        if upto >= 2:
            with ExitStack() as s:
                ffn_memory(k, s)
            ffn_prepare(k)
            ffn_run(k)
        if upto >= 3:
            with ExitStack() as s:
                layer1_memory(k, s)
            layer1_prepare(k)
            layer1_attention(k)
        if upto >= 4:
            with ExitStack() as s:
                moe_memory(k, s)
            moe_route(k)
            moe_experts(k)
            moe_combine(k)
        else:
            store(k)


def store(k):
    done, = k.sems("out_done")
    with k.nc.Block() as block:
        @block.sync
        def _(sp):
            sp.dma_start(k.out.rearrange("(t b) s d -> (b s) t d", b=2), k.resid[:, :, :]).then_inc(done, 16)
            sp.wait_ge(done, 16)


_INS = ["x", "ctx_1024", "g_xattn", "g_ffn", "L0_xattn_Wq", "L0_xattn_bq",
        "L0_xattn_Wk", "L0_xattn_bk", "L0_xattn_Wv", "L0_xattn_bv", "L0_xattn_Wkv_dca",
        "L0_xattn_bkv_dca", "L0_xattn_qn_w", "L0_xattn_qn_b", "L0_xattn_kn_w", "L0_xattn_kn_b",
        "L0_xattn_kn_dca_w", "L0_xattn_kn_dca_b", "L0_xattn_Wo", "L0_xattn_bo",
        "L0_ffn_w_gate", "L0_ffn_w_up", "L0_ffn_w_down", "L0_ffn_up_reorder_index",
        "L0_ffn_down_reorder_index", "L1_xattn_Wq", "L1_xattn_Wk", "L1_xattn_Wv", "L1_xattn_Wo",
        "L1_ffn_w_gate", "L1_ffn_w1", "L1_ffn_w2", "mask_BxS2_bf1"]


def lay_out(inputs):
    import numpy as np
    a = {n: np.asarray(inputs[n]) for n in _INS}
    for kind in ("W", "b"):
        both = np.concatenate([a[f"L0_xattn_{kind}k"], a[f"L0_xattn_{kind}v"]], axis=-1)
        both = both.reshape(both.shape[:-1] + (HEADS, 2, HD0))
        for n, name in enumerate("kv"):
            a[f"L0_xattn_{kind}{name}"] = np.ascontiguousarray(
                both[..., n, :].reshape(both.shape[:-3] + (D,)))
    a["mask_BxS2_bf1"] = a["mask_BxS2_bf1"].view(np.uint8)
    return a


def kernel(**inputs):
    import numpy as np
    import concourse.bacc as bacc
    from concourse.bass_utils import run_bass_kernel_spmd

    arrays = lay_out(inputs)
    nc = bacc.Bacc("TRN2", target_bir_lowering=False, num_devices=1)
    fed, aps = {}, {}
    for name in _INS:
        a = np.ascontiguousarray(arrays[name])
        fed[f"in_{name}_dram"] = a
        aps[name] = nc.dram_tensor(f"in_{name}_dram", a.shape, mybir.dt.from_np(a.dtype),
                                   kind="ExternalInput").ap()
    aps["ctx"], aps["mask"] = aps["ctx_1024"], aps["mask_BxS2_bf1"]
    out = nc.dram_tensor("out_0_dram", (BATCH, SEQ, D), F32, kind="ExternalOutput").ap()
    build(nc, aps, out)
    r = run_bass_kernel_spmd(nc, [fed], core_ids=[0])
    return r.results[0]["out_0_dram"]
```
